# Optimizing a Trainium2 kernel written in Bass

```python
import numpy as np
import jax
import jax.numpy as jnp

def _softmax(x, axis=-1):
    return jax.nn.softmax(x, axis=axis)

def _gelu(x):
    return jax.nn.gelu(x, approximate=True)

def _silu(x):
    return jax.nn.silu(x)

def _sigmoid(x):
    return jax.nn.sigmoid(x)

def _layernorm(x, axis=-1, eps=1e-05):
    m = jnp.mean(x, axis=axis, keepdims=True)
    v = jnp.var(x, axis=axis, keepdims=True)
    return (x - m) / jnp.sqrt(v + eps)

def _scatter_add(tgt, idx, src, axis=0):
    return tgt.at[idx].add(src)

def _segment_sum(src, seg, n):
    return jax.ops.segment_sum(src, seg, n)
kernel_name = 'mk_decoder_postln_d1_seqx_r4_bbcc4e'

def setup_inputs(seed: int=0):
    np.random.seed(seed)
    _w = jnp.asarray

    def _rec_inputs():
        import jax
        import jax.numpy as jnp
        _rk = jax.random.key(seed)
        x = -0.0002928 + 1 * jax.random.normal(jax.random.fold_in(_rk, 1), (8, 512, 256), jnp.float32)
        _lenS = 512 - jax.random.randint(jax.random.fold_in(_rk, 7), (8,), 0, max(1, 512 // 4) + 1, jnp.int32)
        _lenS2 = 1024 - jax.random.randint(jax.random.fold_in(_rk, 8), (8,), 0, max(1, 1024 // 4) + 1, jnp.int32)
        _ctx_512P = jax.random.normal(jax.random.fold_in(_rk, 11), (8, 16, 128), jnp.float32)
        _ctx_512c = jax.random.dirichlet(jax.random.fold_in(_rk, 511), 0.3 * jnp.ones((16,), jnp.float32), (8, 1024))
        _ctx_512t = jnp.einsum('bsk,bkd->bsd', _ctx_512c, _ctx_512P)
        _ctx_512t = _ctx_512t * jax.lax.rsqrt(jnp.mean(jnp.square(_ctx_512t)) + 1e-12) * 0.953939
        ctx_512 = 0.00222621 + 0.99962 * (_ctx_512t + 0.3 * jax.random.normal(jax.random.fold_in(_rk, 611), (8, 1024, 128), jnp.float32))
        return (x, ctx_512)
    x, ctx_512 = _rec_inputs()

    def _L0_attn_setup():
        import jax, jax.numpy as jnp
        import numpy as np
        B, S, D, H = (4, 512, 256, 16)
        HD = D // H
        key = jax.random.key(seed)
        k0, k1, k2, k3, k4 = jax.random.split(key, 5)
        x = jax.random.normal(k0, (B, S, D), dtype=jnp.float32)
        conv_w = jax.random.normal(k1, (D, 1, 3, 3), dtype=jnp.float32) * 0.1
        pe_w = jax.random.normal(k2, (D, D), dtype=jnp.float32) * 0.02
        qkv_w = jax.random.normal(k3, (3 * D, D), dtype=jnp.float32) * 0.02
        out_w = jax.random.normal(k4, (D, D), dtype=jnp.float32) * 0.02
        return {'x': x, 'conv_w': conv_w, 'pe_w': pe_w, 'qkv_w': qkv_w, 'out_w': out_w}
    _L0_attn_all = _L0_attn_setup()
    _L0_attn_in = {k: v for k, v in _L0_attn_all.items() if k in ('conv_w', 'pe_w', 'qkv_w', 'out_w')}
    del _L0_attn_all

    def _L0_xattn_setup():
        import jax, jax.numpy as jnp
        import numpy as np
        B, T, TC, C, CC, H = (2, 512, 128, 256, 128, 16)
        D = C // H

        def _heads(t):
            b, l, _ = t.shape
            return t.reshape(b, l, H, D).transpose(0, 2, 1, 3)
        key = jax.random.key(seed)
        ks = jax.random.split(key, 18)
        w = lambda k, i, o: jax.random.normal(k, (i, o), jnp.float32) / np.sqrt(i).astype(np.float32)
        return {'x': jax.random.normal(ks[0], (B, T, C), jnp.float32), 'cross_input': jax.random.normal(ks[1], (B, TC, CC), jnp.float32), 'Wk': w(ks[2], C, C), 'bk': jnp.zeros((C,), jnp.float32), 'Wq': w(ks[3], C, C), 'bq': jnp.zeros((C,), jnp.float32), 'Wv': w(ks[4], C, C), 'bv': jnp.zeros((C,), jnp.float32), 'Wck': w(ks[5], CC, C), 'bck': jnp.zeros((C,), jnp.float32), 'Wcq': w(ks[6], C, C), 'bcq': jnp.zeros((C,), jnp.float32), 'Wcv': w(ks[7], CC, C), 'bcv': jnp.zeros((C,), jnp.float32), 'Wp': w(ks[8], C, C), 'bp': jnp.zeros((C,), jnp.float32)}
    _L0_xattn_all = _L0_xattn_setup()
    _L0_xattn_in = {k: v for k, v in _L0_xattn_all.items() if k in ('Wk', 'bk', 'Wq', 'bq', 'Wv', 'bv', 'Wck', 'bck', 'Wcq', 'bcq', 'Wcv', 'bcv', 'Wp', 'bp')}
    del _L0_xattn_all

    def _L0_ffn_setup():
        import jax, jax.numpy as jnp
        import numpy as np
        D_MODEL = 256
        NUM_TILES = 64
        TPC = 8
        NUM_CLUSTERS = NUM_TILES // TPC
        GRID = 16
        COMP_H = 64
        NUM_KNOTS = 8
        EPS_LN = 1e-05

        def _calibrate(scores, knots, temperature):
            K = knots.shape[0]
            normalized = jax.nn.sigmoid(scores / (temperature[0] + 1e-06))
            idx_float = normalized * (K - 1)
            idx_low = jnp.clip(idx_float.astype(jnp.int32), 0, K - 2)
            idx_high = idx_low + 1
            t = idx_float - idx_low.astype(scores.dtype)
            val_low = knots[idx_low]
            val_high = knots[idx_high]
            return val_low + t * (val_high - val_low)

        def _forward(x, signatures_raw, knot_values, temperature, compress_w1, compress_b1, compress_w2, compress_b2, spline_w1, spline_b1, spline_w2, spline_b2, directions, norm_gamma, norm_beta, output_scale):
            B, T, D = x.shape
            xf = x.reshape(-1, D)
            q = jnp.where(signatures_raw > 0.3, 1.0, jnp.where(signatures_raw < -0.3, -1.0, 0.0)).astype(signatures_raw.dtype)
            sigs = signatures_raw + jax.lax.stop_gradient(q - signatures_raw)
            cluster_sigs = jnp.sign(sigs.reshape(NUM_CLUSTERS, TPC, D).mean(axis=1))
            cluster_scores = xf @ cluster_sigs.T
            cluster_gates = _calibrate(cluster_scores, knot_values, temperature)
            cluster_idx = jnp.argmax(cluster_gates, axis=-1)
            tile_scores = xf @ sigs.T
            tile_gates = _calibrate(tile_scores, knot_values, temperature)
            gates_by_cluster = tile_gates.reshape(-1, NUM_CLUSTERS, TPC)
            sel_gates = jnp.take_along_axis(gates_by_cluster, cluster_idx[:, None, None], axis=1)[:, 0, :]
            local_idx = jnp.argmax(sel_gates, axis=-1)
            tile_idx = cluster_idx * TPC + local_idx
            h = jax.nn.gelu(xf @ compress_w1 + compress_b1, approximate=False)
            comp = jnp.tanh(h @ compress_w2 + compress_b2)
            w1 = spline_w1[tile_idx]
            b1 = spline_b1[tile_idx]
            hh = jax.nn.relu(jnp.einsum('ni,nig->ng', comp, w1) + b1)
            w2 = spline_w2[tile_idx]
            b2 = spline_b2[tile_idx]
            mag = jnp.einsum('ng,ngo->no', hh, w2) + b2
            ffn_out = mag * directions[tile_idx] * output_scale[0]
            y = xf + ffn_out
            mu = y.mean(axis=-1, keepdims=True)
            var = ((y - mu) ** 2).mean(axis=-1, keepdims=True)
            y = (y - mu) / jnp.sqrt(var + EPS_LN) * norm_gamma + norm_beta
            return y.reshape(B, T, D)
        key = jax.random.key(seed)
        ks = jax.random.split(key, 12)
        B, T = (4, 1024)
        x = jax.random.normal(ks[0], (B, T, D_MODEL), dtype=jnp.float32)
        signatures_raw = jax.random.normal(ks[1], (NUM_TILES, D_MODEL), dtype=jnp.float32) * 0.5
        knot_values = jax.nn.sigmoid(jnp.linspace(-3.0, 3.0, NUM_KNOTS).astype(jnp.float32))
        temperature = jnp.ones((1,), dtype=jnp.float32)
        compress_w1 = jax.random.normal(ks[2], (D_MODEL, COMP_H), dtype=jnp.float32) * (1.0 / np.sqrt(D_MODEL))
        compress_b1 = jnp.zeros((COMP_H,), dtype=jnp.float32)
        compress_w2 = jax.random.normal(ks[3], (COMP_H, 2), dtype=jnp.float32) * (1.0 / np.sqrt(COMP_H))
        compress_b2 = jnp.zeros((2,), dtype=jnp.float32)
        spline_w1 = jax.random.normal(ks[4], (NUM_TILES, 2, GRID), dtype=jnp.float32) * (1.0 / np.sqrt(2.0))
        spline_b1 = jnp.zeros((NUM_TILES, GRID), dtype=jnp.float32)
        spline_w2 = jax.random.normal(ks[5], (NUM_TILES, GRID, 1), dtype=jnp.float32) * (1.0 / np.sqrt(GRID))
        spline_b2 = jnp.zeros((NUM_TILES, 1), dtype=jnp.float32)
        directions = jax.random.normal(ks[6], (NUM_TILES, D_MODEL), dtype=jnp.float32) * 0.02
        norm_gamma = jnp.ones((D_MODEL,), dtype=jnp.float32)
        norm_beta = jnp.zeros((D_MODEL,), dtype=jnp.float32)
        output_scale = jnp.ones((1,), dtype=jnp.float32) * 0.1
        return dict(x=x, signatures_raw=signatures_raw, knot_values=knot_values, temperature=temperature, compress_w1=compress_w1, compress_b1=compress_b1, compress_w2=compress_w2, compress_b2=compress_b2, spline_w1=spline_w1, spline_b1=spline_b1, spline_w2=spline_w2, spline_b2=spline_b2, directions=directions, norm_gamma=norm_gamma, norm_beta=norm_beta, output_scale=output_scale)
    _L0_ffn_all = _L0_ffn_setup()
    _L0_ffn_in = {k: v for k, v in _L0_ffn_all.items() if k in ('signatures_raw', 'knot_values', 'temperature', 'compress_w1', 'compress_b1', 'compress_w2', 'compress_b2', 'spline_w1', 'spline_b1', 'spline_w2', 'spline_b2', 'directions', 'norm_gamma', 'norm_beta', 'output_scale')}
    del _L0_ffn_all
    return {'x': x, 'ctx_512': ctx_512, 'L0_attn_conv_w': _L0_attn_in['conv_w'], 'L0_attn_pe_w': _L0_attn_in['pe_w'], 'L0_attn_qkv_w': _L0_attn_in['qkv_w'], 'L0_attn_out_w': _L0_attn_in['out_w'], 'L0_xattn_Wk': _L0_xattn_in['Wk'], 'L0_xattn_bk': _L0_xattn_in['bk'], 'L0_xattn_Wq': _L0_xattn_in['Wq'], 'L0_xattn_bq': _L0_xattn_in['bq'], 'L0_xattn_Wv': _L0_xattn_in['Wv'], 'L0_xattn_bv': _L0_xattn_in['bv'], 'L0_xattn_Wck': _L0_xattn_in['Wck'], 'L0_xattn_bck': _L0_xattn_in['bck'], 'L0_xattn_Wcq': _L0_xattn_in['Wcq'], 'L0_xattn_bcq': _L0_xattn_in['bcq'], 'L0_xattn_Wcv': _L0_xattn_in['Wcv'], 'L0_xattn_bcv': _L0_xattn_in['bcv'], 'L0_xattn_Wp': _L0_xattn_in['Wp'], 'L0_xattn_bp': _L0_xattn_in['bp'], 'L0_ffn_signatures_raw': _L0_ffn_in['signatures_raw'], 'L0_ffn_knot_values': _L0_ffn_in['knot_values'], 'L0_ffn_temperature': _L0_ffn_in['temperature'], 'L0_ffn_compress_w1': _L0_ffn_in['compress_w1'], 'L0_ffn_compress_b1': _L0_ffn_in['compress_b1'], 'L0_ffn_compress_w2': _L0_ffn_in['compress_w2'], 'L0_ffn_compress_b2': _L0_ffn_in['compress_b2'], 'L0_ffn_spline_w1': _L0_ffn_in['spline_w1'], 'L0_ffn_spline_b1': _L0_ffn_in['spline_b1'], 'L0_ffn_spline_w2': _L0_ffn_in['spline_w2'], 'L0_ffn_spline_b2': _L0_ffn_in['spline_b2'], 'L0_ffn_directions': _L0_ffn_in['directions'], 'L0_ffn_norm_gamma': _L0_ffn_in['norm_gamma'], 'L0_ffn_norm_beta': _L0_ffn_in['norm_beta'], 'L0_ffn_output_scale': _L0_ffn_in['output_scale']}

def reference(x, ctx_512, L0_attn_conv_w, L0_attn_pe_w, L0_attn_qkv_w, L0_attn_out_w, L0_xattn_Wk, L0_xattn_bk, L0_xattn_Wq, L0_xattn_bq, L0_xattn_Wv, L0_xattn_bv, L0_xattn_Wck, L0_xattn_bck, L0_xattn_Wcq, L0_xattn_bcq, L0_xattn_Wcv, L0_xattn_bcv, L0_xattn_Wp, L0_xattn_bp, L0_ffn_signatures_raw, L0_ffn_knot_values, L0_ffn_temperature, L0_ffn_compress_w1, L0_ffn_compress_b1, L0_ffn_compress_w2, L0_ffn_compress_b2, L0_ffn_spline_w1, L0_ffn_spline_b1, L0_ffn_spline_w2, L0_ffn_spline_b2, L0_ffn_directions, L0_ffn_norm_gamma, L0_ffn_norm_beta, L0_ffn_output_scale):
    import jax
    import jax.numpy as jnp

    def _L0_attn_ref(x, conv_w, pe_w, qkv_w, out_w):
        import jax, jax.numpy as jnp
        import numpy as np
        B, S, D, H = (4, 512, 256, 16)
        HD = D // H
        b, s, d = x.shape
        h, hd = (H, d // H)
        xc = jnp.transpose(x, (0, 2, 1))[..., None]
        xc = jax.lax.conv_general_dilated(xc, conv_w, window_strides=(1, 1), padding=((1, 1), (1, 1)), dimension_numbers=('NCHW', 'OIHW', 'NCHW'), feature_group_count=d)
        xs = jnp.transpose(xc[..., 0], (0, 2, 1))
        xs = xs + xs @ pe_w.T
        qkv = (xs @ qkv_w.T).reshape(b, s, 3, d)
        qkv = jnp.transpose(qkv, (0, 2, 1, 3))
        q = qkv[:, 0].reshape(b, h, s, hd).astype(jnp.bfloat16)
        k = qkv[:, 1].reshape(b, h, s, hd).astype(jnp.bfloat16)
        v = qkv[:, 2].reshape(b, h, s, hd).astype(jnp.bfloat16)
        scale = jnp.sqrt(jnp.asarray(hd, dtype=jnp.bfloat16))
        scores = jnp.einsum('bhqd,bhkd->bhqk', q, k) / scale
        attn = jax.nn.softmax(scores, axis=-1)
        o = jnp.einsum('bhqk,bhkd->bhqd', attn, v)
        o = jnp.transpose(o, (0, 2, 1, 3)).reshape(b, s, d).astype(jnp.float32)
        return o @ out_w.T

    def _L0_xattn_ref(x, cross_input, Wk, bk, Wq, bq, Wv, bv, Wck, bck, Wcq, bcq, Wcv, bcv, Wp, bp):
        import jax, jax.numpy as jnp
        import numpy as np
        B, T, TC, C, CC, H = (2, 512, 128, 256, 128, 16)
        D = C // H

        def _heads(t):
            b, l, _ = t.shape
            return t.reshape(b, l, H, D).transpose(0, 2, 1, 3)
        scale = np.float32(1.0 / np.sqrt(D))
        q = _heads(x @ Wq + bq)
        k = _heads(x @ Wk + bk)
        v = _heads(x @ Wv + bv)
        att = jnp.einsum('bhqd,bhkd->bhqk', q, k) * scale
        causal = jnp.tril(jnp.ones((T, T), bool))
        att = jnp.where(causal[None, None], att, -jnp.inf)
        y = jnp.einsum('bhqk,bhkd->bhqd', jax.nn.softmax(att, axis=-1), v)
        qc = _heads(x @ Wcq + bcq)
        kc = _heads(cross_input @ Wck + bck)
        vc = _heads(cross_input @ Wcv + bcv)
        attc = jnp.einsum('bhqd,bhkd->bhqk', qc, kc) * scale
        y = y + jnp.einsum('bhqk,bhkd->bhqd', jax.nn.softmax(attc, axis=-1), vc)
        y = y.transpose(0, 2, 1, 3).reshape(x.shape[0], T, C)
        return y @ Wp + bp

    def _L0_ffn_ref(x, signatures_raw, knot_values, temperature, compress_w1, compress_b1, compress_w2, compress_b2, spline_w1, spline_b1, spline_w2, spline_b2, directions, norm_gamma, norm_beta, output_scale):
        import jax, jax.numpy as jnp
        import numpy as np
        D_MODEL = 256
        NUM_TILES = 64
        TPC = 8
        NUM_CLUSTERS = NUM_TILES // TPC
        GRID = 16
        COMP_H = 64
        NUM_KNOTS = 8
        EPS_LN = 1e-05

        def _calibrate(scores, knots, temperature):
            K = knots.shape[0]
            normalized = jax.nn.sigmoid(scores / (temperature[0] + 1e-06))
            idx_float = normalized * (K - 1)
            idx_low = jnp.clip(idx_float.astype(jnp.int32), 0, K - 2)
            idx_high = idx_low + 1
            t = idx_float - idx_low.astype(scores.dtype)
            val_low = knots[idx_low]
            val_high = knots[idx_high]
            return val_low + t * (val_high - val_low)

        def _forward(x, signatures_raw, knot_values, temperature, compress_w1, compress_b1, compress_w2, compress_b2, spline_w1, spline_b1, spline_w2, spline_b2, directions, norm_gamma, norm_beta, output_scale):
            B, T, D = x.shape
            xf = x.reshape(-1, D)
            q = jnp.where(signatures_raw > 0.3, 1.0, jnp.where(signatures_raw < -0.3, -1.0, 0.0)).astype(signatures_raw.dtype)
            sigs = signatures_raw + jax.lax.stop_gradient(q - signatures_raw)
            cluster_sigs = jnp.sign(sigs.reshape(NUM_CLUSTERS, TPC, D).mean(axis=1))
            cluster_scores = xf @ cluster_sigs.T
            cluster_gates = _calibrate(cluster_scores, knot_values, temperature)
            cluster_idx = jnp.argmax(cluster_gates, axis=-1)
            tile_scores = xf @ sigs.T
            tile_gates = _calibrate(tile_scores, knot_values, temperature)
            gates_by_cluster = tile_gates.reshape(-1, NUM_CLUSTERS, TPC)
            sel_gates = jnp.take_along_axis(gates_by_cluster, cluster_idx[:, None, None], axis=1)[:, 0, :]
            local_idx = jnp.argmax(sel_gates, axis=-1)
            tile_idx = cluster_idx * TPC + local_idx
            h = jax.nn.gelu(xf @ compress_w1 + compress_b1, approximate=False)
            comp = jnp.tanh(h @ compress_w2 + compress_b2)
            w1 = spline_w1[tile_idx]
            b1 = spline_b1[tile_idx]
            hh = jax.nn.relu(jnp.einsum('ni,nig->ng', comp, w1) + b1)
            w2 = spline_w2[tile_idx]
            b2 = spline_b2[tile_idx]
            mag = jnp.einsum('ng,ngo->no', hh, w2) + b2
            ffn_out = mag * directions[tile_idx] * output_scale[0]
            y = xf + ffn_out
            mu = y.mean(axis=-1, keepdims=True)
            var = ((y - mu) ** 2).mean(axis=-1, keepdims=True)
            y = (y - mu) / jnp.sqrt(var + EPS_LN) * norm_gamma + norm_beta
            return y.reshape(B, T, D)
        return _forward(x, signatures_raw, knot_values, temperature, compress_w1, compress_b1, compress_w2, compress_b2, spline_w1, spline_b1, spline_w2, spline_b2, directions, norm_gamma, norm_beta, output_scale)
    x = _layernorm(x + _L0_attn_ref(x, L0_attn_conv_w, L0_attn_pe_w, L0_attn_qkv_w, L0_attn_out_w), axis=-1)
    x = _layernorm(x + _L0_xattn_ref(x, ctx_512, L0_xattn_Wk, L0_xattn_bk, L0_xattn_Wq, L0_xattn_bq, L0_xattn_Wv, L0_xattn_bv, L0_xattn_Wck, L0_xattn_bck, L0_xattn_Wcq, L0_xattn_bcq, L0_xattn_Wcv, L0_xattn_bcv, L0_xattn_Wp, L0_xattn_bp), axis=-1)
    x = _layernorm(x + _L0_ffn_ref(x, L0_ffn_signatures_raw, L0_ffn_knot_values, L0_ffn_temperature, L0_ffn_compress_w1, L0_ffn_compress_b1, L0_ffn_compress_w2, L0_ffn_compress_b2, L0_ffn_spline_w1, L0_ffn_spline_b1, L0_ffn_spline_w2, L0_ffn_spline_b2, L0_ffn_directions, L0_ffn_norm_gamma, L0_ffn_norm_beta, L0_ffn_output_scale), axis=-1)
    return x

_drawn_inputs = setup_inputs


def setup_inputs(seed=0):
    import zlib

    import numpy as np

    out = dict(_drawn_inputs(seed))
    spreads = {'L0_xattn_bk': (0.0, 2.0),
     'L0_xattn_bq': (0.0, 0.634),
     'L0_xattn_bv': (0.0, 0.1),
     'L0_xattn_bck': (0.0, 2.0),
     'L0_xattn_bcq': (0.0, 0.398),
     'L0_xattn_bcv': (0.0, 0.1),
     'L0_xattn_bp': (0.0, 0.1),
     'L0_ffn_compress_b1': (0.0, 0.8),
     'L0_ffn_compress_b2': (0.0, 2.0),
     'L0_ffn_spline_b1': (0.0, 2.0),
     'L0_ffn_spline_b2': (0.0, 2.0),
     'L0_ffn_norm_gamma': (1.0, 0.2),
     'L0_ffn_norm_beta': (0.0, 0.1)}
    factors = {'L0_attn_conv_w': 8.0,
     'L0_attn_pe_w': 8.0,
     'L0_attn_qkv_w': 8.0,
     'L0_attn_out_w': 8.0,
     'L0_ffn_signatures_raw': 8.0,
     'L0_ffn_knot_values': 8.0,
     'L0_ffn_compress_w1': 8.0,
     'L0_ffn_compress_w2': 8.0,
     'L0_ffn_spline_w1': 8.0,
     'L0_ffn_spline_w2': 8.0,
     'L0_ffn_directions': 8.0}
    for name, (base, spread) in spreads.items():
        noise = np.random.default_rng([zlib.crc32(name.encode()), seed]).standard_normal(out[name].shape)
        drawn = base * np.exp(spread * noise) if base else spread * noise
        out[name] = jnp.asarray(drawn.astype(out[name].dtype))
    for name, factor in factors.items():
        out[name] = (out[name] * factor).astype(out[name].dtype)
    return out
```

```python
import concourse.bass as bass
from concourse import mybir
from contextlib import ExitStack


class Steps:

    def __init__(self, sem, per_batch, b):
        self.sem, self.per_batch, self.b, self.n = sem, per_batch, b, 0

    def mark(self, instruction):
        instruction.then_inc(self.sem, 1)
        self.n += 1

    def wait(self, engine):
        engine.wait_ge(self.sem, self.b * self.per_batch + self.n)

    def end(self):
        assert self.n == self.per_batch, (self.n, self.per_batch)


def decoder_layer(nc, x, xT, ctxT, conv_w, peT, qkvT, outT, Wk, bk, Wq, bq, Wv, bv, Wck, bck, Wcq, bcq,
                  Wcv, bcv, Wp, bp, signatures, knots, temperature, cw1, cb1, cw2, cb2, sw1, sb1, sw2, sb2,
                  directions, gamma, beta, output_scale, out):
    fp32 = mybir.dt.float32
    bf16 = mybir.dt.bfloat16
    ALU = mybir.AluOpType
    ACT = mybir.ActivationFunctionType
    AX = mybir.AxisListType

    B, S, D = x.shape
    CC, SC = ctxT.shape[1:]
    H, HD, P = 16, 16, 128
    KD = D // P
    NT = S // P
    NC = SC // P
    RH = S // H
    TILES = signatures.shape[0]
    CL, TPC = 8, TILES // 8
    NK = knots.shape[0]
    HID = cw1.shape[1]
    G = sw1.shape[2]
    SCALE = 1.0 / HD ** 0.5
    SHIFT = 6 * HD
    ROWS = SHIFT + 3
    QPART = (0, 0, 0, 1, 1, 2)
    KPART = (0, 1, 2, 0, 1, 0)
    MASKED = -1.0e30
    EPS = 1e-5
    ST = CL + TILES
    T_W1 = D
    T_B1 = T_W1 + 2 * G
    T_W2 = T_B1 + G
    T_B2 = T_W2 + G
    TABLE = T_B2 + 1
    SELF, CROSS = 0, 1
    UNITS = 10
    FIRST = 1
    DVE_STEPS = 104
    SIG_STEPS = 20
    POOL_STEPS = 4

    ctx = ExitStack()
    with ctx:
        def sb(name, shape, dt=fp32):
            return ctx.enter_context(nc.sbuf_tensor(name, shape, dt))

        def sem(name):
            return ctx.enter_context(nc.semaphore(name))

        conv_sb = sb("conv_sb", [P, KD, 3])
        pe_sb = sb("pe_sb", [P, KD, D])
        qkv_sb = sb("qkv_sb", [P, KD, 3 * D])
        out_sb = sb("out_sb", [P, KD, D])
        wq_sb, wk_sb, wv_sb = sb("wq_sb", [P, KD, D]), sb("wk_sb", [P, KD, D]), sb("wv_sb", [P, KD, D])
        wcq_sb, wck_sb, wcv_sb = sb("wcq_sb", [P, KD, D]), sb("wck_sb", [P, D]), sb("wcv_sb", [P, D])
        wp_sb = sb("wp_sb", [P, KD, D])
        bq_col, bk_col = sb("bq_col", [P, KD]), sb("bk_col", [P, KD])
        bcq_col, bck_col = sb("bcq_col", [P, KD]), sb("bck_col", [P, KD])
        bv_row, bcv_row, bp_row = sb("bv_row", [P, D]), sb("bcv_row", [P, D]), sb("bp_row", [P, D])
        gamma_row, beta_row = sb("gamma_row", [P, D]), sb("beta_row", [P, D])
        sig_raw = sb("sig_raw", [TILES, D])
        sig_work = sb("sig_work", [TILES, 2, D])
        sigT = sb("sigT", [P, KD, ST])
        sig_sum = sb("sig_sum", [P, 2, KD, CL])
        knot_row, knot_step = sb("knot_row", [P, NK]), sb("knot_step", [P, NK - 1])
        temp = sb("temp", [P, 3])
        scale_col = sb("scale_col", [P, 1])
        cw1_sb, cb1_col = sb("cw1_sb", [P, KD, HID]), sb("cb1_col", [HID, 1])
        cw2_sb, cb2_row = sb("cw2_sb", [HID, 2]), sb("cb2_row", [P, 2])
        table = sb("table", [TILES, TABLE])
        ident, identb = sb("ident", [P, P]), sb("identb", [P, P], bf16)
        mask_f = sb("mask_f", [P, P])
        mask_q, mask_k = sb("mask_q", [P, P], bf16), sb("mask_k", [P, P], bf16)
        first_weight = sb("first_weight", [P, CL])
        minus_half = sb("minus_half", [P, NT])

        xT_pad = sb("xT_pad", [P, KD, S + 2])
        ctx_sb = sb("ctx_sb", [P, SC])
        featA = sb("featA", [P, KD, S])
        featB = sb("featB", [P, KD, S])
        x_res = sb("x_res", [P, NT, D])
        y_sb = sb("y_sb", [P, NT, D])
        qk_nat = sb("qk_nat", [P, 2 * KD, S], bf16)
        v_nat = sb("v_nat", [P, NT, D], bf16)
        v1 = sb("v1", [P, H, 4, HD], bf16)
        o_nat = sb("o_nat", [P, NT, D], bf16)
        k1T = sb("k1T", [P, 16, S], bf16)
        q_self, k_self = sb("q_self", [P, H, S], bf16), sb("k_self", [P, H, S], bf16)
        q_cross, k_cross = sb("q_cross", [P, H, S], bf16), sb("k_cross", [P, H, SC], bf16)
        q1T = q_cross[:, :, :].rearrange("p h n -> p (h n)")
        q1_chunks = k_cross[0:HD, 0:H // 2, :].rearrange("p h n -> p (h n)").rearrange("p (c s) -> p c s", c=16)
        v_self, v_cross = sb("v_self", [P, NT, H, HD + 1]), sb("v_cross", [P, NC, H, HD + 1])
        work = sb("work", [P, 6144])
        y_tmp = sb("y_tmp", [P, NT, HD])
        max1 = sb("max1", [P, 2, NT], bf16)
        neg1, den1, rden1 = sb("neg1", [P, 2, NT]), sb("den1", [P, 2, NT]), sb("rden1", [P, 2, NT])
        denb1 = sb("denb1", [P, 2, NT], bf16)
        max_self, max_half = sb("max_self", [P, NT]), sb("max_half", [P, NT, 2])
        max_cross = sb("max_cross", [P, NT])
        max_rest = sb("max_rest", [P, 2, 2, NT])
        max_parts = sb("max_parts", [P, 2, NT, 3], bf16)
        rec = sb("rec", [P, 2, NT])
        stats, mv = sb("stats", [P, NT, 6]), sb("mv", [P, NT, 2])
        ln_var, ln_r = sb("ln_var", [P, NT]), sb("ln_r", [P, NT])

        s1 = work[:, 0:2048].bitcast(bf16).rearrange("p (a t n) -> p a t n", a=2, t=NT)
        e1 = work[:, 2048:4096].bitcast(bf16).rearrange("p (a t n) -> p a t n", a=2, t=NT)
        p1T = work[:, 4096:5120].bitcast(bf16).rearrange("p (t n) -> p t n", t=4)
        parts = work[:, 0:1536].bitcast(bf16).rearrange("p (a s n) -> p a s n", a=2, s=3)
        rest = work[:, 1536:2560].rearrange("p (a n) -> p a n", a=2)
        pT_self = work[:, 0:2048].rearrange("p (t n) -> p t n", t=NT)
        pT_cross = work[:, 2048:6144].rearrange("p (t n) -> p t n", t=NC)
        N = NT * ST

        def piece(i, n, t=NT):
            return work[:, 512 * i:512 * i + n].rearrange("p (t n) -> p t n", t=t)

        gate_in, low, frac, knot_at, step_at, seg = (work[:, 512 * i:512 * i + N] for i in range(6))
        gates = piece(0, N)
        c_eq, c_pick, l_eq, l_pick, sel = (piece(6, 5 * NT * CL)[:, :, CL * i:CL * (i + 1)] for i in range(5))
        sel_all = piece(7, NT * TILES)
        expert = piece(8, NT * TILES)
        top, best = work[:, 4608:4608 + NT], work[:, 4612:4612 + NT]
        comp_in = work[:, 4640:4640 + 2 * NT].rearrange("p (t i) -> p t i", t=NT)
        comp = work[:, 4656:4656 + 2 * NT].rearrange("p (t i) -> p t i", t=NT)
        x_dir = work[:, 0:NT * D].rearrange("p (t d) -> p t d", t=NT)
        hh, hh2 = work[:, 5120:5184].rearrange("p (t g) -> p t g", t=NT), work[:, 5184:5248].rearrange("p (t g) -> p t g", t=NT)
        mag = work[:, 5248:5248 + NT]
        hT = work[0:HID, 5632:6144]
        expertT = work[0:TILES, 3072:3584]

        bank = ctx.enter_context(nc.psum_tensor("bank", [P, 8, 512], fp32))

        def bankb(i, n=1):
            return bank[:, i:i + n, :].rearrange("p a n -> p (a n)").bitcast(bf16)

        waited = {e: sem(f"waited_{n}") for n, e in (("pe", nc.tensor), ("dve", nc.vector), ("pool", nc.gpsimd), ("sp", nc.sync))}
        w_in, x_in, xn_in, ctx_in = sem("w_in"), sem("x_in"), sem("xn_in"), sem("ctx_in")
        const_ready, init_step = sem("const_ready"), sem("init_step")
        sig_tr, sig_ready = sem("sig_tr"), sem("sig_ready")
        dve_step, pool_step = sem("dve_step"), sem("pool_step")
        conv_done, pe_mm, xs_ready = sem("conv_done"), sem("pe_mm"), sem("xs_ready")
        qk_mm, qk_evac, v_mm, v_evac = sem("qk_mm"), sem("qk_evac"), sem("v_mm"), sem("v_evac")
        qk1_in, v1_ready = sem("qk1_in"), sem("v1_ready")
        s1_mm, s1_evac, s1_neg, e1_ready = sem("s1_mm"), sem("s1_evac"), sem("s1_neg"), sem("e1_ready")
        n1_step, p1_ready, p1_tr, p1_evac = sem("n1_step"), sem("p1_ready"), sem("p1_tr"), sem("p1_evac")
        o1_mm, o1_evac = sem("o1_mm"), sem("o1_evac")
        feat_tr, feat_evac = sem("feat_tr"), sem("feat_evac")
        out_mm, res_done = sem("out_mm"), sem("res_done")
        ln_stats, ln_rstd, ln_done = sem("ln_stats"), sem("ln_rstd"), sem("ln_done")
        pj_mm, pj_hi, pj_rest, pj_mid, pj_parts = (sem(n) for n in ("pj_mm", "pj_hi", "pj_rest", "pj_mid", "pj_parts"))
        stack_in = [sem("stack_in_self"), sem("stack_in_cross")]
        qk1_out = [sem(f"qk1_out{i}") for i in range(4)]
        parts_out = [sem("parts_out0"), sem("parts_out1")]
        vj_mm, vj_evac = sem("vj_mm"), sem("vj_evac")
        s_mm, max_done = sem("s_mm"), sem("max_done")
        cross_max, q1_ready = sem("cross_max"), sem("q1_ready")
        parts_ready = [sem("parts_self"), sem("parts_cross")]
        max_tr = [sem("max_tr_self"), sem("max_tr_cross")]
        max_rows, m_step = sem("max_rows"), sem("m_step")
        sT_mm, pT_ready = sem("sT_mm"), sem("pT_ready")
        pv_mm = [sem("pv_self"), sem("pv_cross")]
        y_step, y_done = sem("y_step"), sem("y_done")
        route_mm, gelu_in, gelu_done, comp_mm = sem("route_mm"), sem("gelu_in"), sem("gelu_done"), sem("comp_mm")
        comp_b, comp_done, gate_exp = sem("comp_b"), sem("comp_done"), sem("gate_exp")
        expert_ready, expert_tr, expert_evac, gather_mm = (sem(n) for n in ("expert_ready", "expert_tr", "expert_evac", "gather_mm"))
        out_dma = sem("out_dma")

        def own_wait(engine):
            engine.sem_inc(waited[engine], 1)

        def wide(w):
            return w.rearrange("(k p) n -> p k n", p=P)

        weights = [(conv_sb[:], wide(conv_w)), (pe_sb[:], wide(peT)), (qkv_sb[:], wide(qkvT)),
                   (out_sb[:], wide(outT)), (wq_sb[:], wide(Wq)), (wk_sb[:], wide(Wk)), (wv_sb[:], wide(Wv)),
                   (wcq_sb[:], wide(Wcq)), (wck_sb[:], Wck), (wcv_sb[:], Wcv), (wp_sb[:], wide(Wp)),
                   (bq_col[:], bq), (bk_col[:], bk), (bcq_col[:], bcq), (bck_col[:], bck),
                   (bv_row[:], bv.partition_broadcast(P)), (bcv_row[:], bcv.partition_broadcast(P)),
                   (bp_row[:], bp.partition_broadcast(P)), (gamma_row[:], gamma.partition_broadcast(P)),
                   (beta_row[:], beta.partition_broadcast(P)), (sig_raw[:], signatures),
                   (knot_row[:], knots.partition_broadcast(P)), (temp[:, 0:1], temperature.partition_broadcast(P)),
                   (scale_col[:], output_scale.partition_broadcast(P)), (cw1_sb[:], wide(cw1)),
                   (cb1_col[:], cb1.rearrange("(p o) -> p o", o=1)), (cw2_sb[:], cw2),
                   (cb2_row[:], cb2.partition_broadcast(P)), (table[:, 0:D], directions),
                   (table[:, T_W1:T_B1], sw1.rearrange("t i g -> t (i g)")), (table[:, T_B1:T_W2], sb1),
                   (table[:, T_W2:T_B2], sw2.rearrange("t g o -> t (g o)")), (table[:, T_B2:TABLE], sb2)]
        W_IN = 16 * len(weights)

        unit_list = [(q_self, 0, 0, QPART), (q_self, 1, 0, QPART), (k_self, 0, 0, KPART), (k_self, 1, 0, KPART),
                     (q_cross, 0, 0, QPART), (q_cross, 1, 0, QPART), (k_cross, 0, 0, KPART), (k_cross, 1, 0, KPART),
                     (k_cross, 0, S, KPART), (k_cross, 1, S, KPART)]
        unit_bias = [bq_col, bq_col, bk_col, bk_col, bcq_col, bcq_col, bck_col, bck_col, bck_col, bck_col]
        STACK_IN = (16 * 6 * 4, 16 * 6 * (UNITS - 4))
        qk_dram = nc.dram_tensor("qk_dram", (2 * KD, P, S), bf16, kind="Internal").ap()
        parts_dram = nc.dram_tensor("parts_dram", (UNITS, 3, P, S), bf16, kind="Internal").ap()

        block = ctx.enter_context(nc.Block())

        @block.sync
        def _(sp):
            for primed in (qk1_in, out_dma):
                sp.sem_inc(primed, FIRST)
            for dst, src in weights:
                sp.dma_start(dst, src).then_inc(w_in, 16)
            with sp.Fori(0, B) as b:
                sp.wait_ge(conv_done, FIRST + b * KD)
                sp.wait_ge(const_ready, 1)
                for k in range(KD):
                    sp.dma_start(xT_pad[:, k, 1:S + 1], xT[b, k * P:(k + 1) * P, :]).then_inc(x_in, 16)
                sp.wait_ge(vj_mm, FIRST + b * (NT + NC))
                own_wait(nc.sync)
                sp.wait_ge(pj_mm, FIRST + b * UNITS)
                own_wait(nc.sync)
                sp.dma_start(ctx_sb[:], ctxT[b]).then_inc(ctx_in, 16)
                sp.wait_ge(ln_done, FIRST + b * 4)
                sp.dma_start(x_res[:], x[b].rearrange("(t p) d -> p t d", p=P)).then_inc(xn_in, 16)
                sp.wait_ge(sT_mm, FIRST + b * H * 8)
                own_wait(nc.sync)
                sp.wait_ge(s_mm, FIRST + b * H * 12)
                own_wait(nc.sync)
                for i in range(2 * KD):
                    sp.wait_ge(qk_evac, b * 2 * KD + i + 1)
                    sp.dma_start(qk_dram[i], qk_nat[:, i, :]).then_inc(qk1_out[i], 16)
                for i in range(2 * KD):
                    sp.wait_ge(qk1_out[i], b * 16 + 16)
                    dst = (q1_chunks if i < KD else k1T)[0:HD, 8 * (i % KD):8 * (i % KD) + 8, :]
                    sp.dma_start(dst, qk_dram[i].rearrange("(c j) s -> j c s", j=HD)).then_inc(qk1_in, 16)
                sp.wait_ge(s1_mm, (b + 1) * H * NT)
                own_wait(nc.sync)
                for u in range(UNITS + 1):
                    if u < UNITS:
                        sp.wait_ge(pj_parts, b * UNITS + u + 1)
                        sp.dma_start(parts_dram[u].rearrange("s p n -> p s n"), parts[:, u % 2]).then_inc(parts_out[u % 2], 16)
                    if u > 0:
                        stack, m, c0, which = unit_list[u - 1]
                        sp.wait_ge(parts_out[(u - 1) % 2], (b * (UNITS // 2) + (u - 1) // 2 + 1) * 16)
                        for r, part in enumerate(which):
                            dst = stack[HD * r:HD * (r + 1), 8 * m:8 * m + 8, c0:c0 + S]
                            src = parts_dram[u - 1, part].rearrange("(h j) s -> j h s", j=HD)
                            sp.dma_start(dst, src).then_inc(stack_in[SELF if u <= 4 else CROSS], 16)
                sp.wait_ge(ln_done, FIRST + 4 * (b + 1))
                sp.dma_start(out[b].rearrange("(t p) d -> p t d", p=P), y_sb[:]).then_inc(out_dma, 16)
            sp.wait_ge(out_dma, FIRST + 16 * B)

        @block.gpsimd
        def _(pool):
            for primed in (parts_ready[SELF], parts_ready[CROSS]):
                pool.sem_inc(primed, FIRST)
            n = [0]

            def init(ins):
                ins.then_inc(init_step, 1)
                n[0] += 1
                pool.wait_ge(init_step, n[0])

            init(nc.gpsimd.memset(ident[:], 0.0))
            init(nc.gpsimd.affine_select(out=ident[:], in_=ident[:], compare_op=ALU.not_equal, fill=1.0, base=0,
                                         pattern=[[-1, P]], channel_multiplier=1))
            init(nc.gpsimd.tensor_copy(identb[:], ident[:]))
            init(nc.gpsimd.memset(mask_f[:], 0.0))
            init(nc.gpsimd.affine_select(out=mask_f[:], in_=mask_f[:], compare_op=ALU.is_ge, fill=MASKED, base=0,
                                         pattern=[[-1, P]], channel_multiplier=1))
            init(nc.gpsimd.tensor_copy(mask_q[:], mask_f[:]))
            init(nc.gpsimd.memset(mask_f[:], 0.0))
            init(nc.gpsimd.affine_select(out=mask_f[:], in_=mask_f[:], compare_op=ALU.is_ge, fill=MASKED, base=0,
                                         pattern=[[1, P]], channel_multiplier=-1))
            init(nc.gpsimd.tensor_copy(mask_k[:], mask_f[:]))
            init(nc.gpsimd.iota(first_weight[:], pattern=[[-1, CL]], base=CL, channel_multiplier=0,
                                allow_small_or_imprecise_dtypes=True))
            init(nc.gpsimd.memset(minus_half[:], -0.5))
            init(nc.gpsimd.memset(xT_pad[:], 0.0))
            init(nc.gpsimd.memset(k1T[:], 0.0))
            init(nc.gpsimd.memset(q1T, 0.0))
            init(nc.gpsimd.memset(v_self[:, :, :, HD:HD + 1], 1.0))
            init(nc.gpsimd.memset(v_cross[:, :, :, HD:HD + 1], 1.0))
            init(nc.gpsimd.memset(k_self[SHIFT:P, :, :], -1.0))
            init(nc.gpsimd.memset(k_cross[SHIFT:P, :, :], -1.0))
            nc.gpsimd.memset(work[:, 0:1], 0.0).then_inc(const_ready, 1)

            with pool.Fori(0, B) as b:
                def rstd(k):
                    pool.wait_ge(ln_stats, b * 16 + 4 * k + 4)
                    own_wait(nc.gpsimd)
                    nc.gpsimd.tensor_scalar(ln_var[:], mv[:, :, 1], EPS, None, ALU.add).then_inc(pool_step, 1)
                    pool.wait_ge(pool_step, b * POOL_STEPS + k + 1)
                    nc.gpsimd.tensor_tensor(ln_r[:], ln_var[:], minus_half[:], ALU.pow).then_inc(ln_rstd, 1)

                pool.wait_ge(v_evac, b * 2 + 2)
                own_wait(nc.gpsimd)
                for q in range(4):
                    for a in range(4):
                        src = v_nat[RH * q:RH * (q + 1), :, :].rearrange("p g (t a j) -> p g t a j", t=4, a=4)[:, :, :, a, :]
                        dst = v1[RH * a:RH * (a + 1), :, :, :].rearrange("p (g q) t j -> p g q t j", q=4)[:, :, q]
                        nc.gpsimd.tensor_copy(dst, src).then_inc(v1_ready, 1)
                pool.wait_ge(qk1_in, FIRST + (b + 1) * 16 * 2 * KD)
                own_wait(nc.gpsimd)
                for q in range(4):
                    nc.gpsimd.tensor_copy(q1T[0:HD, S * 4 * q:S * 4 * (q + 1)].rearrange("p (s c) -> p c s", c=16),
                                          q1_chunks[:, :, P * q:P * (q + 1)]).then_inc(q1_ready, 1)
                rstd(0)
                with pool.Fori(0, H) as h:
                    u = b * H + h
                    for kind in (SELF, CROSS):
                        if kind == SELF:
                            pool.wait_ge(max_done, u * 12 + 4)
                        else:
                            pool.wait_ge(cross_max, u + 1)
                        pool.wait_ge(max_tr[kind], FIRST + u)
                        own_wait(nc.gpsimd)
                        step = u * 6 + 3 * kind
                        top_row = max_self if kind == SELF else max_cross
                        part = max_parts[:, kind, :, :]
                        nc.gpsimd.tensor_copy(part[:, :, 0], top_row[:]).then_inc(m_step, 1)
                        pool.wait_ge(m_step, step + 1)
                        nc.gpsimd.tensor_tensor(max_rest[:, kind, 0, :], top_row[:], part[:, :, 0], ALU.subtract).then_inc(m_step, 1)
                        pool.wait_ge(m_step, step + 2)
                        own_wait(nc.gpsimd)
                        nc.gpsimd.tensor_copy(part[:, :, 1], max_rest[:, kind, 0, :]).then_inc(m_step, 1)
                        pool.wait_ge(m_step, step + 3)
                        nc.gpsimd.tensor_tensor(part[:, :, 2], max_rest[:, kind, 0, :], part[:, :, 1], ALU.subtract).then_inc(parts_ready[kind], 1)
                for k in range(1, 4):
                    rstd(k)

        @block.scalar
        def _(act):
            for primed in (p1_evac,):
                act.sem_inc(primed, FIRST)
            act.wait_ge(w_in, W_IN)
            act.wait_ge(const_ready, 1)
            with act.Fori(0, B) as b:
                for i in range(2 * KD):
                    act.wait_ge(qk_mm, b * 2 * KD + i + 1)
                    if i == 0:
                        act.wait_ge(qk1_in, FIRST + b * 16 * 2 * KD)
                    nc.scalar.copy(qk_nat[:, i, :], bank[:, 2 + i, :]).then_inc(qk_evac, 1)

                def exp1(h, p):
                    u = b * H + h
                    act.wait_ge(s1_neg, u + 1)
                    if not (isinstance(h, int) and h == 0):
                        act.wait_ge(p1_ready, FIRST + 4 * u - 4)
                    for t in range(NT):
                        nc.scalar.activation(e1[:, p, t, :], s1[:, p, t, :], ACT.Exp, bias=neg1[:, p, t:t + 1],
                                             scale=SCALE, accum_out=den1[:, p, t:t + 1]).then_inc(e1_ready, 1)

                def evac1(h):
                    u = b * H + h
                    act.wait_ge(p1_tr, FIRST + u + 1)
                    act.wait_ge(o1_mm, FIRST + u)
                    for i in range(2):
                        nc.scalar.copy(p1T[:, 2 * i:2 * i + 2, :].rearrange("p a n -> p (a n)"), bankb(4 + i)).then_inc(p1_evac, 1)

                exp1(0, 0)
                with act.Fori(0, H // 2 - 1) as i:
                    for n in range(2):
                        h = i * 2 + (n + 1)
                        exp1(h, (n + 1) % 2)
                        evac1(h - 1)
                exp1(H - 1, 1)
                evac1(H - 2)
                evac1(H - 1)

                def features(k, dst, src):
                    act.wait_ge(feat_tr, b * 4 + k + 1)
                    nc.scalar.copy(dst[:].rearrange("p k n -> p (k n)"), src).then_inc(feat_evac, 1)

                features(0, featA, bankb(7))
                features(1, featB, bank[:, 2:4, :].rearrange("p a n -> p (a n)"))

                for u in range(UNITS):
                    _, m, _, _ = unit_list[u]
                    act.wait_ge(pj_mm, FIRST + b * UNITS + u + 1)
                    if u < 2:
                        act.wait_ge(pv_mm[CROSS], FIRST + b * H)
                    else:
                        act.wait_ge(parts_out[u % 2], (b * (UNITS // 2) + u // 2) * 16)
                    nc.scalar.activation(parts[:, u % 2, 0, :], bank[:, 4 + u % 4, :], ACT.Identity,
                                         bias=unit_bias[u][:, m:m + 1], scale=1.0).then_inc(pj_hi, 1)
                    act.wait_ge(pj_rest, b * UNITS + u + 1)
                    nc.scalar.copy(parts[:, u % 2, 1, :], rest[:, u % 2, :]).then_inc(pj_mid, 1)

                with act.Fori(0, H) as h:
                    n = b * H + h
                    for kind in (SELF, CROSS):
                        act.wait_ge(pv_mm[kind], FIRST + n)
                        for u in range(4):
                            act.wait_ge(sT_mm, FIRST + n * 8 + 4 * kind + u + 1)
                            c = 2 + 2 * (u % 2)
                            if kind == SELF:
                                nc.scalar.activation(pT_self[:, u, P * u:S], bank[:, c, 0:S - P * u], ACT.Exp,
                                                     scale=SCALE).then_inc(pT_ready, 1)
                            else:
                                nc.scalar.activation(pT_cross[:, 2 * u:2 * u + 2, :], bank[:, c:c + 2, :], ACT.Exp,
                                                     scale=SCALE).then_inc(pT_ready, 1)

                features(2, featA, bank[:, 2:4, :].rearrange("p a n -> p (a n)"))
                features(3, featB, bank[:, 4:6, :].rearrange("p a n -> p (a n)"))
                act.wait_ge(route_mm, b + 1)
                nc.scalar.activation(gate_in.rearrange("p (t n) -> p t n", t=NT), bank[:, 6, 0:N].rearrange("p (t n) -> p t n", t=NT),
                                     ACT.Exp, scale=temp[:, 2:3]).then_inc(gate_exp, 1)
                act.wait_ge(gelu_in, b + 1)
                nc.scalar.activation(hT, bank[0:HID, 7, :], ACT.Gelu, bias=cb1_col[:, 0:1], scale=1.0).then_inc(gelu_done, 1)
                act.wait_ge(comp_b, b + 1)
                nc.scalar.activation(comp, comp_in, ACT.Tanh).then_inc(comp_done, 1)
                act.wait_ge(expert_tr, b + 1)
                nc.scalar.copy(expertT, bank[0:TILES, 5, :]).then_inc(expert_evac, 1)

        @block.vector
        def _(dve):
            for primed in (conv_done, ln_done, p1_ready, o1_evac, max_rows, y_done):
                dve.sem_inc(primed, FIRST)
            dve.wait_ge(w_in, W_IN)
            dve.wait_ge(const_ready, 1)
            q0, q1 = sig_work[:, 0, :], sig_work[:, 1, :]
            setup = [0]

            def link(ins):
                ins.then_inc(sig_ready, 1)
                setup[0] += 1
                dve.wait_ge(sig_ready, setup[0])

            link(nc.vector.tensor_scalar(q0, sig_raw[:], 0.3, None, ALU.is_gt))
            link(nc.vector.tensor_scalar(q1, sig_raw[:], -0.3, None, ALU.is_lt))
            link(nc.vector.tensor_tensor(q0, q0, q1, ALU.subtract))
            link(nc.vector.tensor_tensor(q0, q0, sig_raw[:], ALU.subtract))
            link(nc.vector.tensor_tensor(q0, q0, sig_raw[:], ALU.add))
            SIG_NAT = setup[0]
            dve.wait_ge(sig_tr, 1)
            link(nc.vector.tensor_copy(sigT[:, :, CL:ST], bank[:, 0, 0:KD * TILES].rearrange("p (k n) -> p k n", k=KD)))
            members = sigT[:, :, CL:ST].rearrange("p k (c i) -> p k c i", i=TPC)
            link(nc.vector.tensor_tensor(sig_sum[:, 0], members[:, :, :, 0], members[:, :, :, 1], ALU.add))
            for i in range(2, TPC):
                link(nc.vector.tensor_tensor(sig_sum[:, 0], sig_sum[:, 0], members[:, :, :, i], ALU.add))
            link(nc.vector.tensor_scalar(sig_sum[:, 1], sig_sum[:, 0], 0.0, None, ALU.is_lt))
            link(nc.vector.tensor_scalar(sig_sum[:, 0], sig_sum[:, 0], 0.0, None, ALU.is_gt))
            link(nc.vector.tensor_tensor(sigT[:, :, 0:CL], sig_sum[:, 0], sig_sum[:, 1], ALU.subtract))
            link(nc.vector.tensor_tensor(knot_step[:], knot_row[:, 1:NK], knot_row[:, 0:NK - 1], ALU.subtract))
            link(nc.vector.tensor_scalar(temp[:, 1:2], temp[:, 0:1], 1e-6, None, ALU.add))
            link(nc.vector.reciprocal(temp[:, 2:3], temp[:, 1:2]))
            link(nc.vector.tensor_scalar(temp[:, 2:3], temp[:, 2:3], -1.0, None, ALU.mult))
            assert setup[0] == SIG_STEPS and SIG_NAT == 5

            with dve.Fori(0, B) as b:
                st = Steps(dve_step, DVE_STEPS, b)

                def do(ins):
                    st.mark(ins)
                    st.wait(dve)

                def layernorm(k, src, dst):
                    for t in range(NT):
                        st.mark(nc.vector.bn_stats(stats[:, t, :], src[:, t, :]))
                    st.wait(dve)
                    own_wait(nc.vector)
                    for t in range(NT):
                        nc.vector.bn_aggr(mv[:, t, :], stats[:, t, :]).then_inc(ln_stats, 1)
                    dve.wait_ge(ln_stats, b * 16 + 4 * k + 4)
                    dve.wait_ge(ln_rstd, b * 4 + k + 1)
                    for t in range(NT):
                        ins = nc.vector.tensor_scalar(dst[:, t, :], src[:, t, :], mv[:, t, 0:1], ln_r[:, t:t + 1],
                                                      ALU.subtract, ALU.mult)
                        if t < NT - 1:
                            st.mark(ins)
                        else:
                            ins.then_inc(ln_done, 1)
                    st.wait(dve)
                    dve.wait_ge(ln_done, FIRST + b * 4 + k + 1)

                dve.wait_ge(x_in, b * 16 * KD + 16 * KD)
                for k in range(KD):
                    do(nc.vector.tensor_scalar(featA[:, k, :], xT_pad[:, k, 0:S], conv_sb[:, k, 0:1], None, ALU.mult))
                    do(nc.vector.scalar_tensor_tensor(featA[:, k, :], xT_pad[:, k, 1:S + 1], conv_sb[:, k, 1:2],
                                                      featA[:, k, :], ALU.mult, ALU.add))
                    nc.vector.scalar_tensor_tensor(featA[:, k, :], xT_pad[:, k, 2:S + 2], conv_sb[:, k, 2:3],
                                                   featA[:, k, :], ALU.mult, ALU.add).then_inc(conv_done, 1)
                dve.wait_ge(conv_done, FIRST + b * KD + KD)
                for k in range(KD):
                    dve.wait_ge(pe_mm, b * KD + k + 1)
                    nc.vector.tensor_tensor(featB[:, k, :], bank[:, k, :], featA[:, k, :], ALU.add).then_inc(xs_ready, 1)
                for i in range(2):
                    dve.wait_ge(v_mm, b * 2 + i + 1)
                    nc.vector.tensor_copy(v_nat[:, 2 * i:2 * i + 2, :].rearrange("p a n -> p (a n)"), bank[:, 6 + i, :]).then_inc(v_evac, 1)

                def scores1(h, p):
                    u = b * H + h
                    if not (isinstance(h, int) and h == 0):
                        dve.wait_ge(p1_tr, FIRST + u - 1)
                    for t in range(NT):
                        dve.wait_ge(s1_mm, u * 4 + t + 1)
                        nc.vector.tensor_scalar(s1[:, p, t, :], bank[:, t, :], 1.0, None, ALU.mult, ALU.max,
                                                accum_out=max1[:, p, t:t + 1]).then_inc(s1_evac, 1)
                    dve.wait_ge(s1_evac, u * 4 + 4)
                    nc.vector.tensor_scalar(neg1[:, p, :], max1[:, p, :], -SCALE, None, ALU.mult).then_inc(s1_neg, 1)

                def norm1(h, p):
                    u = b * H + h
                    dve.wait_ge(e1_ready, u * 4 + 4)
                    nc.vector.tensor_copy(denb1[:, p, :], den1[:, p, :]).then_inc(n1_step, 1)
                    dve.wait_ge(n1_step, u * 2 + 1)
                    nc.vector.reciprocal(rden1[:, p, :], denb1[:, p, :]).then_inc(n1_step, 1)
                    dve.wait_ge(n1_step, u * 2 + 2)
                    for t in range(NT):
                        nc.vector.tensor_scalar(s1[:, p, t, :], e1[:, p, t, :], rden1[:, p, t:t + 1], None,
                                                ALU.mult).then_inc(p1_ready, 1)

                def out1(h):
                    u = b * H + h
                    dve.wait_ge(o1_mm, FIRST + u + 1)
                    nc.vector.tensor_copy(o_nat[:, :, bass.ts(h, HD)],
                                          bank[:, 6, 0:NT * HD].rearrange("p (t j) -> p t j", t=NT)).then_inc(o1_evac, 1)

                scores1(0, 0)
                scores1(1, 1)
                norm1(0, 0)
                with dve.Fori(0, H // 2 - 1) as i:
                    for p in range(2):
                        h = i * 2 + (2 + p)
                        scores1(h, p)
                        norm1(h - 1, 1 - p)
                        out1(h - 2)
                norm1(H - 1, 1)
                out1(H - 2)
                out1(H - 1)

                dve.wait_ge(xn_in, b * 16 + 16)
                for i in range(2):
                    dve.wait_ge(out_mm, b * 4 + i + 1)
                    nc.vector.tensor_tensor(x_res[:, 2 * i:2 * i + 2, :].rearrange("p a n -> p (a n)"),
                                            x_res[:, 2 * i:2 * i + 2, :].rearrange("p a n -> p (a n)"), bank[:, i, :],
                                            ALU.add).then_inc(res_done, 1)
                dve.wait_ge(res_done, b * 2 + 2)
                layernorm(0, x_res, x_res)

                def unit(u):
                    _, m, _, _ = unit_list[u]
                    dve.wait_ge(pj_hi, b * UNITS + u + 1)
                    nc.vector.scalar_tensor_tensor(rest[:, u % 2, :], bank[:, 4 + u % 4, :], unit_bias[u][:, m:m + 1],
                                                   parts[:, u % 2, 0, :], ALU.add, ALU.subtract).then_inc(pj_rest, 1)
                    dve.wait_ge(pj_mid, b * UNITS + u + 1)
                    nc.vector.tensor_tensor(parts[:, u % 2, 2, :], rest[:, u % 2, :], parts[:, u % 2, 1, :],
                                            ALU.subtract).then_inc(pj_parts, 1)

                def values(i):
                    dve.wait_ge(vj_mm, FIRST + b * (NT + NC) + i + 1)
                    dst, row, t = (v_self, bv_row, i) if i < NT else (v_cross, bcv_row, i - NT)
                    nc.vector.tensor_tensor(dst[:, t, :, 0:HD], bank[:, i % 4, 0:D].rearrange("p (h j) -> p h j", h=H),
                                            row[:].rearrange("p (h j) -> p h j", h=H), ALU.add).then_inc(vj_evac, 1)

                for u in range(4):
                    unit(u)
                for i in range(NT):
                    values(i)
                for u in range(4, UNITS):
                    unit(u)
                for i in range(NT, NT + NC):
                    values(i)

                def maxima(kind, h, j):
                    n = b * H + h
                    idx = n * 12 + 4 * kind + j
                    if j == 0:
                        dve.wait_ge(parts_ready[kind], FIRST + n)
                    dve.wait_ge(s_mm, FIRST + idx + 1)
                    if kind == SELF:
                        nc.vector.tensor_reduce(max_self[:, j:j + 1], bank[:, j % 2, 0:P * (j + 1)], AX.X, ALU.max).then_inc(max_done, 1)
                    else:
                        nc.vector.tensor_reduce(max_half[:, j // 2, j % 2:j % 2 + 1], bank[:, j % 2, :], AX.X, ALU.max).then_inc(max_done, 1)
                        if j == 7:
                            dve.wait_ge(max_done, idx + 1)
                            nc.vector.tensor_tensor(max_cross[:], max_half[:, :, 0], max_half[:, :, 1], ALU.max).then_inc(cross_max, 1)

                def put_rows(kind, h):
                    dve.wait_ge(max_tr[kind], FIRST + b * H + h + 1)
                    stack = q_self if kind == SELF else q_cross
                    nc.vector.tensor_copy(stack[SHIFT:ROWS, h, :], bankb(7)[0:3, S * kind:S * (kind + 1)]).then_inc(max_rows, 1)

                def finish(kind, h):
                    n = b * H + h
                    dve.wait_ge(pv_mm[kind], FIRST + n + 1)
                    o = bank[:, 6, 0:NT * 32].rearrange("p (t j) -> p t j", t=NT)
                    nc.vector.reciprocal(rec[:, kind, :], o[:, :, HD]).then_inc(y_step, 1)
                    dve.wait_ge(y_step, n * 3 + kind + 1)
                    r = rec[:, kind, :].unsqueeze(2).broadcast_to([P, NT, HD])
                    ys = y_sb[:, :, bass.ts(h, HD)]
                    if kind == SELF:
                        nc.vector.tensor_tensor(ys, o[:, :, 0:HD], r, ALU.mult).then_inc(y_done, 1)
                    else:
                        nc.vector.tensor_tensor(y_tmp[:], o[:, :, 0:HD], r, ALU.mult).then_inc(y_done, 1)
                        dve.wait_ge(y_done, FIRST + n * 2 + 2)
                        nc.vector.tensor_tensor(ys, ys, y_tmp[:], ALU.add).then_inc(y_step, 1)

                def slot(kind, h, first=False, last=False):
                    for u in range(4):
                        if not last:
                            if kind == SELF:
                                maxima(SELF, h + 1, u)
                            else:
                                maxima(CROSS, h + 1, 2 * u)
                                maxima(CROSS, h + 1, 2 * u + 1)
                        if u == 1:
                            if kind == SELF:
                                put_rows(CROSS, h)
                            elif not last:
                                put_rows(SELF, h + 1)
                    if kind == CROSS:
                        finish(SELF, h)
                    elif not first:
                        finish(CROSS, h - 1)

                for j in range(4):
                    maxima(SELF, 0, j)
                for j in range(8):
                    maxima(CROSS, 0, j)
                put_rows(SELF, 0)
                dve.wait_ge(out_dma, FIRST + b * 16)
                slot(SELF, 0, first=True)
                slot(CROSS, 0)
                with dve.Fori(1, H - 1) as h:
                    slot(SELF, h)
                    slot(CROSS, h)
                slot(SELF, H - 1, last=True)
                slot(CROSS, H - 1, last=True)
                finish(CROSS, H - 1)

                def over_tiles(row):
                    return row[:].unsqueeze(1).broadcast_to([P, NT, D])

                do(nc.vector.tensor_tensor(x_res[:], x_res[:], over_tiles(bp_row), ALU.add))
                for i in range(2):
                    dve.wait_ge(out_mm, b * 4 + 2 + i + 1)
                    half = x_res[:, 2 * i:2 * i + 2, :].rearrange("p a n -> p (a n)")
                    do(nc.vector.tensor_tensor(half, half, bank[:, i, :], ALU.add))
                layernorm(1, x_res, y_sb)

                dve.wait_ge(gate_exp, b + 1)
                do(nc.vector.tensor_scalar(gate_in, gate_in, 1.0, None, ALU.add))
                do(nc.vector.reciprocal(gate_in, gate_in))
                do(nc.vector.tensor_scalar(gate_in, gate_in, float(NK - 1), None, ALU.mult))
                do(nc.vector.tensor_scalar(low, gate_in, 1.0, None, ALU.is_ge))
                for i in range(2, NK - 1):
                    do(nc.vector.scalar_tensor_tensor(low, gate_in, float(i), low, ALU.is_ge, ALU.add))
                do(nc.vector.tensor_tensor(frac, gate_in, low, ALU.subtract))
                do(nc.vector.tensor_scalar(knot_at, low, 0.0, knot_row[:, 0:1], ALU.is_equal, ALU.mult))
                do(nc.vector.tensor_scalar(step_at, low, 0.0, knot_step[:, 0:1], ALU.is_equal, ALU.mult))
                for i in range(1, NK - 1):
                    do(nc.vector.tensor_scalar(seg, low, float(i), knot_row[:, i:i + 1], ALU.is_equal, ALU.mult))
                    do(nc.vector.tensor_tensor(knot_at, knot_at, seg, ALU.add))
                    do(nc.vector.tensor_scalar(seg, low, float(i), knot_step[:, i:i + 1], ALU.is_equal, ALU.mult))
                    do(nc.vector.tensor_tensor(step_at, step_at, seg, ALU.add))
                do(nc.vector.tensor_tensor(frac, frac, step_at, ALU.mult))
                do(nc.vector.tensor_tensor(gate_in, frac, knot_at, ALU.add))

                def first_max(values, eq, pick):
                    do(nc.vector.tensor_reduce(top, values, AX.X, ALU.max))
                    do(nc.vector.tensor_tensor(eq, values, top.unsqueeze(2).broadcast_to([P, NT, CL]), ALU.is_equal))
                    do(nc.vector.tensor_tensor(eq, eq, first_weight[:].unsqueeze(1).broadcast_to([P, NT, CL]), ALU.mult))
                    do(nc.vector.tensor_reduce(best, eq, AX.X, ALU.max))
                    do(nc.vector.tensor_tensor(pick, eq, best.unsqueeze(2).broadcast_to([P, NT, CL]), ALU.is_equal))

                first_max(gates[:, :, 0:CL], c_eq, c_pick)
                for t in range(NT):
                    st.mark(nc.vector.tensor_tensor(sel_all[:, t, :].rearrange("p (c l) -> p c l", c=CL),
                                                    gates[:, t, CL:ST].rearrange("p (c l) -> p c l", c=CL),
                                                    c_pick[:, t, :].unsqueeze(2).broadcast_to([P, CL, TPC]), ALU.mult))
                st.wait(dve)
                do(nc.vector.tensor_reduce(sel, sel_all.rearrange("p t (c l) -> p t l c", c=CL), AX.X, ALU.add))
                first_max(sel, l_eq, l_pick)
                for t in range(NT):
                    ins = nc.vector.tensor_tensor(expert[:, t, :].rearrange("p (c l) -> p c l", c=CL),
                                                  c_pick[:, t, :].unsqueeze(2).broadcast_to([P, CL, TPC]),
                                                  l_pick[:, t, :].unsqueeze(1).broadcast_to([P, CL, TPC]), ALU.mult)
                    ins.then_inc(expert_ready, 1)

                dve.wait_ge(comp_mm, b + 1)
                nc.vector.tensor_tensor(comp_in, bank[:, 4, 0:2 * NT].rearrange("p (t i) -> p t i", t=NT),
                                        cb2_row[:].unsqueeze(1).broadcast_to([P, NT, 2]), ALU.add).then_inc(comp_b, 1)
                dve.wait_ge(comp_done, b + 1)
                dve.wait_ge(gather_mm, b + 1)

                def column(i):
                    return comp[:, :, i:i + 1].broadcast_to([P, NT, G])

                do(nc.vector.tensor_tensor(hh, bank[:, 0:NT, T_W1:T_W1 + G], column(0), ALU.mult))
                do(nc.vector.tensor_tensor(hh2, bank[:, 0:NT, T_W1 + G:T_B1], column(1), ALU.mult))
                do(nc.vector.tensor_tensor(hh, hh, hh2, ALU.add))
                do(nc.vector.tensor_tensor(hh, bank[:, 0:NT, T_B1:T_W2], hh, ALU.add))
                do(nc.vector.tensor_scalar(hh, hh, 0.0, None, ALU.max))
                do(nc.vector.tensor_tensor(hh, bank[:, 0:NT, T_W2:T_B2], hh, ALU.mult))
                do(nc.vector.tensor_reduce(mag, hh, AX.X, ALU.add))
                do(nc.vector.tensor_tensor(mag, bank[:, 0:NT, T_B2], mag, ALU.add))
                for t in range(NT):
                    st.mark(nc.vector.tensor_scalar(x_dir[:, t, :], bank[:, t, 0:D], mag[:, t:t + 1], scale_col[:, 0:1],
                                                    ALU.mult, ALU.mult))
                st.wait(dve)
                do(nc.vector.tensor_tensor(x_res[:], y_sb[:], x_dir, ALU.add))
                layernorm(2, x_res, x_res)
                do(nc.vector.tensor_tensor(x_res[:], x_res[:], over_tiles(gamma_row), ALU.mult))
                do(nc.vector.tensor_tensor(x_res[:], x_res[:], over_tiles(beta_row), ALU.add))
                do(nc.vector.tensor_tensor(y_sb[:], y_sb[:], x_res[:], ALU.add))
                layernorm(3, y_sb, y_sb)
                st.end()

        @block.tensor
        def _(pe):
            for primed in (vj_mm, pj_mm, sT_mm, s_mm, max_tr[SELF], max_tr[CROSS], o1_mm, pv_mm[SELF], pv_mm[CROSS], p1_tr):
                pe.sem_inc(primed, FIRST)
            mm = nc.tensor.matmul
            pe.wait_ge(const_ready, 1)
            pe.wait_ge(w_in, W_IN)
            pe.wait_ge(sig_ready, 5)
            for k in range(KD):
                last = nc.tensor.transpose(bank[:, 0, TILES * k:TILES * (k + 1)], sig_work[:, 0, P * k:P * (k + 1)],
                                           ident[0:TILES, 0:TILES])
            last.then_inc(sig_tr, 1)
            pe.wait_ge(sig_ready, SIG_STEPS)

            with pe.Fori(0, B) as b:
                def project(dst, lhsT, rhs, tiles=KD):
                    for k in range(tiles):
                        last = mm(dst, lhsT(k), rhs(k), start=(k == 0), stop=(k == tiles - 1))
                    return last

                pe.wait_ge(conv_done, FIRST + b * KD + KD)
                for m in range(KD):
                    project(bank[:, m, :], lambda k: pe_sb[:, k, P * m:P * (m + 1)], lambda k: featA[:, k, :]).then_inc(pe_mm, 1)
                pe.wait_ge(xs_ready, b * KD + KD)
                for i in range(2 * KD):
                    project(bank[:, 2 + i, :], lambda k: qkv_sb[:, k, P * i:P * (i + 1)], lambda k: featB[:, k, :]).then_inc(qk_mm, 1)
                for i in range(NT):
                    last = project(bank[:, 6 + i // 2, D * (i % 2):D * (i % 2 + 1)], lambda k: featB[:, k, P * i:P * (i + 1)],
                                   lambda k: qkv_sb[:, k, 2 * D:3 * D])
                    if i % 2:
                        last.then_inc(v_mm, 1)

                def scores1(h, static):
                    u = b * H + h
                    for t in range(NT):
                        if not static:
                            pe.wait_ge(s1_evac, u * 4 + (t - 3))
                        mm(bank[:, t, :], q1T[:, bass.ds(h * S + P * t, P)],
                           k1T[:, :, bass.ts(h, RH)], start=True, stop=True).then_inc(s1_mm, 1)

                def transpose1(h, p):
                    u = b * H + h
                    pe.wait_ge(p1_evac, FIRST + u * 2)
                    for t in range(NT):
                        pe.wait_ge(p1_ready, FIRST + u * 4 + t + 1)
                        for j in range(4):
                            last = nc.tensor.transpose(bankb(4, 2)[:, S * j + P * t:S * j + P * (t + 1)],
                                                       s1[:, p, t, P * j:P * (j + 1)], identb[:])
                    last.then_inc(p1_tr, 1)

                def pv1(h):
                    u = b * H + h
                    pe.wait_ge(p1_evac, FIRST + u * 2 + 2)
                    pe.wait_ge(o1_evac, FIRST + u)
                    for t in range(NT):
                        for j in range(4):
                            last = mm(bank[:, 6, HD * t:HD * (t + 1)], p1T[:, j, P * t:P * (t + 1)], v1[:, h, j, :],
                                      start=(j == 0), stop=(j == 3))
                    last.then_inc(o1_mm, 1)

                pe.wait_ge(qk1_in, FIRST + (b + 1) * 16 * 2 * KD)
                pe.wait_ge(q1_ready, b * 4 + 4)
                pe.wait_ge(v_evac, b * 2 + 2)
                pe.wait_ge(v1_ready, b * 16 + 16)
                scores1(0, True)
                scores1(1, False)
                transpose1(0, 0)
                with pe.Fori(0, H // 2 - 1) as i:
                    for p in range(2):
                        h = i * 2 + (2 + p)
                        scores1(h, False)
                        pv1(h - 2)
                        transpose1(h - 1, 1 - p)
                pv1(H - 2)
                transpose1(H - 1, 1)
                pv1(H - 1)

                pe.wait_ge(o1_evac, FIRST + (b + 1) * H)
                for t in range(NT):
                    for k in range(KD):
                        last = nc.tensor.transpose(bankb(7)[:, S * k + P * t:S * k + P * (t + 1)],
                                                   o_nat[:, t, P * k:P * (k + 1)], identb[:])
                last.then_inc(feat_tr, 1)
                pe.wait_ge(feat_evac, b * 4 + 1)

                def token_out(w):
                    for t in range(NT):
                        last = project(bank[:, t // 2, D * (t % 2):D * (t % 2 + 1)], lambda k: featA[:, k, P * t:P * (t + 1)],
                                       lambda k: w[:, k, :])
                        if t % 2:
                            last.then_inc(out_mm, 1)

                def to_features(src, first_bank):
                    for t in range(NT):
                        for k in range(KD):
                            last = nc.tensor.transpose(bank[:, first_bank + k, P * t:P * (t + 1)], src[:, t, P * k:P * (k + 1)], ident[:])
                    last.then_inc(feat_tr, 1)

                token_out(out_sb)
                pe.wait_ge(ln_done, FIRST + b * 4 + 1)
                to_features(x_res, 2)
                pe.wait_ge(feat_evac, b * 4 + 2)

                pe.wait_ge(ctx_in, b * 16 + 16)

                def unit(u):
                    stack, m, c0, _ = unit_list[u]
                    if u >= 4:
                        pe.wait_ge(pj_rest, b * UNITS + u - 3)
                    dst = bank[:, 4 + u % 4, :]
                    if u < 6:
                        w = (wq_sb, wk_sb, wcq_sb)[u // 2]
                        project(dst, lambda k: w[:, k, P * m:P * (m + 1)], lambda k: featB[:, k, :]).then_inc(pj_mm, 1)
                    else:
                        mm(dst, wck_sb[:, P * m:P * (m + 1)], ctx_sb[:, c0:c0 + S], start=True, stop=True).then_inc(pj_mm, 1)

                def values(i):
                    if i >= 4:
                        pe.wait_ge(vj_evac, b * (NT + NC) + i - 3)
                    if i < NT:
                        project(bank[:, i % 4, 0:D], lambda k: featB[:, k, P * i:P * (i + 1)], lambda k: wv_sb[:, k, :]).then_inc(vj_mm, 1)
                    else:
                        mm(bank[:, i % 4, 0:D], ctx_sb[:, P * (i - NT):P * (i - NT + 1)], wcv_sb[:], start=True, stop=True).then_inc(vj_mm, 1)

                for u in range(4):
                    unit(u)
                for i in range(NT):
                    values(i)
                for u in range(4, UNITS):
                    unit(u)
                for i in range(NT, NT + NC):
                    values(i)

                def scores(kind, h, j, static=False):
                    idx = (b * H + h) * 12 + 4 * kind + j
                    if not (static and idx_free(kind, j)):
                        pe.wait_ge(max_done, idx - 1)
                    if kind == SELF:
                        n = P * (j + 1)
                        mm(bank[:, j % 2, 0:n], q_self[0:SHIFT, h, P * j:n], k_self[0:SHIFT, h, 0:n], start=True, stop=False)
                        mm(bank[:, j % 2, P * j:n], identb[:], mask_q[:], start=False, stop=True).then_inc(s_mm, 1)
                    else:
                        mm(bank[:, j % 2, :], q_cross[0:SHIFT, h, P * (j // 2):P * (j // 2 + 1)],
                           k_cross[0:SHIFT, h, S * (j % 2):S * (j % 2 + 1)], start=True, stop=True).then_inc(s_mm, 1)

                def idx_free(kind, j):
                    return kind == SELF and j < 2

                def max_transpose(kind, h):
                    n = b * H + h
                    pe.wait_ge(parts_ready[kind], FIRST + n + 1)
                    pe.wait_ge(max_rows, FIRST + n * 2 + kind)
                    for t in range(NT):
                        last = nc.tensor.transpose(bankb(7)[0:3, S * kind + P * t:S * kind + P * (t + 1)],
                                                   max_parts[:, kind, t, :], identb[:])
                    last.then_inc(max_tr[kind], 1)

                def scoresT(kind, h, u, static=False):
                    n = b * H + h
                    if u == 0:
                        pe.wait_ge(max_rows, FIRST + n * 2 + kind + 1)
                    if not (static and kind == SELF and u < 2):
                        pe.wait_ge(pT_ready, n * 8 + 4 * kind + u - 1)
                    c = 2 + 2 * (u % 2)
                    if kind == SELF:
                        w = S - P * u
                        mm(bank[:, c, 0:w], k_self[0:ROWS, h, P * u:P * (u + 1)], q_self[0:ROWS, h, P * u:S], start=True, stop=False)
                        mm(bank[:, c, 0:P], identb[:], mask_k[:], start=False, stop=True).then_inc(sT_mm, 1)
                    else:
                        for i in range(2):
                            t = 2 * u + i
                            last = mm(bank[:, c + i, :], k_cross[0:ROWS, h, P * t:P * (t + 1)], q_cross[0:ROWS, h, :], start=True, stop=True)
                        last.then_inc(sT_mm, 1)

                def pv(kind, h, t):
                    n = b * H + h
                    if t == 0:
                        pe.wait_ge(pT_ready, n * 8 + 4 * kind + 4)
                        pe.wait_ge(y_done, FIRST + n * 2 + kind)
                    pT, v, tiles = (pT_self, v_self, t + 1) if kind == SELF else (pT_cross, v_cross, NC)
                    for j in range(tiles):
                        last = mm(bank[:, 6, 32 * t:32 * t + HD + 1], pT[:, j, P * t:P * (t + 1)], v[:, j, h, :],
                                  start=(j == 0), stop=(j == tiles - 1))
                    if t == NT - 1:
                        last.then_inc(pv_mm[kind], 1)

                def slot(kind, h, first=False, last=False):
                    for u in range(4):
                        scoresT(kind, h, u, first)
                        if not last:
                            if kind == SELF:
                                scores(SELF, h + 1, u)
                            else:
                                scores(CROSS, h + 1, 2 * u)
                                scores(CROSS, h + 1, 2 * u + 1)
                        if u == 1:
                            if kind == SELF:
                                max_transpose(CROSS, h)
                            elif not last:
                                max_transpose(SELF, h + 1)
                        if kind == CROSS:
                            pv(SELF, h, u)
                        elif not first:
                            pv(CROSS, h - 1, u)

                pe.wait_ge(stack_in[SELF], (b + 1) * STACK_IN[SELF])
                pe.wait_ge(vj_evac, (b + 1) * (NT + NC))
                for j in range(4):
                    scores(SELF, 0, j, static=True)
                pe.wait_ge(stack_in[CROSS], (b + 1) * STACK_IN[CROSS])
                for j in range(8):
                    scores(CROSS, 0, j)
                max_transpose(SELF, 0)
                slot(SELF, 0, first=True)
                slot(CROSS, 0)
                with pe.Fori(1, H - 1) as h:
                    slot(SELF, h)
                    slot(CROSS, h)
                slot(SELF, H - 1, last=True)
                slot(CROSS, H - 1, last=True)
                for t in range(NT):
                    pv(CROSS, H - 1, t)

                pe.wait_ge(y_step, (b + 1) * H * 3)
                to_features(y_sb, 2)
                pe.wait_ge(feat_evac, b * 4 + 3)
                token_out(wp_sb)
                pe.wait_ge(ln_done, FIRST + b * 4 + 2)
                to_features(y_sb, 4)
                pe.wait_ge(feat_evac, b * 4 + 4)
                for t in range(NT):
                    last = project(bank[:, 6, ST * t:ST * (t + 1)], lambda k: featB[:, k, P * t:P * (t + 1)], lambda k: sigT[:, k, :])
                last.then_inc(route_mm, 1)
                project(bank[0:HID, 7, :], lambda k: cw1_sb[:, k, :], lambda k: featB[:, k, :]).then_inc(gelu_in, 1)
                pe.wait_ge(gelu_done, b + 1)
                for t in range(NT):
                    last = mm(bank[:, 4, 2 * t:2 * t + 2], hT[:, P * t:P * (t + 1)], cw2_sb[:], start=True, stop=True)
                last.then_inc(comp_mm, 1)
                pe.wait_ge(expert_ready, b * NT + NT)
                own_wait(nc.tensor)
                for t in range(NT):
                    last = nc.tensor.transpose(bank[0:TILES, 5, P * t:P * (t + 1)], expert[:, t, :], ident[:])
                last.then_inc(expert_tr, 1)
                pe.wait_ge(expert_evac, b + 1)
                for t in range(NT):
                    last = mm(bank[:, t, 0:TABLE], expertT[:, P * t:P * (t + 1)], table[:], start=True, stop=True)
                last.then_inc(gather_mm, 1)


_OUT = ((8, 512, 256), "float32")


def kernel(**inputs):
    import numpy as np
    import concourse.bacc as bacc
    from concourse.bass_utils import run_bass_kernel_spmd

    nc = bacc.Bacc("TRN2", target_bir_lowering=False, num_devices=1)
    given = {k: np.asarray(v) for k, v in inputs.items()}

    def attn(n):
        return given["L0_attn_" + n]

    arrays = {"x": given["x"], "xT": given["x"].transpose(0, 2, 1), "ctxT": given["ctx_512"].transpose(0, 2, 1),
              "conv_w": attn("conv_w")[:, 0, :, 1], "peT": attn("pe_w").T, "qkvT": attn("qkv_w").T, "outT": attn("out_w").T}
    for n in ("Wk", "bk", "Wq", "bq", "Wv", "bv", "Wck", "bck", "Wcq", "bcq", "Wcv", "bcv", "Wp", "bp"):
        arrays[n] = given["L0_xattn_" + n]
    for n in ("signatures_raw", "knot_values", "temperature", "compress_w1", "compress_b1", "compress_w2", "compress_b2",
              "spline_w1", "spline_b1", "spline_w2", "spline_b2", "directions", "norm_gamma", "norm_beta", "output_scale"):
        arrays[n] = given["L0_ffn_" + n]
    for n in ("bq", "bk", "bcq", "bck"):
        arrays[n] = arrays[n].reshape(2, 128).T
    arrays = {n: np.ascontiguousarray(a) for n, a in arrays.items()}
    args = [nc.dram_tensor(n, a.shape, mybir.dt.from_np(a.dtype), kind="ExternalInput").ap() for n, a in arrays.items()]
    out = nc.dram_tensor("out", _OUT[0], mybir.dt.float32, kind="ExternalOutput").ap()
    decoder_layer(nc, *args, out)
    return run_bass_kernel_spmd(nc, [arrays], core_ids=[0]).results[0]["out"]
```

```python
import concourse.bass as bass
from concourse import mybir
from contextlib import ExitStack


class Steps:

    def __init__(self, sem, per_batch, b):
        self.sem, self.per_batch, self.b, self.n = sem, per_batch, b, 0

    def mark(self, instruction):
        instruction.then_inc(self.sem, 1)
        self.n += 1

    def wait(self, engine):
        engine.wait_ge(self.sem, self.b * self.per_batch + self.n)

    def end(self):
        assert self.n == self.per_batch, (self.n, self.per_batch)


def decoder_layer(nc, x, xT, ctxT, conv_w, peT, qkvT, outT, Wk, bk, Wq, bq, Wv, bv, Wck, bck, Wcq, bcq,
                  Wcv, bcv, Wp, bp, signatures, knots, temperature, cw1, cb1, cw2, cb2, sw1, sb1, sw2, sb2,
                  directions, gamma, beta, output_scale, out):
    fp32 = mybir.dt.float32
    bf16 = mybir.dt.bfloat16
    ALU = mybir.AluOpType
    ACT = mybir.ActivationFunctionType
    AX = mybir.AxisListType

    B, S, D = x.shape
    CC, SC = ctxT.shape[1:]
    H, HD, P = 16, 16, 128
    KD = D // P
    NT = S // P
    NC = SC // P
    RH = S // H
    TILES = signatures.shape[0]
    CL, TPC = 8, TILES // 8
    NK = knots.shape[0]
    HID = cw1.shape[1]
    G = sw1.shape[2]
    SCALE = 1.0 / HD ** 0.5
    SHIFT = 6 * HD
    ROWS = SHIFT + 3
    RUNS = [(0, 3, 0, 0), (3, 2, 1, 0), (5, 1, 2, 0)]
    MASKED = -1.0e30
    EPS = 1e-5
    ST = CL + TILES
    T_W1 = D
    T_B1 = T_W1 + 2 * G
    T_W2 = T_B1 + G
    T_B2 = T_W2 + G
    TABLE = T_B2 + 1
    SELF, CROSS = 0, 1
    GROUP = 32
    ROUNDS = [[(CROSS, 0, 0), (CROSS, 1, 1), (CROSS, 2, 2), (SELF, 0, 3)],
              [(CROSS, 3, 0), (CROSS, 4, 1), (CROSS, 5, 2), (SELF, 1, 3)],
              [(CROSS, 6, 0), (CROSS, 7, 1), (SELF, 2, 3), (SELF, 3, 3)]]
    GROUP_TILES = [[(k, t) for r in ROUNDS for k, t, g in r if g == group] for group in range(4)]
    UNITS = 10
    PART_BUFS = 4
    FIRST = 1
    PV_FIRST = 5
    DVE_STEPS = 100
    SIG_STEPS = 20
    POOL_STEPS = 4

    ctx = ExitStack()
    with ctx:
        def sb(name, shape, dt=fp32):
            return ctx.enter_context(nc.sbuf_tensor(name, shape, dt))

        def sem(name):
            return ctx.enter_context(nc.semaphore(name))

        conv_sb = sb("conv_sb", [P, KD, 3])
        pe_sb = sb("pe_sb", [P, KD, D])
        qkv_sb = sb("qkv_sb", [P, KD, 3 * D])
        out_sb = sb("out_sb", [P, KD, D])
        wq_sb, wk_sb, wv_sb = sb("wq_sb", [P, KD, D]), sb("wk_sb", [P, KD, D]), sb("wv_sb", [P, KD, D])
        wcq_sb, wck_sb, wcv_sb = sb("wcq_sb", [P, KD, D]), sb("wck_sb", [P, D]), sb("wcv_sb", [P, D])
        wp_sb = sb("wp_sb", [P, KD, D])
        bq_col, bk_col = sb("bq_col", [P, KD]), sb("bk_col", [P, KD])
        bcq_col, bck_col = sb("bcq_col", [P, KD]), sb("bck_col", [P, KD])
        bv_row, bcv_row, bp_row = sb("bv_row", [P, D]), sb("bcv_row", [P, D]), sb("bp_row", [P, D])
        gamma_row, beta_row = sb("gamma_row", [P, D]), sb("beta_row", [P, D])
        sig_raw = sb("sig_raw", [TILES, D])
        sig_work = sb("sig_work", [TILES, 2, D])
        sigT = sb("sigT", [P, KD, ST])
        sig_sum = sb("sig_sum", [P, 2, KD, CL])
        knot_row, knot_step = sb("knot_row", [P, NK]), sb("knot_step", [P, NK - 1])
        temp = sb("temp", [P, 3])
        scale_col = sb("scale_col", [P, 1])
        cw1_sb, cb1_col = sb("cw1_sb", [P, KD, HID]), sb("cb1_col", [HID, 1])
        cw2_sb, cb2_row = sb("cw2_sb", [HID, 2]), sb("cb2_row", [P, 2])
        table = sb("table", [TILES, TABLE])
        ident, identb = sb("ident", [P, P]), sb("identb", [P, P], bf16)
        mask_f = sb("mask_f", [P, P])
        mask_q, mask_k = sb("mask_q", [P, P], bf16), sb("mask_k", [P, P], bf16)
        first_weight = sb("first_weight", [P, CL])
        minus_half = sb("minus_half", [P, NT])

        xT_pad = sb("xT_pad", [P, KD, S + 2])
        ctx_sb = sb("ctx_sb", [P, SC])
        featA = sb("featA", [P, KD, S])
        featB = sb("featB", [P, KD, S])
        x_res = sb("x_res", [P, NT, D])
        y_sb = sb("y_sb", [P, NT, D])
        shared = sb("shared", [P, 2048])
        qk_nat = shared[:, 0:1024].bitcast(bf16).rearrange("p (i n) -> p i n", i=2 * KD)
        v_nat = shared[:, 1024:1536].bitcast(bf16).rearrange("p (t d) -> p t d", t=NT)
        o_nat = shared[:, 1536:2048].bitcast(bf16).rearrange("p (t d) -> p t d", t=NT)
        v1 = sb("v1", [P, H, 4, HD], bf16)
        k1T = sb("k1T", [P, 16, S], bf16)
        q_self, k_self = sb("q_self", [P, H, S], bf16), sb("k_self", [P, H, S], bf16)
        q_cross, k_cross = sb("q_cross", [P, H, S], bf16), sb("k_cross", [P, H, SC], bf16)
        q1T = q_cross[:, :, :].rearrange("p h n -> p (h n)")
        q1_chunks = k_self[0:HD, :, :]
        xs = q_self[:, 0:4 * KD // 2, :].rearrange("p h n -> p (h n)").bitcast(fp32).rearrange("p (k n) -> p k n", k=KD)
        v_all = sb("v_all", [P, NT + NC, H, HD + 1])
        v_head = [featB[:, p, 0:(NT + NC) * GROUP].rearrange("p (t j) -> p t j", j=GROUP) for p in range(2)]
        o_groups = featA[:, 0, :]
        gather_groups = sb("gather_groups", [P, 2 * (HD + 1)])
        work = sb("work", [P, 6144])
        y_tmp = sb("y_tmp", [P, NT, 2, HD])
        max1 = sb("max1", [P, 2, NT], bf16)
        neg1, den1, rden1 = sb("neg1", [P, 2, NT]), sb("den1", [P, 2, NT]), sb("rden1", [P, 2, NT])
        denb1 = sb("denb1", [P, 2, NT], bf16)
        max_self, max_half = sb("max_self", [P, NT]), sb("max_half", [P, NT, 2])
        max_cross = sb("max_cross", [P, NT])
        max_rest = sb("max_rest", [P, 2, 2, NT])
        max_parts = sb("max_parts", [P, 2, NT, 3], bf16)
        rec = sb("rec", [P, NT, 2])
        stats, mv = sb("stats", [P, NT, 6]), sb("mv", [P, NT, 2])
        ln_var, ln_r = sb("ln_var", [P, NT]), sb("ln_r", [P, NT])

        s1 = work[:, 0:2048].bitcast(bf16).rearrange("p (a t n) -> p a t n", a=2, t=NT)
        e1 = work[:, 2048:4096].bitcast(bf16).rearrange("p (a t n) -> p a t n", a=2, t=NT)
        p1T = work[:, 4096:5120].bitcast(bf16).rearrange("p (t n) -> p t n", t=4)
        parts = work[:, 0:3072].bitcast(bf16).rearrange("p (a s n) -> p a s n", a=PART_BUFS, s=3)
        rest = work[:, 3072:4608].rearrange("p (a n) -> p a n", a=3)
        pT_self = [w.rearrange("p (t n) -> p t n", t=NT) for w in (work[:, 0:2048], shared[:])]
        pT_cross = work[:, 2048:6144].rearrange("p (t n) -> p t n", t=NC)
        N = NT * ST

        def piece(i, n, t=NT):
            return work[:, 512 * i:512 * i + n].rearrange("p (t n) -> p t n", t=t)

        gate_in, low, frac, knot_at, step_at, seg = (work[:, 512 * i:512 * i + N] for i in range(6))
        gates = piece(0, N)
        c_eq, c_pick, l_eq, l_pick, sel = (piece(6, 5 * NT * CL)[:, :, CL * i:CL * (i + 1)] for i in range(5))
        sel_all = piece(7, NT * TILES)
        expert = piece(8, NT * TILES)
        top, best = work[:, 4608:4608 + NT], work[:, 4612:4612 + NT]
        comp_in = work[:, 4640:4640 + 2 * NT].rearrange("p (t i) -> p t i", t=NT)
        comp = work[:, 4656:4656 + 2 * NT].rearrange("p (t i) -> p t i", t=NT)
        x_dir = work[:, 0:NT * D].rearrange("p (t d) -> p t d", t=NT)
        hh, hh2 = work[:, 5120:5184].rearrange("p (t g) -> p t g", t=NT), work[:, 5184:5248].rearrange("p (t g) -> p t g", t=NT)
        mag = work[:, 5248:5248 + NT]
        hT = work[0:HID, 5632:6144]
        expertT = work[0:TILES, 3072:3584]

        bank = ctx.enter_context(nc.psum_tensor("bank", [P, 8, 512], fp32))

        def bankb(i, n=1):
            return bank[:, i:i + n, :].rearrange("p a n -> p (a n)").bitcast(bf16)

        waited = {e: sem(f"waited_{n}") for n, e in (("pe", nc.tensor), ("dve", nc.vector), ("pool", nc.gpsimd), ("sp", nc.sync))}
        w_in, x_in, xn_in, ctx_in = sem("w_in"), sem("x_in"), sem("xn_in"), sem("ctx_in")
        const_ready, init_step = sem("const_ready"), sem("init_step")
        sig_tr, sig_ready = sem("sig_tr"), sem("sig_ready")
        dve_step, pool_step = sem("dve_step"), sem("pool_step")
        conv_step, conv_done, pe_mm, xs_ready = (sem(n) for n in ("conv_step", "conv_done", "pe_mm", "xs_ready"))
        qk_mm, qk_evac, v_mm, v_evac = sem("qk_mm"), sem("qk_evac"), sem("v_mm"), sem("v_evac")
        qk1_in, v1_ready = sem("qk1_in"), sem("v1_ready")
        s1_mm, s1_evac, s1_neg, e1_ready = sem("s1_mm"), sem("s1_evac"), sem("s1_neg"), sem("e1_ready")
        n1_step, p1_ready, p1_tr, p1_evac = sem("n1_step"), sem("p1_ready"), sem("p1_tr"), sem("p1_evac")
        o1_mm, o1_evac = sem("o1_mm"), sem("o1_evac")
        feat_tr, feat_evac = sem("feat_tr"), sem("feat_evac")
        out_mm, res_done = sem("out_mm"), sem("res_done")
        ln_stats, ln_rstd, ln_done = sem("ln_stats"), sem("ln_rstd"), sem("ln_done")
        pj_mm, pj_hi, pj_rest, pj_mid, pj_parts = (sem(n) for n in ("pj_mm", "pj_hi", "pj_rest", "pj_mid", "pj_parts"))
        stack_in = [sem("stack_in_self"), sem("stack_in_cross")]
        qk1_out = [sem(f"qk1_out{i}") for i in range(4)]
        parts_out = [sem(f"parts_out{i}") for i in range(PART_BUFS)]
        vj_mm, vj_evac = sem("vj_mm"), sem("vj_evac")
        s_mm, max_done = sem("s_mm"), sem("max_done")
        cross_max, q1_ready = sem("cross_max"), sem("q1_ready")
        parts_ready = [sem("parts_self"), sem("parts_cross")]
        max_tr = [sem("max_tr_self"), sem("max_tr_cross")]
        max_rows, m_step = sem("max_rows"), sem("m_step")
        sT_mm, pT_ready = sem("sT_mm"), sem("pT_ready")
        pv_mm, pv_evac, v_ready, v_pad, o_mm = (sem(n) for n in ("pv_mm", "pv_evac", "v_ready", "v_pad", "o_mm"))
        y_step, y_done = sem("y_step"), sem("y_done")
        route_mm, gelu_in, gelu_done, comp_mm = sem("route_mm"), sem("gelu_in"), sem("gelu_done"), sem("comp_mm")
        comp_b, comp_done, gate_exp = sem("comp_b"), sem("comp_done"), sem("gate_exp")
        expert_ready, expert_tr, expert_evac, gather_mm = (sem(n) for n in ("expert_ready", "expert_tr", "expert_evac", "gather_mm"))
        out_dma = sem("out_dma")

        def own_wait(engine):
            engine.sem_inc(waited[engine], 1)

        def wide(w):
            return w.rearrange("(k p) n -> p k n", p=P)

        weights = [(conv_sb[:], wide(conv_w)), (pe_sb[:], wide(peT)), (qkv_sb[:], wide(qkvT)),
                   (out_sb[:], wide(outT)), (wq_sb[:], wide(Wq)), (wk_sb[:], wide(Wk)), (wv_sb[:], wide(Wv)),
                   (wcq_sb[:], wide(Wcq)), (wck_sb[:], Wck), (wcv_sb[:], Wcv), (wp_sb[:], wide(Wp)),
                   (bq_col[:], bq), (bk_col[:], bk), (bcq_col[:], bcq), (bck_col[:], bck),
                   (bv_row[:], bv.partition_broadcast(P)), (bcv_row[:], bcv.partition_broadcast(P)),
                   (bp_row[:], bp.partition_broadcast(P)), (gamma_row[:], gamma.partition_broadcast(P)),
                   (beta_row[:], beta.partition_broadcast(P)), (sig_raw[:], signatures),
                   (knot_row[:], knots.partition_broadcast(P)), (temp[:, 0:1], temperature.partition_broadcast(P)),
                   (scale_col[:], output_scale.partition_broadcast(P)), (cw1_sb[:], wide(cw1)),
                   (cb1_col[:], cb1.rearrange("(p o) -> p o", o=1)), (cw2_sb[:], cw2),
                   (cb2_row[:], cb2.partition_broadcast(P)), (table[:, 0:D], directions),
                   (table[:, T_W1:T_B1], sw1.rearrange("t i g -> t (i g)")), (table[:, T_B1:T_W2], sb1),
                   (table[:, T_W2:T_B2], sw2.rearrange("t g o -> t (g o)")), (table[:, T_B2:TABLE], sb2)]
        W_IN = 16 * len(weights)

        unit_list = [(q_self, 0, 0), (q_self, 1, 0), (k_self, 0, 0), (k_self, 1, 0),
                     (q_cross, 0, 0), (q_cross, 1, 0), (k_cross, 0, 0), (k_cross, 1, 0), (k_cross, 0, S), (k_cross, 1, S)]
        unit_bias = [bq_col, bq_col, bk_col, bk_col, bcq_col, bcq_col, bck_col, bck_col, bck_col, bck_col]
        STACK_IN = (16 * len(RUNS) * 4, 16 * len(RUNS) * (UNITS - 4))
        HT = H // KD

        def parts_stored(b, u):
            per_batch = len(range(u % PART_BUFS, UNITS, PART_BUFS))
            return (b * per_batch + u // PART_BUFS + 1) * 16

        qk_dram = nc.dram_tensor("qk_dram", (2 * KD, P, S), bf16, kind="Internal").ap()
        parts_dram = nc.dram_tensor("parts_dram", (UNITS, 3, P, S), bf16, kind="Internal").ap()

        block = ctx.enter_context(nc.Block())

        @block.sync
        def _(sp):
            for primed in (qk1_in, out_dma):
                sp.sem_inc(primed, FIRST)
            for dst, src in weights:
                sp.dma_start(dst, src).then_inc(w_in, 16)

            def load_x(b):
                sp.wait_ge(conv_done, FIRST + b * KD)
                for k in range(KD):
                    sp.dma_start(xT_pad[:, k, 1:S + 1], xT[b, k * P:(k + 1) * P, :]).then_inc(x_in, 16)

            def chunks(b):
                sp.wait_ge(sT_mm, FIRST + b * H * 8)
                own_wait(nc.sync)
                sp.wait_ge(s_mm, FIRST + b * H * 12)
                own_wait(nc.sync)
                for i in range(2 * KD):
                    sp.wait_ge(qk_evac, b * 2 * KD + i + 1)
                    sp.dma_start(qk_dram[i], qk_nat[:, i, :]).then_inc(qk1_out[i], 16)
                for i in range(2 * KD):
                    sp.wait_ge(qk1_out[i], b * 16 + 16)
                    dst = (q1_chunks if i < KD else k1T)[0:HD, 8 * (i % KD):8 * (i % KD) + 8, :]
                    sp.dma_start(dst, qk_dram[i].rearrange("(c j) s -> j c s", j=HD)).then_inc(qk1_in, 16)

            def batch(b, last=False):
                sp.wait_ge(vj_mm, FIRST + b * (NT + NC))
                own_wait(nc.sync)
                sp.wait_ge(pj_mm, FIRST + b * UNITS)
                own_wait(nc.sync)
                sp.dma_start(ctx_sb[:], ctxT[b]).then_inc(ctx_in, 16)
                sp.wait_ge(ln_done, FIRST + b * 4)
                sp.dma_start(x_res[:], x[b].rearrange("(t p) d -> p t d", p=P)).then_inc(xn_in, 16)
                if not last:
                    load_x(b + 1)
                sp.wait_ge(s1_mm, (b + 1) * H * NT)
                own_wait(nc.sync)
                for u in range(UNITS + 1):
                    if u < UNITS:
                        sp.wait_ge(pj_parts, b * UNITS + u + 1)
                        sp.dma_start(parts_dram[u].rearrange("s p n -> p s n"), parts[:, u % PART_BUFS]).then_inc(parts_out[u % PART_BUFS], 16)
                    if u > 0:
                        stack, m, c0 = unit_list[u - 1]
                        sp.wait_ge(parts_out[(u - 1) % PART_BUFS], parts_stored(b, u - 1))
                        for group, n, q_part, k_part in RUNS:
                            dst = stack[HD * group:HD * (group + n), HT * m:HT * (m + 1), c0:c0 + S]
                            if stack is q_self or stack is q_cross:
                                dst = dst.rearrange("p h n -> p (h n)")
                                src = parts_dram[u - 1, q_part].rearrange("(j h) n -> j (h n)", h=HT).unsqueeze(0).broadcast_to([n, HD, HT * S])
                            else:
                                src = parts_dram[u - 1, k_part:k_part + n].rearrange("s (j h) n -> (s j) h n", h=HT)
                            sp.dma_start(dst, src).then_inc(stack_in[SELF if u <= 4 else CROSS], 16)
                if not last:
                    chunks(b + 1)
                sp.wait_ge(ln_done, FIRST + 4 * (b + 1))
                sp.dma_start(out[b].rearrange("(t p) d -> p t d", p=P), y_sb[:]).then_inc(out_dma, 16)

            sp.wait_ge(const_ready, 1)
            load_x(0)
            chunks(0)
            with sp.Fori(0, B - 1) as b:
                batch(b)
            batch(B - 1, last=True)
            sp.wait_ge(out_dma, FIRST + 16 * B)

        @block.gpsimd
        def _(pool):
            for primed in (parts_ready[SELF], parts_ready[CROSS]):
                pool.sem_inc(primed, FIRST)
            n = [0]

            def init(ins):
                ins.then_inc(init_step, 1)
                n[0] += 1
                pool.wait_ge(init_step, n[0])

            init(nc.gpsimd.memset(ident[:], 0.0))
            init(nc.gpsimd.affine_select(out=ident[:], in_=ident[:], compare_op=ALU.not_equal, fill=1.0, base=0,
                                         pattern=[[-1, P]], channel_multiplier=1))
            init(nc.gpsimd.tensor_copy(identb[:], ident[:]))
            init(nc.gpsimd.memset(mask_f[:], 0.0))
            init(nc.gpsimd.affine_select(out=mask_f[:], in_=mask_f[:], compare_op=ALU.is_ge, fill=MASKED, base=0,
                                         pattern=[[-1, P]], channel_multiplier=1))
            init(nc.gpsimd.tensor_copy(mask_q[:], mask_f[:]))
            init(nc.gpsimd.memset(mask_f[:], 0.0))
            init(nc.gpsimd.affine_select(out=mask_f[:], in_=mask_f[:], compare_op=ALU.is_ge, fill=MASKED, base=0,
                                         pattern=[[1, P]], channel_multiplier=-1))
            init(nc.gpsimd.tensor_copy(mask_k[:], mask_f[:]))
            init(nc.gpsimd.iota(first_weight[:], pattern=[[-1, CL]], base=CL, channel_multiplier=0,
                                allow_small_or_imprecise_dtypes=True))
            init(nc.gpsimd.memset(minus_half[:], -0.5))
            init(nc.gpsimd.memset(xT_pad[:], 0.0))
            init(nc.gpsimd.memset(k1T[:], 0.0))
            init(nc.gpsimd.memset(q1T, 0.0))
            init(nc.gpsimd.memset(v_all[:, :, :, HD:HD + 1], 1.0))
            init(nc.gpsimd.tensor_copy(gather_groups[:, 0:HD + 1], ident[:, 3 * GROUP:3 * GROUP + HD + 1]))
            init(nc.gpsimd.tensor_copy(gather_groups[:, HD + 1:], ident[:, 0:HD + 1]))
            for g in (1, 2):
                init(nc.gpsimd.tensor_tensor(gather_groups[:, HD + 1:], gather_groups[:, HD + 1:],
                                             ident[:, g * GROUP:g * GROUP + HD + 1], ALU.add))
            init(nc.gpsimd.memset(k_self[SHIFT:P, :, :], -1.0))
            init(nc.gpsimd.memset(k_cross[SHIFT:P, :, :], -1.0))
            nc.gpsimd.memset(work[:, 0:1], 0.0).then_inc(const_ready, 1)

            def first_values(b):
                pool.wait_ge(v_evac, b * 2 + 2)
                own_wait(nc.gpsimd)
                for q in range(4):
                    for a in range(4):
                        src = v_nat[RH * q:RH * (q + 1), :, :].rearrange("p g (t a j) -> p g t a j", t=4, a=4)[:, :, :, a, :]
                        dst = v1[RH * a:RH * (a + 1), :, :, :].rearrange("p (g q) t j -> p g q t j", q=4)[:, :, q]
                        nc.gpsimd.tensor_copy(dst, src).then_inc(v1_ready, 1)
                pool.wait_ge(v1_ready, (b + 1) * 16)
                own_wait(nc.gpsimd)

            def batch(b, last=False):
                def rstd(k):
                    pool.wait_ge(ln_stats, b * 16 + 4 * k + 4)
                    own_wait(nc.gpsimd)
                    nc.gpsimd.tensor_scalar(ln_var[:], mv[:, :, 1], EPS, None, ALU.add).then_inc(pool_step, 1)
                    pool.wait_ge(pool_step, b * POOL_STEPS + k + 1)
                    nc.gpsimd.tensor_tensor(ln_r[:], ln_var[:], minus_half[:], ALU.pow).then_inc(ln_rstd, 1)

                rstd(0)
                pool.wait_ge(pj_mm, FIRST + (b + 1) * UNITS)
                own_wait(nc.gpsimd)
                pool.wait_ge(vj_mm, FIRST + (b + 1) * (NT + NC))
                own_wait(nc.gpsimd)
                for p in range(2):
                    nc.gpsimd.memset(v_head[p][:, :, HD + 1:], 0.0).then_inc(v_pad, 1)
                pool.wait_ge(vj_evac, (b + 1) * (NT + NC))
                own_wait(nc.gpsimd)
                with pool.Fori(0, H // 2) as i:
                    for p in range(2):
                        h = i * 2 + p
                        u = b * H + h
                        for kind in (SELF, CROSS):
                            if kind == SELF:
                                pool.wait_ge(max_done, u * 12 + 4)
                            else:
                                pool.wait_ge(cross_max, u + 1)
                            pool.wait_ge(max_tr[kind], FIRST + u)
                            own_wait(nc.gpsimd)
                            step = u * 6 + 3 * kind
                            top_row = max_self if kind == SELF else max_cross
                            part = max_parts[:, kind, :, :]
                            nc.gpsimd.tensor_copy(part[:, :, 0], top_row[:]).then_inc(m_step, 1)
                            pool.wait_ge(m_step, step + 1)
                            nc.gpsimd.tensor_tensor(max_rest[:, kind, 0, :], top_row[:], part[:, :, 0], ALU.subtract).then_inc(m_step, 1)
                            pool.wait_ge(m_step, step + 2)
                            own_wait(nc.gpsimd)
                            nc.gpsimd.tensor_copy(part[:, :, 1], max_rest[:, kind, 0, :]).then_inc(m_step, 1)
                            pool.wait_ge(m_step, step + 3)
                            nc.gpsimd.tensor_tensor(part[:, :, 2], max_rest[:, kind, 0, :], part[:, :, 1], ALU.subtract).then_inc(parts_ready[kind], 1)
                        pool.wait_ge(pv_mm, PV_FIRST + 4 * u - 4)
                        own_wait(nc.gpsimd)
                        nc.gpsimd.tensor_copy(v_head[p][:, :, 0:HD + 1], v_all[:, :, h, :]).then_inc(v_ready, 1)
                rstd(1)
                if not last:
                    pool.wait_ge(ln_rstd, b * 4 + 2)
                    own_wait(nc.gpsimd)
                    first_values(b + 1)
                rstd(2)
                rstd(3)

            first_values(0)
            with pool.Fori(0, B - 1) as b:
                batch(b)
            batch(B - 1, last=True)

        @block.scalar
        def _(act):
            for primed in (p1_evac,):
                act.sem_inc(primed, FIRST)
            act.wait_ge(w_in, W_IN)
            act.wait_ge(const_ready, 1)
            def first_qk(b, *tiles):
                for i in tiles:
                    act.wait_ge(qk_mm, b * 2 * KD + i + 1)
                    if i == 0:
                        act.wait_ge(qk1_in, FIRST + b * 16 * 2 * KD)
                    nc.scalar.copy(qk_nat[:, i, :], bank[:, 6 + i % 2, :]).then_inc(qk_evac, 1)

            def first_v(b):
                for i in range(2):
                    act.wait_ge(v_mm, b * 2 + i + 1)
                    nc.scalar.copy(v_nat[:, 2 * i:2 * i + 2, :].rearrange("p a n -> p (a n)"), bank[:, 4 + i, :]).then_inc(v_evac, 1)

            def first_queries(b):
                act.wait_ge(qk1_in, FIRST + (b + 1) * 16 * 2 * KD)
                for q in range(4):
                    nc.scalar.copy(q1T[0:HD, S * 4 * q:S * 4 * (q + 1)].rearrange("p (s c) -> p c s", c=16),
                                   q1_chunks[:, :, P * q:P * (q + 1)]).then_inc(q1_ready, 1)

            def batch(b, last=False):
                def exp1(h, p):
                    u = b * H + h
                    act.wait_ge(s1_neg, u + 1)
                    if not (isinstance(h, int) and h == 0):
                        act.wait_ge(p1_ready, FIRST + 4 * u - 4)
                    for t in range(NT):
                        nc.scalar.activation(e1[:, p, t, :], s1[:, p, t, :], ACT.Exp, bias=neg1[:, p, t:t + 1],
                                             scale=SCALE, accum_out=den1[:, p, t:t + 1]).then_inc(e1_ready, 1)

                def evac1(h):
                    u = b * H + h
                    act.wait_ge(p1_tr, FIRST + u + 1)
                    act.wait_ge(o1_mm, FIRST + u)
                    for i in range(2):
                        nc.scalar.copy(p1T[:, 2 * i:2 * i + 2, :].rearrange("p a n -> p (a n)"), bankb(4 + i)).then_inc(p1_evac, 1)

                exp1(0, 0)
                with act.Fori(0, H // 2 - 1) as i:
                    for n in range(2):
                        h = i * 2 + (n + 1)
                        exp1(h, (n + 1) % 2)
                        evac1(h - 1)
                exp1(H - 1, 1)
                evac1(H - 2)
                evac1(H - 1)

                def features(k, dst, src):
                    act.wait_ge(feat_tr, b * 4 + k + 1)
                    nc.scalar.copy(dst[:].rearrange("p k n -> p (k n)"), src).then_inc(feat_evac, 1)

                features(0, featA, bankb(7))
                features(1, featB, bank[:, 2:4, :].rearrange("p a n -> p (a n)"))

                def high(u):
                    m = unit_list[u][1]
                    act.wait_ge(pj_mm, FIRST + b * UNITS + u + 1)
                    if u == 0:
                        act.wait_ge(pv_mm, PV_FIRST + b * 4 * H)
                    elif u >= PART_BUFS:
                        act.wait_ge(parts_out[u % PART_BUFS], parts_stored(b, u - PART_BUFS))
                    nc.scalar.activation(parts[:, u % PART_BUFS, 0, :], bank[:, 4 + u % 4, :], ACT.Identity,
                                         bias=unit_bias[u][:, m:m + 1], scale=1.0).then_inc(pj_hi, 1)

                def middle(u):
                    act.wait_ge(pj_rest, b * UNITS + u + 1)
                    nc.scalar.copy(parts[:, u % PART_BUFS, 1, :], rest[:, u % 3, :]).then_inc(pj_mid, 1)

                high(0)
                for u in range(1, UNITS):
                    high(u)
                    middle(u - 1)
                middle(UNITS - 1)

                def probabilities(kind, h, p):
                    n = b * H + h
                    for u in range(4):
                        act.wait_ge(sT_mm, FIRST + n * 8 + 4 * kind + u + 1)
                        c = 2 + 2 * (u % 2)
                        if kind == SELF:
                            nc.scalar.activation(pT_self[p][:, u, P * u:S], bank[:, c, 0:S - P * u], ACT.Exp,
                                                 scale=SCALE).then_inc(pT_ready, 1)
                        else:
                            nc.scalar.activation(pT_cross[:, 2 * u:2 * u + 2, :], bank[:, c:c + 2, :], ACT.Exp,
                                                 scale=SCALE).then_inc(pT_ready, 1)

                def groups(h):
                    act.wait_ge(pv_mm, PV_FIRST + (b * H + h) * 4 + 4)
                    nc.scalar.copy(o_groups, bank[:, 6, :]).then_inc(pv_evac, 1)

                def head(h, p):
                    probabilities(SELF, h, p)
                    groups(h - 1)
                    probabilities(CROSS, h, p)

                probabilities(SELF, 0, 0)
                probabilities(CROSS, 0, 0)
                with act.Fori(0, H // 2 - 1) as i:
                    for n in range(2):
                        head(i * 2 + (n + 1), (n + 1) % 2)
                head(H - 1, 1)
                groups(H - 1)

                features(2, featA, bank[:, 2:4, :].rearrange("p a n -> p (a n)"))
                if not last:
                    first_qk(b + 1, 0, 1)
                    first_v(b + 1)
                features(3, featB, bank[:, 2:4, :].rearrange("p a n -> p (a n)"))
                act.wait_ge(route_mm, b + 1)
                nc.scalar.activation(gate_in.rearrange("p (t n) -> p t n", t=NT), bank[:, 0, 0:N].rearrange("p (t n) -> p t n", t=NT),
                                     ACT.Exp, scale=temp[:, 2:3]).then_inc(gate_exp, 1)
                act.wait_ge(gelu_in, b + 1)
                nc.scalar.activation(hT, bank[0:HID, 1, :], ACT.Gelu, bias=cb1_col[:, 0:1], scale=1.0).then_inc(gelu_done, 1)
                if not last:
                    first_qk(b + 1, 2, 3)
                    first_queries(b + 1)
                act.wait_ge(comp_b, b + 1)
                nc.scalar.activation(comp, comp_in, ACT.Tanh).then_inc(comp_done, 1)
                act.wait_ge(expert_tr, b + 1)
                nc.scalar.copy(expertT, bank[0:TILES, 3, :]).then_inc(expert_evac, 1)

            first_qk(0, 0, 1, 2, 3)
            first_v(0)
            first_queries(0)
            with act.Fori(0, B - 1) as b:
                batch(b)
            batch(B - 1, last=True)

        @block.vector
        def _(dve):
            for primed in (conv_done, ln_done, p1_ready, o1_evac, max_rows, y_done):
                dve.sem_inc(primed, FIRST)
            dve.wait_ge(w_in, W_IN)
            dve.wait_ge(const_ready, 1)
            q0, q1 = sig_work[:, 0, :], sig_work[:, 1, :]
            setup = [0]

            def link(ins):
                ins.then_inc(sig_ready, 1)
                setup[0] += 1
                dve.wait_ge(sig_ready, setup[0])

            link(nc.vector.tensor_scalar(q0, sig_raw[:], 0.3, None, ALU.is_gt))
            link(nc.vector.tensor_scalar(q1, sig_raw[:], -0.3, None, ALU.is_lt))
            link(nc.vector.tensor_tensor(q0, q0, q1, ALU.subtract))
            link(nc.vector.tensor_tensor(q0, q0, sig_raw[:], ALU.subtract))
            link(nc.vector.tensor_tensor(q0, q0, sig_raw[:], ALU.add))
            SIG_NAT = setup[0]
            dve.wait_ge(sig_tr, 1)
            link(nc.vector.tensor_copy(sigT[:, :, CL:ST], bank[:, 0, 0:KD * TILES].rearrange("p (k n) -> p k n", k=KD)))
            members = sigT[:, :, CL:ST].rearrange("p k (c i) -> p k c i", i=TPC)
            link(nc.vector.tensor_tensor(sig_sum[:, 0], members[:, :, :, 0], members[:, :, :, 1], ALU.add))
            for i in range(2, TPC):
                link(nc.vector.tensor_tensor(sig_sum[:, 0], sig_sum[:, 0], members[:, :, :, i], ALU.add))
            link(nc.vector.tensor_scalar(sig_sum[:, 1], sig_sum[:, 0], 0.0, None, ALU.is_lt))
            link(nc.vector.tensor_scalar(sig_sum[:, 0], sig_sum[:, 0], 0.0, None, ALU.is_gt))
            link(nc.vector.tensor_tensor(sigT[:, :, 0:CL], sig_sum[:, 0], sig_sum[:, 1], ALU.subtract))
            link(nc.vector.tensor_tensor(knot_step[:], knot_row[:, 1:NK], knot_row[:, 0:NK - 1], ALU.subtract))
            link(nc.vector.tensor_scalar(temp[:, 1:2], temp[:, 0:1], 1e-6, None, ALU.add))
            link(nc.vector.reciprocal(temp[:, 2:3], temp[:, 1:2]))
            link(nc.vector.tensor_scalar(temp[:, 2:3], temp[:, 2:3], -1.0, None, ALU.mult))
            assert setup[0] == SIG_STEPS and SIG_NAT == 5

            def convolve(b):
                dve.wait_ge(x_in, b * 16 * KD + 16 * KD)
                for k in range(KD):
                    nc.vector.tensor_scalar(xs[:, k, :], xT_pad[:, k, 0:S], conv_sb[:, k, 0:1], None, ALU.mult).then_inc(conv_step, 1)
                    dve.wait_ge(conv_step, (b * KD + k) * 2 + 1)
                    nc.vector.scalar_tensor_tensor(xs[:, k, :], xT_pad[:, k, 1:S + 1], conv_sb[:, k, 1:2],
                                                   xs[:, k, :], ALU.mult, ALU.add).then_inc(conv_step, 1)
                    dve.wait_ge(conv_step, (b * KD + k) * 2 + 2)
                    nc.vector.scalar_tensor_tensor(xs[:, k, :], xT_pad[:, k, 2:S + 2], conv_sb[:, k, 2:3],
                                                   xs[:, k, :], ALU.mult, ALU.add).then_inc(conv_done, 1)

            def add_position(b):
                dve.wait_ge(pe_mm, b * KD + KD)
                for k in range(KD):
                    nc.vector.tensor_tensor(xs[:, k, :], bank[:, 4 + k, :], xs[:, k, :], ALU.add).then_inc(xs_ready, 1)

            def batch(b, last=False):
                st = Steps(dve_step, DVE_STEPS, b)

                def do(ins):
                    st.mark(ins)
                    st.wait(dve)

                def layernorm(k, src, dst):
                    for t in range(NT):
                        st.mark(nc.vector.bn_stats(stats[:, t, :], src[:, t, :]))
                    st.wait(dve)
                    own_wait(nc.vector)
                    for t in range(NT):
                        nc.vector.bn_aggr(mv[:, t, :], stats[:, t, :]).then_inc(ln_stats, 1)
                    dve.wait_ge(ln_stats, b * 16 + 4 * k + 4)
                    dve.wait_ge(ln_rstd, b * 4 + k + 1)
                    for t in range(NT):
                        ins = nc.vector.tensor_scalar(dst[:, t, :], src[:, t, :], mv[:, t, 0:1], ln_r[:, t:t + 1],
                                                      ALU.subtract, ALU.mult)
                        if t < NT - 1:
                            st.mark(ins)
                        else:
                            ins.then_inc(ln_done, 1)
                    st.wait(dve)
                    dve.wait_ge(ln_done, FIRST + b * 4 + k + 1)

                def scores1(h, p):
                    u = b * H + h
                    if not (isinstance(h, int) and h == 0):
                        dve.wait_ge(p1_tr, FIRST + u - 1)
                    for t in range(NT):
                        dve.wait_ge(s1_mm, u * 4 + t + 1)
                        nc.vector.tensor_scalar(s1[:, p, t, :], bank[:, t, :], 1.0, None, ALU.mult, ALU.max,
                                                accum_out=max1[:, p, t:t + 1]).then_inc(s1_evac, 1)
                    dve.wait_ge(s1_evac, u * 4 + 4)
                    nc.vector.tensor_scalar(neg1[:, p, :], max1[:, p, :], -SCALE, None, ALU.mult).then_inc(s1_neg, 1)

                def norm1(h, p):
                    u = b * H + h
                    dve.wait_ge(e1_ready, u * 4 + 4)
                    nc.vector.tensor_copy(denb1[:, p, :], den1[:, p, :]).then_inc(n1_step, 1)
                    dve.wait_ge(n1_step, u * 2 + 1)
                    nc.vector.reciprocal(rden1[:, p, :], denb1[:, p, :]).then_inc(n1_step, 1)
                    dve.wait_ge(n1_step, u * 2 + 2)
                    for t in range(NT):
                        nc.vector.tensor_scalar(s1[:, p, t, :], e1[:, p, t, :], rden1[:, p, t:t + 1], None,
                                                ALU.mult).then_inc(p1_ready, 1)

                def out1(h):
                    u = b * H + h
                    dve.wait_ge(o1_mm, FIRST + u + 1)
                    nc.vector.tensor_copy(o_nat[:, :, bass.ts(h, HD)],
                                          bank[:, 6, 0:NT * HD].rearrange("p (t j) -> p t j", t=NT)).then_inc(o1_evac, 1)

                scores1(0, 0)
                scores1(1, 1)
                norm1(0, 0)
                with dve.Fori(0, H // 2 - 1) as i:
                    for p in range(2):
                        h = i * 2 + (2 + p)
                        scores1(h, p)
                        norm1(h - 1, 1 - p)
                        out1(h - 2)
                norm1(H - 1, 1)
                out1(H - 2)
                out1(H - 1)

                dve.wait_ge(xn_in, b * 16 + 16)
                for i in range(2):
                    dve.wait_ge(out_mm, b * 4 + i + 1)
                    nc.vector.tensor_tensor(x_res[:, 2 * i:2 * i + 2, :].rearrange("p a n -> p (a n)"),
                                            x_res[:, 2 * i:2 * i + 2, :].rearrange("p a n -> p (a n)"), bank[:, i, :],
                                            ALU.add).then_inc(res_done, 1)
                dve.wait_ge(res_done, b * 2 + 2)
                layernorm(0, x_res, x_res)

                def remainder(u):
                    m = unit_list[u][1]
                    dve.wait_ge(pj_hi, b * UNITS + u + 1)
                    if u >= 3:
                        dve.wait_ge(pj_parts, b * UNITS + u - 2)
                    nc.vector.scalar_tensor_tensor(rest[:, u % 3, :], bank[:, 4 + u % 4, :], unit_bias[u][:, m:m + 1],
                                                   parts[:, u % PART_BUFS, 0, :], ALU.add, ALU.subtract).then_inc(pj_rest, 1)

                def lowest(u):
                    dve.wait_ge(pj_mid, b * UNITS + u + 1)
                    nc.vector.tensor_tensor(parts[:, u % PART_BUFS, 2, :], rest[:, u % 3, :], parts[:, u % PART_BUFS, 1, :],
                                            ALU.subtract).then_inc(pj_parts, 1)

                def values(i):
                    dve.wait_ge(vj_mm, FIRST + b * (NT + NC) + i + 1)
                    row = bv_row if i < NT else bcv_row
                    nc.vector.tensor_tensor(v_all[:, i, :, 0:HD], bank[:, i % 4, 0:D].rearrange("p (h j) -> p h j", h=H),
                                            row[:].rearrange("p (h j) -> p h j", h=H), ALU.add).then_inc(vj_evac, 1)

                remainder(0)
                for u in range(1, UNITS):
                    remainder(u)
                    lowest(u - 1)
                lowest(UNITS - 1)
                for i in range(NT + NC):
                    values(i)

                def maxima(kind, h, j):
                    n = b * H + h
                    idx = n * 12 + 4 * kind + j
                    if j == 0:
                        dve.wait_ge(parts_ready[kind], FIRST + n)
                    dve.wait_ge(s_mm, FIRST + idx + 1)
                    if kind == SELF:
                        nc.vector.tensor_reduce(max_self[:, j:j + 1], bank[:, j % 2, 0:P * (j + 1)], AX.X, ALU.max).then_inc(max_done, 1)
                    else:
                        nc.vector.tensor_reduce(max_half[:, j // 2, j % 2:j % 2 + 1], bank[:, j % 2, :], AX.X, ALU.max).then_inc(max_done, 1)
                        if j == 7:
                            dve.wait_ge(max_done, idx + 1)
                            nc.vector.tensor_tensor(max_cross[:], max_half[:, :, 0], max_half[:, :, 1], ALU.max).then_inc(cross_max, 1)

                def put_rows(kind, h):
                    dve.wait_ge(max_tr[kind], FIRST + b * H + h + 1)
                    stack = q_self if kind == SELF else q_cross
                    nc.vector.tensor_copy(stack[SHIFT:ROWS, h, :], bankb(7)[0:3, S * kind:S * (kind + 1)]).then_inc(max_rows, 1)

                def finish(h):
                    n = b * H + h
                    dve.wait_ge(o_mm, n + 1)
                    o = bank[:, 6, 0:NT * 2 * (HD + 1)].rearrange("p (t k j) -> p t k j", t=NT, k=2)
                    nc.vector.reciprocal(rec[:], o[:, :, :, HD]).then_inc(y_step, 1)
                    dve.wait_ge(y_step, n * 2 + 1)
                    nc.vector.tensor_tensor(y_tmp[:], o[:, :, :, 0:HD], rec[:].unsqueeze(3).broadcast_to([P, NT, 2, HD]),
                                            ALU.mult).then_inc(y_done, 1)
                    dve.wait_ge(y_done, FIRST + n + 1)
                    nc.vector.tensor_tensor(y_sb[:, :, bass.ts(h, HD)], y_tmp[:, :, 0, :], y_tmp[:, :, 1, :],
                                            ALU.add).then_inc(y_step, 1)

                def head(h, first=False, last=False):
                    if not last:
                        for j in range(4):
                            maxima(SELF, h + 1, j)
                    put_rows(CROSS, h)
                    if not last:
                        for j in range(4):
                            maxima(CROSS, h + 1, j)
                        put_rows(SELF, h + 1)
                        maxima(CROSS, h + 1, 4)
                    if not first:
                        finish(h - 1)
                    if not last:
                        for j in range(5, 8):
                            maxima(CROSS, h + 1, j)

                for j in range(4):
                    maxima(SELF, 0, j)
                for j in range(8):
                    maxima(CROSS, 0, j)
                put_rows(SELF, 0)
                dve.wait_ge(out_dma, FIRST + b * 16)
                head(0, first=True)
                with dve.Fori(1, H - 1) as h:
                    head(h)
                head(H - 1, last=True)
                if not last:
                    convolve(b + 1)
                finish(H - 1)

                def over_tiles(row):
                    return row[:].unsqueeze(1).broadcast_to([P, NT, D])

                if not last:
                    add_position(b + 1)
                do(nc.vector.tensor_tensor(x_res[:], x_res[:], over_tiles(bp_row), ALU.add))
                for i in range(2):
                    dve.wait_ge(out_mm, b * 4 + 2 + i + 1)
                    half = x_res[:, 2 * i:2 * i + 2, :].rearrange("p a n -> p (a n)")
                    do(nc.vector.tensor_tensor(half, half, bank[:, i, :], ALU.add))
                layernorm(1, x_res, y_sb)

                dve.wait_ge(gate_exp, b + 1)
                do(nc.vector.tensor_scalar(gate_in, gate_in, 1.0, None, ALU.add))
                do(nc.vector.reciprocal(gate_in, gate_in))
                do(nc.vector.tensor_scalar(gate_in, gate_in, float(NK - 1), None, ALU.mult))
                do(nc.vector.tensor_scalar(low, gate_in, 1.0, None, ALU.is_ge))
                for i in range(2, NK - 1):
                    do(nc.vector.scalar_tensor_tensor(low, gate_in, float(i), low, ALU.is_ge, ALU.add))
                do(nc.vector.tensor_tensor(frac, gate_in, low, ALU.subtract))
                do(nc.vector.tensor_scalar(knot_at, low, 0.0, knot_row[:, 0:1], ALU.is_equal, ALU.mult))
                do(nc.vector.tensor_scalar(step_at, low, 0.0, knot_step[:, 0:1], ALU.is_equal, ALU.mult))
                for i in range(1, NK - 1):
                    do(nc.vector.tensor_scalar(seg, low, float(i), knot_row[:, i:i + 1], ALU.is_equal, ALU.mult))
                    do(nc.vector.tensor_tensor(knot_at, knot_at, seg, ALU.add))
                    do(nc.vector.tensor_scalar(seg, low, float(i), knot_step[:, i:i + 1], ALU.is_equal, ALU.mult))
                    do(nc.vector.tensor_tensor(step_at, step_at, seg, ALU.add))
                do(nc.vector.tensor_tensor(frac, frac, step_at, ALU.mult))
                do(nc.vector.tensor_tensor(gate_in, frac, knot_at, ALU.add))

                def first_max(values, eq, pick):
                    do(nc.vector.tensor_reduce(top, values, AX.X, ALU.max))
                    do(nc.vector.tensor_tensor(eq, values, top.unsqueeze(2).broadcast_to([P, NT, CL]), ALU.is_equal))
                    do(nc.vector.tensor_tensor(eq, eq, first_weight[:].unsqueeze(1).broadcast_to([P, NT, CL]), ALU.mult))
                    do(nc.vector.tensor_reduce(best, eq, AX.X, ALU.max))
                    do(nc.vector.tensor_tensor(pick, eq, best.unsqueeze(2).broadcast_to([P, NT, CL]), ALU.is_equal))

                first_max(gates[:, :, 0:CL], c_eq, c_pick)
                for t in range(NT):
                    st.mark(nc.vector.tensor_tensor(sel_all[:, t, :].rearrange("p (c l) -> p c l", c=CL),
                                                    gates[:, t, CL:ST].rearrange("p (c l) -> p c l", c=CL),
                                                    c_pick[:, t, :].unsqueeze(2).broadcast_to([P, CL, TPC]), ALU.mult))
                st.wait(dve)
                do(nc.vector.tensor_reduce(sel, sel_all.rearrange("p t (c l) -> p t l c", c=CL), AX.X, ALU.add))
                first_max(sel, l_eq, l_pick)
                for t in range(NT):
                    ins = nc.vector.tensor_tensor(expert[:, t, :].rearrange("p (c l) -> p c l", c=CL),
                                                  c_pick[:, t, :].unsqueeze(2).broadcast_to([P, CL, TPC]),
                                                  l_pick[:, t, :].unsqueeze(1).broadcast_to([P, CL, TPC]), ALU.mult)
                    ins.then_inc(expert_ready, 1)

                dve.wait_ge(comp_mm, b + 1)
                nc.vector.tensor_tensor(comp_in, bank[:, 2, 0:2 * NT].rearrange("p (t i) -> p t i", t=NT),
                                        cb2_row[:].unsqueeze(1).broadcast_to([P, NT, 2]), ALU.add).then_inc(comp_b, 1)
                dve.wait_ge(comp_done, b + 1)
                dve.wait_ge(gather_mm, b + 1)

                def column(i):
                    return comp[:, :, i:i + 1].broadcast_to([P, NT, G])

                do(nc.vector.tensor_tensor(hh, bank[:, 4:4 + NT, T_W1:T_W1 + G], column(0), ALU.mult))
                do(nc.vector.tensor_tensor(hh2, bank[:, 4:4 + NT, T_W1 + G:T_B1], column(1), ALU.mult))
                do(nc.vector.tensor_tensor(hh, hh, hh2, ALU.add))
                do(nc.vector.tensor_tensor(hh, bank[:, 4:4 + NT, T_B1:T_W2], hh, ALU.add))
                do(nc.vector.tensor_scalar(hh, hh, 0.0, None, ALU.max))
                do(nc.vector.tensor_tensor(hh, bank[:, 4:4 + NT, T_W2:T_B2], hh, ALU.mult))
                do(nc.vector.tensor_reduce(mag, hh, AX.X, ALU.add))
                do(nc.vector.tensor_tensor(mag, bank[:, 4:4 + NT, T_B2], mag, ALU.add))
                for t in range(NT):
                    st.mark(nc.vector.tensor_scalar(x_dir[:, t, :], bank[:, 4 + t, 0:D], mag[:, t:t + 1], scale_col[:, 0:1],
                                                    ALU.mult, ALU.mult))
                st.wait(dve)
                do(nc.vector.tensor_tensor(x_res[:], y_sb[:], x_dir, ALU.add))
                layernorm(2, x_res, x_res)
                do(nc.vector.tensor_tensor(x_res[:], x_res[:], over_tiles(gamma_row), ALU.mult))
                do(nc.vector.tensor_tensor(x_res[:], x_res[:], over_tiles(beta_row), ALU.add))
                do(nc.vector.tensor_tensor(y_sb[:], y_sb[:], x_res[:], ALU.add))
                layernorm(3, y_sb, y_sb)
                st.end()

            convolve(0)
            add_position(0)
            with dve.Fori(0, B - 1) as b:
                batch(b)
            batch(B - 1, last=True)

        @block.tensor
        def _(pe):
            for primed in (vj_mm, pj_mm, sT_mm, s_mm, max_tr[SELF], max_tr[CROSS], o1_mm, p1_tr):
                pe.sem_inc(primed, FIRST)
            pe.sem_inc(pv_mm, PV_FIRST)
            mm = nc.tensor.matmul
            pe.wait_ge(const_ready, 1)
            pe.wait_ge(w_in, W_IN)
            pe.wait_ge(sig_ready, 5)
            for k in range(KD):
                last = nc.tensor.transpose(bank[:, 0, TILES * k:TILES * (k + 1)], sig_work[:, 0, P * k:P * (k + 1)],
                                           ident[0:TILES, 0:TILES])
            last.then_inc(sig_tr, 1)
            pe.wait_ge(sig_ready, SIG_STEPS)

            def project(dst, lhsT, rhs, tiles=KD):
                for k in range(tiles):
                    last = mm(dst, lhsT(k), rhs(k), start=(k == 0), stop=(k == tiles - 1))
                return last

            def position(b):
                pe.wait_ge(conv_done, FIRST + b * KD + KD)
                for m in range(KD):
                    project(bank[:, 4 + m, :], lambda k: pe_sb[:, k, P * m:P * (m + 1)], lambda k: xs[:, k, :]).then_inc(pe_mm, 1)

            def first_qk(b, *tiles):
                for i in tiles:
                    if i >= 2:
                        pe.wait_ge(qk_evac, b * 2 * KD + i - 1)
                    project(bank[:, 6 + i % 2, :], lambda k: qkv_sb[:, k, P * i:P * (i + 1)], lambda k: xs[:, k, :]).then_inc(qk_mm, 1)

            def first_v(b):
                for i in range(NT):
                    last = project(bank[:, 4 + i // 2, D * (i % 2):D * (i % 2 + 1)], lambda k: xs[:, k, P * i:P * (i + 1)],
                                   lambda k: qkv_sb[:, k, 2 * D:3 * D])
                    if i % 2:
                        last.then_inc(v_mm, 1)

            def batch(b, last_batch=False):
                def scores1(h, static):
                    u = b * H + h
                    for t in range(NT):
                        if not static:
                            pe.wait_ge(s1_evac, u * 4 + (t - 3))
                        mm(bank[:, t, :], q1T[:, bass.ds(h * S + P * t, P)],
                           k1T[:, :, bass.ts(h, RH)], start=True, stop=True).then_inc(s1_mm, 1)

                def transpose1(h, p):
                    u = b * H + h
                    pe.wait_ge(p1_evac, FIRST + u * 2)
                    for t in range(NT):
                        pe.wait_ge(p1_ready, FIRST + u * 4 + t + 1)
                        for j in range(4):
                            last = nc.tensor.transpose(bankb(4, 2)[:, S * j + P * t:S * j + P * (t + 1)],
                                                       s1[:, p, t, P * j:P * (j + 1)], identb[:])
                    last.then_inc(p1_tr, 1)

                def pv1(h):
                    u = b * H + h
                    pe.wait_ge(p1_evac, FIRST + u * 2 + 2)
                    pe.wait_ge(o1_evac, FIRST + u)
                    for t in range(NT):
                        for j in range(4):
                            last = mm(bank[:, 6, HD * t:HD * (t + 1)], p1T[:, j, P * t:P * (t + 1)], v1[:, h, j, :],
                                      start=(j == 0), stop=(j == 3))
                    last.then_inc(o1_mm, 1)

                pe.wait_ge(qk1_in, FIRST + (b + 1) * 16 * 2 * KD)
                pe.wait_ge(q1_ready, b * 4 + 4)
                pe.wait_ge(v_evac, b * 2 + 2)
                pe.wait_ge(v1_ready, b * 16 + 16)
                scores1(0, True)
                scores1(1, False)
                transpose1(0, 0)
                with pe.Fori(0, H // 2 - 1) as i:
                    for p in range(2):
                        h = i * 2 + (2 + p)
                        scores1(h, False)
                        pv1(h - 2)
                        transpose1(h - 1, 1 - p)
                pv1(H - 2)
                transpose1(H - 1, 1)
                pv1(H - 1)

                pe.wait_ge(o1_evac, FIRST + (b + 1) * H)
                for t in range(NT):
                    for k in range(KD):
                        last = nc.tensor.transpose(bankb(7)[:, S * k + P * t:S * k + P * (t + 1)],
                                                   o_nat[:, t, P * k:P * (k + 1)], identb[:])
                last.then_inc(feat_tr, 1)
                pe.wait_ge(feat_evac, b * 4 + 1)

                def token_out(w):
                    for t in range(NT):
                        last = project(bank[:, t // 2, D * (t % 2):D * (t % 2 + 1)], lambda k: featA[:, k, P * t:P * (t + 1)],
                                       lambda k: w[:, k, :])
                        if t % 2:
                            last.then_inc(out_mm, 1)

                def to_features(src, first_bank):
                    for t in range(NT):
                        for k in range(KD):
                            last = nc.tensor.transpose(bank[:, first_bank + k, P * t:P * (t + 1)], src[:, t, P * k:P * (k + 1)], ident[:])
                    last.then_inc(feat_tr, 1)

                token_out(out_sb)
                pe.wait_ge(ln_done, FIRST + b * 4 + 1)
                to_features(x_res, 2)
                pe.wait_ge(feat_evac, b * 4 + 2)

                pe.wait_ge(ctx_in, b * 16 + 16)

                def unit(u):
                    stack, m, c0 = unit_list[u]
                    if u >= 4:
                        pe.wait_ge(pj_rest, b * UNITS + u - 3)
                    dst = bank[:, 4 + u % 4, :]
                    if u < 6:
                        w = (wq_sb, wk_sb, wcq_sb)[u // 2]
                        project(dst, lambda k: w[:, k, P * m:P * (m + 1)], lambda k: featB[:, k, :]).then_inc(pj_mm, 1)
                    else:
                        mm(dst, wck_sb[:, P * m:P * (m + 1)], ctx_sb[:, c0:c0 + S], start=True, stop=True).then_inc(pj_mm, 1)

                def values(i):
                    if i >= 4:
                        pe.wait_ge(vj_evac, b * (NT + NC) + i - 3)
                    if i < NT:
                        project(bank[:, i % 4, 0:D], lambda k: featB[:, k, P * i:P * (i + 1)], lambda k: wv_sb[:, k, :]).then_inc(vj_mm, 1)
                    else:
                        mm(bank[:, i % 4, 0:D], ctx_sb[:, P * (i - NT):P * (i - NT + 1)], wcv_sb[:], start=True, stop=True).then_inc(vj_mm, 1)

                for u in range(UNITS):
                    unit(u)
                for i in range(NT + NC):
                    values(i)

                def scores(kind, h, j, static=False):
                    idx = (b * H + h) * 12 + 4 * kind + j
                    if not (static and idx_free(kind, j)):
                        pe.wait_ge(max_done, idx - 1)
                    if kind == SELF:
                        n = P * (j + 1)
                        mm(bank[:, j % 2, 0:n], q_self[0:SHIFT, h, P * j:n], k_self[0:SHIFT, h, 0:n], start=True, stop=False)
                        mm(bank[:, j % 2, P * j:n], identb[:], mask_q[:], start=False, stop=True).then_inc(s_mm, 1)
                    else:
                        mm(bank[:, j % 2, :], q_cross[0:SHIFT, h, P * (j // 2):P * (j // 2 + 1)],
                           k_cross[0:SHIFT, h, S * (j % 2):S * (j % 2 + 1)], start=True, stop=True).then_inc(s_mm, 1)

                def idx_free(kind, j):
                    return kind == SELF and j < 2

                def max_transpose(kind, h):
                    n = b * H + h
                    pe.wait_ge(parts_ready[kind], FIRST + n + 1)
                    pe.wait_ge(max_rows, FIRST + n * 2 + kind)
                    for t in range(NT):
                        last = nc.tensor.transpose(bankb(7)[0:3, S * kind + P * t:S * kind + P * (t + 1)],
                                                   max_parts[:, kind, t, :], identb[:])
                    last.then_inc(max_tr[kind], 1)

                def scoresT(kind, h, u, static=False):
                    n = b * H + h
                    if u == 0:
                        pe.wait_ge(max_rows, FIRST + n * 2 + kind + 1)
                    if not (static and kind == SELF and u < 2):
                        pe.wait_ge(pT_ready, n * 8 + 4 * kind + u - 1)
                    c = 2 + 2 * (u % 2)
                    if kind == SELF:
                        w = S - P * u
                        mm(bank[:, c, 0:w], k_self[0:ROWS, h, P * u:P * (u + 1)], q_self[0:ROWS, h, P * u:S], start=True, stop=False)
                        mm(bank[:, c, 0:P], identb[:], mask_k[:], start=False, stop=True).then_inc(sT_mm, 1)
                    else:
                        for i in range(2):
                            t = 2 * u + i
                            last = mm(bank[:, c + i, :], k_cross[0:ROWS, h, P * t:P * (t + 1)], q_cross[0:ROWS, h, :], start=True, stop=True)
                        last.then_inc(sT_mm, 1)

                def pv(h, p, r):
                    n = b * H + h
                    pe.wait_ge(pT_ready, n * 8 + 4 + 2 + r)
                    if r == 0:
                        pe.wait_ge(v_ready, n + 1)
                        pe.wait_ge(v_pad, b * 2 + 2)
                        pe.wait_ge(y_done, FIRST + n)
                    for kind, t, g in ROUNDS[r]:
                        tiles = GROUP_TILES[g]
                        q0 = P * t if kind == SELF else 0
                        pT = pT_self[p] if kind == SELF else pT_cross
                        ins = mm(bank[GROUP * g:GROUP * (g + 1), 6, q0:S], v_head[p][:, t if kind == SELF else NT + t, :],
                                 pT[:, t, q0:S], start=((kind, t) == tiles[0]), stop=((kind, t) == tiles[-1]),
                                 tile_position=(0, GROUP * g))
                        if (kind, t) == tiles[-1]:
                            ins.then_inc(pv_mm, 1)

                def sum_groups(h):
                    pe.wait_ge(pv_evac, b * H + h + 1)
                    w = 2 * (HD + 1)
                    for t in range(NT):
                        last = mm(bank[:, 6, w * t:w * (t + 1)], o_groups[:, P * t:P * (t + 1)], gather_groups[:],
                                  start=True, stop=True)
                    last.then_inc(o_mm, 1)

                def head(h, p, first=False, last=False):
                    def next_scores(kind, *tiles):
                        if not last:
                            for j in tiles:
                                scores(kind, h + 1, j)

                    def outputs(r):
                        if not first:
                            pv(h - 1, 1 - p, r)

                    scoresT(SELF, h, 0, first)
                    next_scores(SELF, 0)
                    scoresT(SELF, h, 1, first)
                    next_scores(SELF, 1)
                    outputs(0)
                    next_scores(SELF, 2)
                    scoresT(SELF, h, 2, first)
                    next_scores(SELF, 3)
                    outputs(1)
                    max_transpose(CROSS, h)
                    scoresT(SELF, h, 3, first)
                    next_scores(CROSS, 0)
                    outputs(2)
                    next_scores(CROSS, 1)
                    scoresT(CROSS, h, 0)
                    next_scores(CROSS, 2, 3)
                    if not last:
                        max_transpose(SELF, h + 1)
                    scoresT(CROSS, h, 1)
                    next_scores(CROSS, 4)
                    if not first:
                        sum_groups(h - 1)
                    next_scores(CROSS, 5)
                    scoresT(CROSS, h, 2)
                    next_scores(CROSS, 6)
                    scoresT(CROSS, h, 3)
                    next_scores(CROSS, 7)

                pe.wait_ge(stack_in[SELF], (b + 1) * STACK_IN[SELF])
                pe.wait_ge(vj_evac, (b + 1) * (NT + NC))
                for j in range(4):
                    scores(SELF, 0, j, static=True)
                pe.wait_ge(stack_in[CROSS], (b + 1) * STACK_IN[CROSS])
                for j in range(8):
                    scores(CROSS, 0, j)
                max_transpose(SELF, 0)
                head(0, 0, first=True)
                with pe.Fori(0, H // 2 - 1) as i:
                    for p in range(2):
                        head(i * 2 + (p + 1), (p + 1) % 2)
                head(H - 1, 1, last=True)
                for r in range(len(ROUNDS)):
                    pv(H - 1, 1, r)
                sum_groups(H - 1)

                if not last_batch:
                    position(b + 1)
                pe.wait_ge(y_step, (b + 1) * H * 2)
                to_features(y_sb, 2)
                pe.wait_ge(feat_evac, b * 4 + 3)
                token_out(wp_sb)
                if not last_batch:
                    pe.wait_ge(xs_ready, (b + 1) * KD + KD)
                    first_qk(b + 1, 0, 1)
                    first_v(b + 1)
                pe.wait_ge(ln_done, FIRST + b * 4 + 2)
                to_features(y_sb, 2)
                pe.wait_ge(feat_evac, b * 4 + 4)
                for t in range(NT):
                    last = project(bank[:, 0, ST * t:ST * (t + 1)], lambda k: featB[:, k, P * t:P * (t + 1)], lambda k: sigT[:, k, :])
                last.then_inc(route_mm, 1)
                project(bank[0:HID, 1, :], lambda k: cw1_sb[:, k, :], lambda k: featB[:, k, :]).then_inc(gelu_in, 1)
                if not last_batch:
                    first_qk(b + 1, 2, 3)
                pe.wait_ge(gelu_done, b + 1)
                for t in range(NT):
                    last = mm(bank[:, 2, 2 * t:2 * t + 2], hT[:, P * t:P * (t + 1)], cw2_sb[:], start=True, stop=True)
                last.then_inc(comp_mm, 1)
                pe.wait_ge(expert_ready, b * NT + NT)
                own_wait(nc.tensor)
                for t in range(NT):
                    last = nc.tensor.transpose(bank[0:TILES, 3, P * t:P * (t + 1)], expert[:, t, :], ident[:])
                last.then_inc(expert_tr, 1)
                pe.wait_ge(expert_evac, b + 1)
                if not last_batch:
                    pe.wait_ge(qk_evac, (b + 2) * 2 * KD)
                    pe.wait_ge(v_evac, (b + 2) * 2)
                for t in range(NT):
                    last = mm(bank[:, 4 + t, 0:TABLE], expertT[:, P * t:P * (t + 1)], table[:], start=True, stop=True)
                last.then_inc(gather_mm, 1)
                pe.wait_ge(comp_b, b + 1)

            position(0)
            pe.wait_ge(xs_ready, KD)
            first_qk(0, 0, 1)
            first_v(0)
            first_qk(0, 2, 3)
            with pe.Fori(0, B - 1) as b:
                batch(b)
            batch(B - 1, last_batch=True)


_OUT = ((8, 512, 256), "float32")


def kernel(**inputs):
    import numpy as np
    import concourse.bacc as bacc
    from concourse.bass_utils import run_bass_kernel_spmd

    nc = bacc.Bacc("TRN2", target_bir_lowering=False, num_devices=1)
    given = {k: np.asarray(v) for k, v in inputs.items()}

    def attn(n):
        return given["L0_attn_" + n]

    arrays = {"x": given["x"], "xT": given["x"].transpose(0, 2, 1), "ctxT": given["ctx_512"].transpose(0, 2, 1),
              "conv_w": attn("conv_w")[:, 0, :, 1], "peT": attn("pe_w").T, "qkvT": attn("qkv_w").T, "outT": attn("out_w").T}
    for n in ("Wk", "bk", "Wq", "bq", "Wv", "bv", "Wck", "bck", "Wcq", "bcq", "Wcv", "bcv", "Wp", "bp"):
        arrays[n] = given["L0_xattn_" + n]
    for n in ("signatures_raw", "knot_values", "temperature", "compress_w1", "compress_b1", "compress_w2", "compress_b2",
              "spline_w1", "spline_b1", "spline_w2", "spline_b2", "directions", "norm_gamma", "norm_beta", "output_scale"):
        arrays[n] = given["L0_ffn_" + n]
    for n in ("Wq", "Wk", "Wcq", "Wck"):
        w = arrays[n]
        arrays[n] = w.reshape(w.shape[0], 2, 8, 16).transpose(0, 1, 3, 2).reshape(w.shape)
    for n in ("bq", "bk", "bcq", "bck"):
        arrays[n] = arrays[n].reshape(2, 8, 16).transpose(2, 1, 0).reshape(128, 2)
    arrays = {n: np.ascontiguousarray(a) for n, a in arrays.items()}
    args = [nc.dram_tensor(n, a.shape, mybir.dt.from_np(a.dtype), kind="ExternalInput").ap() for n, a in arrays.items()]
    out = nc.dram_tensor("out", _OUT[0], mybir.dt.float32, kind="ExternalOutput").ap()
    decoder_layer(nc, *args, out)
    return run_bass_kernel_spmd(nc, [arrays], core_ids=[0]).results[0]["out"]
```

```python
import concourse.bass as bass
from concourse import mybir
from contextlib import ExitStack


class Steps:

    def __init__(self, sem, per_batch, b):
        self.sem, self.per_batch, self.b, self.n = sem, per_batch, b, 0

    def mark(self, instruction):
        instruction.then_inc(self.sem, 1)
        self.n += 1

    def wait(self, engine):
        engine.wait_ge(self.sem, self.b * self.per_batch + self.n)

    def end(self):
        assert self.n == self.per_batch, (self.n, self.per_batch)


def decoder_layer(nc, x, xT, ctxT, conv_w, peT, qkvT, outT, Wk, bk, Wq, bq, Wv, bv, Wck, bck, Wcq, bcq,
                  Wcv, bcv, Wp, bp, signatures, knots, temperature, cw1, cb1, cw2, cb2, sw1, sb1, sw2, sb2,
                  directions, gamma, beta, output_scale, out):
    fp32 = mybir.dt.float32
    bf16 = mybir.dt.bfloat16
    ALU = mybir.AluOpType
    ACT = mybir.ActivationFunctionType
    AX = mybir.AxisListType

    B, S, D = x.shape
    CC, SC = ctxT.shape[1:]
    H, HD, P = 16, 16, 128
    KD = D // P
    NT = S // P
    NC = SC // P
    RH = S // H
    TILES = signatures.shape[0]
    CL, TPC = 8, TILES // 8
    NK = knots.shape[0]
    HID = cw1.shape[1]
    G = sw1.shape[2]
    SCALE = 1.0 / HD ** 0.5
    SHIFT = 6 * HD
    ROWS = SHIFT + 3
    RUNS = [(0, 3, 0, 0), (3, 2, 1, 0), (5, 1, 2, 0)]
    MASKED = -1.0e30
    EPS = 1e-5
    ST = CL + TILES
    T_W1 = D
    T_B1 = T_W1 + 2 * G
    T_W2 = T_B1 + G
    T_B2 = T_W2 + G
    TABLE = T_B2 + 1
    SELF, CROSS, LATER = 0, 1, 2
    GROUP = 32
    ROUNDS = [[(CROSS, 0, 0), (CROSS, 1, 1), (CROSS, 2, 2), (SELF, 0, 3)],
              [(CROSS, 3, 0), (CROSS, 4, 1), (CROSS, 5, 2), (SELF, 1, 3)],
              [(CROSS, 6, 0), (CROSS, 7, 1), (SELF, 2, 3), (SELF, 3, 3)]]
    SCORES = [(CROSS, 0), (CROSS, 1), (CROSS, 2), (CROSS, 3), (CROSS, 4), (SELF, 3), (SELF, 2), (SELF, 1), (SELF, 0),
              (CROSS, 5), (CROSS, 6), (CROSS, 7)]
    FIRST_SCORES = [(SELF, j) for j in range(4)] + [(CROSS, j) for j in range(8)]
    SELF_MAXIMA = 9
    GROUP_TILES = [[(k, t) for r in ROUNDS for k, t, g in r if g == group] for group in range(4)]
    UNITS, CTX_UNITS = 6, 4
    PART_BUFS = 4
    FIRST = 1
    PV_FIRST = 5
    DVE_STEPS = 89
    SIG_STEPS = 20
    POOL_STEPS = 4

    ctx = ExitStack()
    with ctx:
        def sb(name, shape, dt=fp32):
            return ctx.enter_context(nc.sbuf_tensor(name, shape, dt))

        def sem(name):
            return ctx.enter_context(nc.semaphore(name))

        conv_sb = sb("conv_sb", [P, KD, 3])
        pe_sb = sb("pe_sb", [P, KD, D])
        qkv_sb = sb("qkv_sb", [P, KD, 3 * D])
        out_sb = sb("out_sb", [P, KD, D])
        wq_sb, wk_sb, wv_sb = sb("wq_sb", [P, KD, D]), sb("wk_sb", [P, KD, D]), sb("wv_sb", [P, KD, D])
        wcq_sb, wck_sb, wcv_sb = sb("wcq_sb", [P, KD, D]), sb("wck_sb", [P, D]), sb("wcv_sb", [P, D])
        wp_sb = sb("wp_sb", [P, KD, D])
        bq_col, bk_col = sb("bq_col", [P, KD]), sb("bk_col", [P, KD])
        bcq_col, bck_col = sb("bcq_col", [P, KD]), sb("bck_col", [P, KD])
        bv_row, bcv_row, bp_row = sb("bv_row", [P, D]), sb("bcv_row", [P, D]), sb("bp_row", [P, D])
        gamma_row, beta_row = sb("gamma_row", [P, D]), sb("beta_row", [P, D])
        sig_raw = sb("sig_raw", [TILES, D])
        sig_work = sb("sig_work", [TILES, 2, D])
        sigT = sb("sigT", [P, KD, ST])
        sig_sum = sb("sig_sum", [P, 2, KD, CL])
        knot_row, knot_step = sb("knot_row", [P, NK]), sb("knot_step", [P, NK - 1])
        temp = sb("temp", [P, 3])
        scale_col = sb("scale_col", [P, 1])
        cw1_sb, cb1_col = sb("cw1_sb", [P, KD, HID]), sb("cb1_col", [HID, 1])
        cw2_sb, cb2_row = sb("cw2_sb", [HID, 2]), sb("cb2_row", [P, 2])
        table = sb("table", [TILES, TABLE])
        ident, identb = sb("ident", [P, P]), sb("identb", [P, P], bf16)
        mask_f = sb("mask_f", [P, P])
        mask_q, mask_k = sb("mask_q", [P, P], bf16), sb("mask_k", [P, P], bf16)
        first_weight = sb("first_weight", [P, CL])
        minus_half = sb("minus_half", [P, NT])
        segments = sb("segments", [P, NK - 1])

        xT_pad = sb("xT_pad", [P, KD, S + 2])
        ctx_sb = sb("ctx_sb", [P, SC])
        featA = sb("featA", [P, KD, S])
        featB = sb("featB", [P, KD, S])
        x_res = sb("x_res", [P, NT, D])
        y_sb = sb("y_sb", [P, NT, D])
        shared = sb("shared", [P, 2048])
        qk_nat = shared[:, 0:1024].bitcast(bf16).rearrange("p (i n) -> p i n", i=2 * KD)
        v_nat = shared[:, 1024:1536].bitcast(bf16).rearrange("p (t d) -> p t d", t=NT)
        o_nat = shared[:, 1536:2048].bitcast(bf16).rearrange("p (t d) -> p t d", t=NT)
        v1 = sb("v1", [P, H, 4, HD], bf16)
        k1T = sb("k1T", [P, 16, S], bf16)
        q_self, k_self = sb("q_self", [P, H, S], bf16), sb("k_self", [P, H, S], bf16)
        q_cross, k_cross = sb("q_cross", [P, H, S], bf16), sb("k_cross", [P, H, SC], bf16)
        q1T = q_cross[:, :, :].rearrange("p h n -> p (h n)")
        q1_chunks = k_self[0:HD, :, :]
        xs = q_self[:, 0:4 * KD // 2, :].rearrange("p h n -> p (h n)").bitcast(fp32).rearrange("p (k n) -> p k n", k=KD)
        v_all = sb("v_all", [P, NT + NC, H, HD + 1])
        v_head = [featB[:, p, 0:(NT + NC) * GROUP].rearrange("p (t j) -> p t j", j=GROUP) for p in range(2)]
        o_groups = featA[:, 0, :]
        gather_groups = sb("gather_groups", [P, 2 * (HD + 1)])
        work = sb("work", [P, 6144])
        y_tmp = sb("y_tmp", [P, NT, 2, HD])
        max1 = sb("max1", [P, 2, NT], bf16)
        neg1, den1, rden1 = sb("neg1", [P, 2, NT]), sb("den1", [P, 2, NT]), sb("rden1", [P, 2, NT])
        denb1 = sb("denb1", [P, 2, NT], bf16)
        max_self, max_half = sb("max_self", [P, NT]), sb("max_half", [P, 2, NT, 2])
        max_cross = sb("max_cross", [P, NT])
        max_rest = sb("max_rest", [P, 2, 2, NT])
        max_parts = sb("max_parts", [P, 2, NT, 3], bf16)
        rec = sb("rec", [P, NT, 2])
        stats, mv = sb("stats", [P, NT, 6]), sb("mv", [P, NT, 2])
        ln_var, ln_r = sb("ln_var", [P, NT]), sb("ln_r", [P, NT])

        s1 = work[:, 0:2048].bitcast(bf16).rearrange("p (a t n) -> p a t n", a=2, t=NT)
        e1 = work[:, 2048:4096].bitcast(bf16).rearrange("p (a t n) -> p a t n", a=2, t=NT)
        p1T = work[:, 4096:5120].bitcast(bf16).rearrange("p (t n) -> p t n", t=4)
        parts = work[:, 0:3072].bitcast(bf16).rearrange("p (a s n) -> p a s n", a=PART_BUFS, s=3)
        rest = work[:, 3072:4608].rearrange("p (a n) -> p a n", a=3)
        ctx_keys = [feat[:, k, :] for feat in (featA, featB) for k in range(KD)]
        ctx_parts = shared[:, 0:1536].bitcast(bf16).rearrange("p (a s n) -> p a s n", a=2, s=3)
        pT_self = [w.rearrange("p (t n) -> p t n", t=NT) for w in (work[:, 0:2048], shared[:])]
        pT_cross = work[:, 2048:6144].rearrange("p (t n) -> p t n", t=NC)
        N = NT * CL

        def piece(i, n, t=NT):
            return work[:, 512 * i:512 * i + n].rearrange("p (t n) -> p t n", t=t)

        gates, low, frac, knot_at, step_at, scores_sel = (work[:, N * i:N * (i + 1)] for i in range(6))
        at_least, segment, seg_knot, seg_step = (work[:, 512 * i:512 * i + N * n].rearrange("p (g i) -> p g i", i=n)
                                                 for i, n in ((1, NK - 2), (2, NK - 1), (3, NK - 1), (4, NK - 1)))
        c_eq, c_pick, l_eq, l_pick = (piece(6, 4 * NT * CL)[:, :, CL * i:CL * (i + 1)] for i in range(4))
        sel_all = piece(7, NT * TILES)
        expert = piece(8, NT * TILES)
        top, best = work[:, 4608:4608 + NT], work[:, 4612:4612 + NT]
        comp_in = work[:, 4640:4640 + 2 * NT].rearrange("p (t i) -> p t i", t=NT)
        comp = work[:, 4656:4656 + 2 * NT].rearrange("p (t i) -> p t i", t=NT)
        y_beta = work[:, 0:NT * D].rearrange("p (t d) -> p t d", t=NT)
        hh, hh2 = work[:, 5120:5184].rearrange("p (t g) -> p t g", t=NT), work[:, 5184:5248].rearrange("p (t g) -> p t g", t=NT)
        mag = work[:, 5248:5248 + NT]
        hT = work[0:HID, 5632:6144]
        expertT = work[0:TILES, 3072:3584]

        bank = ctx.enter_context(nc.psum_tensor("bank", [P, 8, 512], fp32))

        def bankb(i, n=1):
            return bank[:, i:i + n, :].rearrange("p a n -> p (a n)").bitcast(bf16)

        waited = {e: sem(f"waited_{n}") for n, e in (("pe", nc.tensor), ("dve", nc.vector), ("pool", nc.gpsimd), ("sp", nc.sync))}
        w_first, w_in, zeros_ready, pad_ready, minus_ones = (sem(n) for n in ("w_first", "w_in", "zeros_ready", "pad_ready", "minus_ones"))
        x_in, xn_in, ctx_in = sem("x_in"), sem("xn_in"), sem("ctx_in")
        const_ready, init_step = sem("const_ready"), sem("init_step")
        sig_tr, sig_ready = sem("sig_tr"), sem("sig_ready")
        dve_step, pool_step = sem("dve_step"), sem("pool_step")
        conv_step, conv_done, pe_mm, xs_ready = (sem(n) for n in ("conv_step", "conv_done", "pe_mm", "xs_ready"))
        qk_mm, qk_evac, v_mm, v_evac = sem("qk_mm"), sem("qk_evac"), sem("v_mm"), sem("v_evac")
        qk1_in, v1_ready = sem("qk1_in"), sem("v1_ready")
        s1_mm, s1_evac, s1_neg, e1_ready = sem("s1_mm"), sem("s1_evac"), sem("s1_neg"), sem("e1_ready")
        n1_step, p1_ready, p1_tr, p1_evac = sem("n1_step"), sem("p1_ready"), sem("p1_tr"), sem("p1_evac")
        o1_mm, o1_evac = sem("o1_mm"), sem("o1_evac")
        feat_tr, feat_evac = sem("feat_tr"), sem("feat_evac")
        out_mm, res_done = sem("out_mm"), sem("res_done")
        ln_stats, ln_rstd, ln_done = sem("ln_stats"), sem("ln_rstd"), sem("ln_done")
        pj_mm, pj_hi, pj_rest, pj_mid, pj_parts = (sem(n) for n in ("pj_mm", "pj_hi", "pj_rest", "pj_mid", "pj_parts"))
        stack_in = [sem("stack_in_self"), sem("stack_in_cross"), sem("stack_in_later")]
        qk1_out = [sem(f"qk1_out{i}") for i in range(4)]
        parts_out = [sem(f"parts_out{i}") for i in range(PART_BUFS)]
        ctx_out = [sem("ctx_out0"), sem("ctx_out1")]
        ck_mm, ck_evac, ck_step, ck_parts = (sem(n) for n in ("ck_mm", "ck_evac", "ck_step", "ck_parts"))
        vj_mm, vj_evac = sem("vj_mm"), sem("vj_evac")
        s_mm, max_done = sem("s_mm"), sem("max_done")
        cross_max, q1_ready = sem("cross_max"), sem("q1_ready")
        parts_ready = [sem("parts_self"), sem("parts_cross")]
        max_tr = [sem("max_tr_self"), sem("max_tr_cross")]
        max_rows, m_step = sem("max_rows"), sem("m_step")
        sT_mm, pT_ready = sem("sT_mm"), sem("pT_ready")
        pv_mm, pv_evac, v_ready, v_pad, o_mm = (sem(n) for n in ("pv_mm", "pv_evac", "v_ready", "v_pad", "o_mm"))
        y_step, y_done = sem("y_step"), sem("y_done")
        route_mm, gelu_in, gelu_done, comp_mm = sem("route_mm"), sem("gelu_in"), sem("gelu_done"), sem("comp_mm")
        comp_b, comp_done, gate_exp, sel_ready = sem("comp_b"), sem("comp_done"), sem("gate_exp"), sem("sel_ready")
        expert_ready, expert_tr, expert_evac, gather_mm = (sem(n) for n in ("expert_ready", "expert_tr", "expert_evac", "gather_mm"))
        out_dma = sem("out_dma")

        def own_wait(engine):
            engine.sem_inc(waited[engine], 1)

        def wide(w):
            return w.rearrange("(k p) n -> p k n", p=P)

        first_weights = [(conv_sb[:], wide(conv_w)), (pe_sb[:], wide(peT)), (qkv_sb[:], wide(qkvT))]
        weights = [(wck_sb[:], Wck), (bck_col[:], bck), (out_sb[:], wide(outT)), (wq_sb[:], wide(Wq)), (wk_sb[:], wide(Wk)), (wv_sb[:], wide(Wv)),
                   (wcq_sb[:], wide(Wcq)), (wcv_sb[:], Wcv), (wp_sb[:], wide(Wp)),
                   (bq_col[:], bq), (bk_col[:], bk), (bcq_col[:], bcq),
                   (bv_row[:], bv.partition_broadcast(P)), (bcv_row[:], bcv.partition_broadcast(P)),
                   (bp_row[:], bp.partition_broadcast(P)), (gamma_row[:], gamma.partition_broadcast(P)),
                   (beta_row[:], beta.partition_broadcast(P)), (sig_raw[:], signatures),
                   (knot_row[:], knots.partition_broadcast(P)), (temp[:, 0:1], temperature.partition_broadcast(P)),
                   (scale_col[:], output_scale.partition_broadcast(P)), (cw1_sb[:], wide(cw1)),
                   (cb1_col[:], cb1.rearrange("(p o) -> p o", o=1)), (cw2_sb[:], cw2),
                   (cb2_row[:], cb2.partition_broadcast(P)), (table[:, 0:D], directions),
                   (table[:, T_W1:T_B1], sw1.rearrange("t i g -> t (i g)")), (table[:, T_B1:T_W2], sb1),
                   (table[:, T_W2:T_B2], sw2.rearrange("t g o -> t (g o)")), (table[:, T_B2:TABLE], sb2)]
        W_FIRST, W_IN = 16 * len(first_weights), 16 * len(weights)

        unit_list = [(q_self, 0, 0), (k_self, 0, 0), (q_cross, 0, 0), (q_self, 1, 0), (k_self, 1, 0), (q_cross, 1, 0)]
        unit_bias = [bq_col, bk_col, bcq_col] * 2
        ctx_units = [(k_cross, 0, 0), (k_cross, 1, 0), (k_cross, 0, S), (k_cross, 1, S)]
        unit_in = [stack_in[SELF], stack_in[SELF], stack_in[CROSS]] + [stack_in[LATER]] * 3
        unit_copies = {SELF: 2, CROSS: 1 + CTX_UNITS, LATER: 3}

        def unit_bank(u):
            return 4 + (u + 2) % 4

        def stacks_loaded(b, group):
            return (b + 1) * 16 * len(RUNS) * unit_copies[group]

        PAIRS, CTX_PAIRS = (NT + NC) // 2, NC // 2
        HT = H // KD

        def parts_stored(b, u):
            per_batch = len(range(u % PART_BUFS, UNITS, PART_BUFS))
            return (b * per_batch + u // PART_BUFS + 1) * 16

        qk_dram = nc.dram_tensor("qk_dram", (2 * KD, P, S), bf16, kind="Internal").ap()
        parts_dram = nc.dram_tensor("parts_dram", (UNITS, 3, P, S), bf16, kind="Internal").ap()
        ctx_dram = nc.dram_tensor("ctx_dram", (CTX_UNITS, 3, P, S), bf16, kind="Internal").ap()

        block = ctx.enter_context(nc.Block())

        @block.sync
        def _(sp):
            for primed in (qk1_in, out_dma):
                sp.sem_inc(primed, FIRST)

            def load_x(b):
                sp.wait_ge(conv_done, FIRST + b * KD)
                for k in range(KD):
                    sp.dma_start(xT_pad[:, k, 1:S + 1], xT[b, k * P:(k + 1) * P, :]).then_inc(x_in, 16)

            def chunks(b):
                sp.wait_ge(sT_mm, FIRST + b * H * 8)
                own_wait(nc.sync)
                sp.wait_ge(s_mm, FIRST + b * H * 12)
                own_wait(nc.sync)
                for i in range(2 * KD):
                    sp.wait_ge(qk_evac, b * 2 * KD + i + 1)
                    sp.dma_start(qk_dram[i], qk_nat[:, i, :]).then_inc(qk1_out[i], 16)
                for i in range(2 * KD):
                    sp.wait_ge(qk1_out[i], b * 16 + 16)
                    dst = (q1_chunks if i < KD else k1T)[0:HD, 8 * (i % KD):8 * (i % KD) + 8, :]
                    sp.dma_start(dst, qk_dram[i].rearrange("(c j) s -> j c s", j=HD)).then_inc(qk1_in, 16)

            def load_context(b):
                sp.wait_ge(vj_mm, FIRST + b * PAIRS)
                own_wait(nc.sync)
                sp.wait_ge(ck_mm, FIRST + b * CTX_UNITS)
                own_wait(nc.sync)
                sp.dma_start(ctx_sb[:], ctxT[b]).then_inc(ctx_in, 16)

            def copies(unit, parts_of, signal):
                stack, m, c0 = unit
                for group, n, q_part, k_part in RUNS:
                    dst = stack[HD * group:HD * (group + n), HT * m:HT * (m + 1), c0:c0 + S]
                    if stack is q_self or stack is q_cross:
                        dst = dst.rearrange("p h n -> p (h n)")
                        src = parts_of[q_part].rearrange("(j h) n -> j (h n)", h=HT).unsqueeze(0).broadcast_to([n, HD, HT * S])
                    else:
                        src = parts_of[k_part:k_part + n].rearrange("s (j h) n -> (s j) h n", h=HT)
                    sp.dma_start(dst, src).then_inc(signal, 16)

            def batch(b, last=False):
                sp.wait_ge(ln_done, FIRST + b * 4)
                sp.dma_start(x_res[:], x[b].rearrange("(t p) d -> p t d", p=P)).then_inc(xn_in, 16)
                if not last:
                    load_x(b + 1)
                for u in range(CTX_UNITS):
                    sp.wait_ge(ck_parts, b * CTX_UNITS + u + 1)
                    sp.dma_start(ctx_dram[u].rearrange("s p n -> p s n"), ctx_parts[:, u % 2]).then_inc(ctx_out[u % 2], 16)
                    sp.wait_ge(ctx_out[u % 2], (b * 2 + u // 2 + 1) * 16)
                    copies(ctx_units[u], ctx_dram[u], stack_in[CROSS])
                sp.wait_ge(s1_mm, (b + 1) * H * NT)
                own_wait(nc.sync)

                def store(u):
                    sp.wait_ge(pj_parts, b * UNITS + u + 1)
                    sp.dma_start(parts_dram[u].rearrange("s p n -> p s n"), parts[:, u % PART_BUFS]).then_inc(parts_out[u % PART_BUFS], 16)

                def stack_up(u):
                    sp.wait_ge(parts_out[u % PART_BUFS], parts_stored(b, u))
                    copies(unit_list[u], parts_dram[u], unit_in[u])

                for u in range(UNITS):
                    store(u)
                    if 0 < u < UNITS - 2:
                        stack_up(u - 1)
                for u in range(UNITS - 3, UNITS):
                    stack_up(u)
                if not last:
                    load_context(b + 1)
                    chunks(b + 1)
                sp.wait_ge(ln_done, FIRST + 4 * (b + 1))
                sp.dma_start(out[b].rearrange("(t p) d -> p t d", p=P), y_sb[:]).then_inc(out_dma, 16)

            load_x(0)
            for dst, src in first_weights:
                sp.dma_start(dst, src).then_inc(w_first, 16)
            load_context(0)
            for dst, src in weights:
                sp.dma_start(dst, src).then_inc(w_in, 16)
            sp.wait_ge(zeros_ready, 2)
            chunks(0)
            with sp.Fori(0, B - 1) as b:
                batch(b)
            batch(B - 1, last=True)
            sp.wait_ge(out_dma, FIRST + 16 * B)

        @block.gpsimd
        def _(pool):
            for primed in (parts_ready[SELF], parts_ready[CROSS]):
                pool.sem_inc(primed, FIRST)
            n = [0]

            def init(ins):
                ins.then_inc(init_step, 1)
                n[0] += 1
                pool.wait_ge(init_step, n[0])

            nc.gpsimd.memset(xT_pad[:, :, 0:1], 0.0).then_inc(pad_ready, 1)
            nc.gpsimd.memset(xT_pad[:, :, S + 1:], 0.0).then_inc(pad_ready, 1)
            pool.wait_ge(pad_ready, 2)
            init(nc.gpsimd.memset(ident[:], 0.0))
            init(nc.gpsimd.affine_select(out=ident[:], in_=ident[:], compare_op=ALU.not_equal, fill=1.0, base=0,
                                         pattern=[[-1, P]], channel_multiplier=1))
            init(nc.gpsimd.tensor_copy(identb[:], ident[:]))
            init(nc.gpsimd.memset(mask_f[:], 0.0))
            init(nc.gpsimd.affine_select(out=mask_f[:], in_=mask_f[:], compare_op=ALU.is_ge, fill=MASKED, base=0,
                                         pattern=[[-1, P]], channel_multiplier=1))
            init(nc.gpsimd.tensor_copy(mask_q[:], mask_f[:]))
            init(nc.gpsimd.memset(mask_f[:], 0.0))
            init(nc.gpsimd.affine_select(out=mask_f[:], in_=mask_f[:], compare_op=ALU.is_ge, fill=MASKED, base=0,
                                         pattern=[[1, P]], channel_multiplier=-1))
            init(nc.gpsimd.tensor_copy(mask_k[:], mask_f[:]))
            init(nc.gpsimd.iota(first_weight[:], pattern=[[-1, CL]], base=CL, channel_multiplier=0,
                                allow_small_or_imprecise_dtypes=True))
            init(nc.gpsimd.memset(minus_half[:], -0.5))
            init(nc.gpsimd.iota(segments[:], pattern=[[1, NK - 1]], base=0, channel_multiplier=0,
                                allow_small_or_imprecise_dtypes=True))
            init(nc.gpsimd.memset(v_all[:, :, :, HD:HD + 1], 1.0))
            init(nc.gpsimd.tensor_copy(gather_groups[:, 0:HD + 1], ident[:, 3 * GROUP:3 * GROUP + HD + 1]))
            init(nc.gpsimd.tensor_copy(gather_groups[:, HD + 1:], ident[:, 0:HD + 1]))
            for g in (1, 2):
                init(nc.gpsimd.tensor_tensor(gather_groups[:, HD + 1:], gather_groups[:, HD + 1:],
                                             ident[:, g * GROUP:g * GROUP + HD + 1], ALU.add))
            nc.gpsimd.memset(work[:, 0:1], 0.0).then_inc(const_ready, 1)
            pool.wait_ge(const_ready, 1)
            nc.gpsimd.memset(k_self[SHIFT:P, :, :], -1.0).then_inc(minus_ones, 1)
            nc.gpsimd.memset(k_cross[SHIFT:P, :, :], -1.0).then_inc(minus_ones, 1)
            pool.wait_ge(minus_ones, 2)

            def first_values(b):
                pool.wait_ge(v_evac, b * 2 + 2)
                own_wait(nc.gpsimd)
                for q in range(4):
                    for a in range(4):
                        src = v_nat[RH * q:RH * (q + 1), :, :].rearrange("p g (t a j) -> p g t a j", t=4, a=4)[:, :, :, a, :]
                        dst = v1[RH * a:RH * (a + 1), :, :, :].rearrange("p (g q) t j -> p g q t j", q=4)[:, :, q]
                        nc.gpsimd.tensor_copy(dst, src).then_inc(v1_ready, 1)
                pool.wait_ge(v1_ready, (b + 1) * 16)
                own_wait(nc.gpsimd)

            def batch(b, last=False):
                def rstd(k):
                    pool.wait_ge(ln_stats, b * 16 + 4 * k + 4)
                    own_wait(nc.gpsimd)
                    nc.gpsimd.tensor_scalar(ln_var[:], mv[:, :, 1], EPS, None, ALU.add).then_inc(pool_step, 1)
                    pool.wait_ge(pool_step, b * POOL_STEPS + k + 1)
                    nc.gpsimd.tensor_tensor(ln_r[:], ln_var[:], minus_half[:], ALU.pow).then_inc(ln_rstd, 1)

                context_parts(b)
                rstd(0)
                pool.wait_ge(pj_mm, FIRST + (b + 1) * UNITS)
                own_wait(nc.gpsimd)
                pool.wait_ge(vj_mm, FIRST + (b + 1) * PAIRS)
                own_wait(nc.gpsimd)
                for p in range(2):
                    nc.gpsimd.memset(v_head[p][:, :, HD + 1:], 0.0).then_inc(v_pad, 1)
                pool.wait_ge(vj_evac, (b + 1) * PAIRS)
                own_wait(nc.gpsimd)
                with pool.Fori(0, H // 2) as i:
                    for p in range(2):
                        h = i * 2 + p
                        u = b * H + h
                        for kind in (SELF, CROSS):
                            if kind == SELF:
                                pool.wait_ge(max_done, u * 12 + SELF_MAXIMA)
                            else:
                                pool.wait_ge(cross_max, FIRST + u + 1)
                            pool.wait_ge(max_tr[kind], FIRST + u)
                            own_wait(nc.gpsimd)
                            step = u * 6 + 3 * kind
                            top_row = max_self if kind == SELF else max_cross
                            part = max_parts[:, kind, :, :]
                            nc.gpsimd.tensor_copy(part[:, :, 0], top_row[:]).then_inc(m_step, 1)
                            pool.wait_ge(m_step, step + 1)
                            nc.gpsimd.tensor_tensor(max_rest[:, kind, 0, :], top_row[:], part[:, :, 0], ALU.subtract).then_inc(m_step, 1)
                            pool.wait_ge(m_step, step + 2)
                            own_wait(nc.gpsimd)
                            nc.gpsimd.tensor_copy(part[:, :, 1], max_rest[:, kind, 0, :]).then_inc(m_step, 1)
                            pool.wait_ge(m_step, step + 3)
                            nc.gpsimd.tensor_tensor(part[:, :, 2], max_rest[:, kind, 0, :], part[:, :, 1], ALU.subtract).then_inc(parts_ready[kind], 1)
                        pool.wait_ge(pv_mm, PV_FIRST + 4 * u - 4)
                        own_wait(nc.gpsimd)
                        nc.gpsimd.tensor_copy(v_head[p][:, :, 0:HD + 1], v_all[:, :, h, :]).then_inc(v_ready, 1)
                rstd(1)
                if not last:
                    pool.wait_ge(ln_rstd, b * 4 + 2)
                    own_wait(nc.gpsimd)
                    first_values(b + 1)
                rstd(2)
                rstd(3)

            def context_parts(b):
                pool.wait_ge(qk1_in, FIRST + (b + 1) * 16 * 2 * KD)
                own_wait(nc.gpsimd)
                for u in range(CTX_UNITS):
                    keys, part, step = ctx_keys[u], ctx_parts[:, u % 2], (b * CTX_UNITS + u) * 3
                    pool.wait_ge(ck_evac, b * CTX_UNITS + u + 1)
                    own_wait(nc.gpsimd)
                    if u >= 2:
                        pool.wait_ge(ctx_out[u % 2], (b * 2 + 1) * 16)
                        own_wait(nc.gpsimd)
                    nc.gpsimd.tensor_copy(part[:, 0, :], keys).then_inc(ck_step, 1)
                    pool.wait_ge(ck_step, step + 1)
                    nc.gpsimd.tensor_tensor(keys, keys, part[:, 0, :], ALU.subtract).then_inc(ck_step, 1)
                    pool.wait_ge(ck_step, step + 2)
                    own_wait(nc.gpsimd)
                    nc.gpsimd.tensor_copy(part[:, 1, :], keys).then_inc(ck_step, 1)
                    pool.wait_ge(ck_step, step + 3)
                    nc.gpsimd.tensor_tensor(part[:, 2, :], keys, part[:, 1, :], ALU.subtract).then_inc(ck_parts, 1)
                pool.wait_ge(ck_parts, (b + 1) * CTX_UNITS)
                own_wait(nc.gpsimd)

            first_values(0)
            with pool.Fori(0, B - 1) as b:
                batch(b)
            batch(B - 1, last=True)

        @block.scalar
        def _(act):
            for primed in (p1_evac,):
                act.sem_inc(primed, FIRST)
            def first_qk(b, *tiles):
                for i in tiles:
                    act.wait_ge(qk_mm, b * 2 * KD + i + 1)
                    if i == 0:
                        act.wait_ge(qk1_in, FIRST + b * 16 * 2 * KD)
                    nc.scalar.copy(qk_nat[:, i, :], bank[:, 6 + i % 2, :]).then_inc(qk_evac, 1)

            def first_v(b):
                for i in range(2):
                    act.wait_ge(v_mm, b * 2 + i + 1)
                    nc.scalar.copy(v_nat[:, 2 * i:2 * i + 2, :].rearrange("p a n -> p (a n)"), bank[:, 4 + i, :]).then_inc(v_evac, 1)

            def context_keys(b):
                for u in range(CTX_UNITS):
                    act.wait_ge(ck_mm, FIRST + b * CTX_UNITS + u + 1)
                    nc.scalar.activation(ctx_keys[u], bank[:, u, :], ACT.Identity, bias=bck_col[:, u % KD:u % KD + 1],
                                         scale=1.0).then_inc(ck_evac, 1)

            def first_queries(b):
                act.wait_ge(qk1_in, FIRST + (b + 1) * 16 * 2 * KD)
                for q in range(4):
                    nc.scalar.copy(q1T[0:HD, S * 4 * q:S * 4 * (q + 1)].rearrange("p (s c) -> p c s", c=16),
                                   q1_chunks[:, :, P * q:P * (q + 1)]).then_inc(q1_ready, 1)

            def batch(b, last=False):
                def exp1(h, p):
                    u = b * H + h
                    act.wait_ge(s1_neg, u + 1)
                    if not (isinstance(h, int) and h == 0):
                        act.wait_ge(p1_tr, FIRST + u - 1)
                    for t in range(NT):
                        nc.scalar.activation(e1[:, p, t, :], s1[:, p, t, :], ACT.Exp, bias=neg1[:, p, t:t + 1],
                                             scale=SCALE, accum_out=den1[:, p, t:t + 1]).then_inc(e1_ready, 1)

                def evac1(h, odd):
                    u = b * H + h
                    act.wait_ge(p1_tr, FIRST + u + 1)
                    act.wait_ge(o1_mm, FIRST + u)
                    for i in range(1 if odd else 2):
                        nc.scalar.copy(p1T[:, 2 * i:2 * i + 2, :].rearrange("p a n -> p (a n)"), bankb(4 + i)).then_inc(p1_evac, 1)

                exp1(0, 0)
                with act.Fori(0, H // 2 - 1) as i:
                    for n in range(2):
                        h = i * 2 + (n + 1)
                        exp1(h, (n + 1) % 2)
                        evac1(h - 1, odd=n == 1)
                exp1(H - 1, 1)
                evac1(H - 2, odd=False)
                evac1(H - 1, odd=True)

                def features(k, dst, src):
                    act.wait_ge(feat_tr, b * 4 + k + 1)
                    nc.scalar.copy(dst[:].rearrange("p k n -> p (k n)"), src).then_inc(feat_evac, 1)


                def high(u):
                    m = unit_list[u][1]
                    act.wait_ge(pj_mm, FIRST + b * UNITS + u + 1)
                    if u == 0:
                        act.wait_ge(pv_mm, PV_FIRST + b * 4 * H)
                    elif u >= PART_BUFS:
                        act.wait_ge(parts_out[u % PART_BUFS], parts_stored(b, u - PART_BUFS))
                    nc.scalar.activation(parts[:, u % PART_BUFS, 0, :], bank[:, unit_bank(u), :], ACT.Identity,
                                         bias=unit_bias[u][:, m:m + 1], scale=1.0).then_inc(pj_hi, 1)

                def middle(u):
                    act.wait_ge(pj_rest, b * UNITS + u + 1)
                    nc.scalar.copy(parts[:, u % PART_BUFS, 1, :], rest[:, u % 3, :]).then_inc(pj_mid, 1)

                act.wait_ge(ck_parts, (b + 1) * CTX_UNITS)
                features(0, featA, bankb(7))
                features(1, featB, bank[:, 0:2, :].rearrange("p a n -> p (a n)"))
                high(0)
                for u in range(1, UNITS):
                    high(u)
                    middle(u - 1)
                middle(UNITS - 1)

                def probabilities(kind, h, p):
                    n = b * H + h
                    for u in range(4):
                        act.wait_ge(sT_mm, FIRST + n * 8 + 4 * kind + u + 1)
                        c = 2 + 2 * (u % 2)
                        if kind == SELF:
                            nc.scalar.activation(pT_self[p][:, u, P * u:S], bank[:, c, 0:S - P * u], ACT.Exp,
                                                 scale=SCALE).then_inc(pT_ready, 1)
                        else:
                            nc.scalar.activation(pT_cross[:, 2 * u:2 * u + 2, :], bank[:, c:c + 2, :], ACT.Exp,
                                                 scale=SCALE).then_inc(pT_ready, 1)

                def groups(h):
                    act.wait_ge(pv_mm, PV_FIRST + (b * H + h) * 4 + 4)
                    nc.scalar.copy(o_groups, bank[:, 6, :]).then_inc(pv_evac, 1)

                def head(h, p):
                    probabilities(SELF, h, p)
                    groups(h - 1)
                    probabilities(CROSS, h, p)

                for u in range(UNITS - PART_BUFS, UNITS):
                    act.wait_ge(parts_out[u % PART_BUFS], parts_stored(b, u))
                probabilities(SELF, 0, 0)
                probabilities(CROSS, 0, 0)
                with act.Fori(0, H // 2 - 1) as i:
                    for n in range(2):
                        head(i * 2 + (n + 1), (n + 1) % 2)
                head(H - 1, 1)
                groups(H - 1)

                features(2, featA, bank[:, 2:4, :].rearrange("p a n -> p (a n)"))
                features(3, featB, bank[:, 2:4, :].rearrange("p a n -> p (a n)"))
                act.wait_ge(route_mm, b + 1)
                nc.scalar.activation(gates.rearrange("p (t n) -> p t n", t=NT), bank[:, 0, 0:NT * ST].rearrange("p (t n) -> p t n", t=NT)[:, :, 0:CL],
                                     ACT.Exp, scale=temp[:, 2:3]).then_inc(gate_exp, 1)
                if not last:
                    first_v(b + 1)
                act.wait_ge(sel_ready, b + 1)
                nc.scalar.activation(gates, scores_sel, ACT.Exp, scale=temp[:, 2:3]).then_inc(gate_exp, 1)
                if not last:
                    first_qk(b + 1, 0, 1, 2, 3)
                act.wait_ge(expert_tr, b + 1)
                nc.scalar.copy(expertT, bank[0:TILES, 3, :]).then_inc(expert_evac, 1)
                act.wait_ge(gelu_in, b + 1)
                nc.scalar.activation(hT, bank[0:HID, 1, :], ACT.Gelu, bias=cb1_col[:, 0:1], scale=1.0).then_inc(gelu_done, 1)
                act.wait_ge(comp_b, b + 1)
                nc.scalar.activation(comp, comp_in, ACT.Tanh).then_inc(comp_done, 1)
                if not last:
                    first_queries(b + 1)
                    context_keys(b + 1)

            first_qk(0, 0, 1, 2, 3)
            first_v(0)
            first_queries(0)
            act.wait_ge(w_in, W_IN)
            act.wait_ge(const_ready, 1)
            context_keys(0)
            with act.Fori(0, B - 1) as b:
                batch(b)
            batch(B - 1, last=True)

        @block.vector
        def _(dve):
            for primed in (cross_max, conv_done, ln_done, p1_ready, o1_evac, max_rows, y_done):
                dve.sem_inc(primed, FIRST)
            nc.vector.memset(q1T, 0.0).then_inc(zeros_ready, 1)
            nc.vector.memset(k1T[:], 0.0).then_inc(zeros_ready, 1)

            def convolve(b):
                dve.wait_ge(x_in, b * 16 * KD + 16 * KD)
                for k in range(KD):
                    nc.vector.tensor_scalar(xs[:, k, :], xT_pad[:, k, 0:S], conv_sb[:, k, 0:1], None, ALU.mult).then_inc(conv_step, 1)
                    dve.wait_ge(conv_step, (b * KD + k) * 2 + 1)
                    nc.vector.scalar_tensor_tensor(xs[:, k, :], xT_pad[:, k, 1:S + 1], conv_sb[:, k, 1:2],
                                                   xs[:, k, :], ALU.mult, ALU.add).then_inc(conv_step, 1)
                    dve.wait_ge(conv_step, (b * KD + k) * 2 + 2)
                    nc.vector.scalar_tensor_tensor(xs[:, k, :], xT_pad[:, k, 2:S + 2], conv_sb[:, k, 2:3],
                                                   xs[:, k, :], ALU.mult, ALU.add).then_inc(conv_done, 1)

            def add_position(b):
                dve.wait_ge(pe_mm, b * KD + KD)
                for k in range(KD):
                    nc.vector.tensor_tensor(xs[:, k, :], bank[:, 4 + k, :], xs[:, k, :], ALU.add).then_inc(xs_ready, 1)

            def scores1(b, h, p):
                u = b * H + h
                for t in range(NT):
                    dve.wait_ge(s1_mm, u * 4 + t + 1)
                    nc.vector.tensor_scalar(s1[:, p, t, :], bank[:, t, :], 1.0, None, ALU.mult, ALU.max,
                                            accum_out=max1[:, p, t:t + 1]).then_inc(s1_evac, 1)
                dve.wait_ge(s1_evac, u * 4 + 4)
                nc.vector.tensor_scalar(neg1[:, p, :], max1[:, p, :], -SCALE, None, ALU.mult).then_inc(s1_neg, 1)

            def batch(b, last=False):
                st = Steps(dve_step, DVE_STEPS, b)

                def do(ins):
                    st.mark(ins)
                    st.wait(dve)

                def layernorm(k, src, dst, meanwhile=None, apply=None):
                    for t in range(NT):
                        st.mark(nc.vector.bn_stats(stats[:, t, :], src[:, t, :]))
                    st.wait(dve)
                    own_wait(nc.vector)
                    for t in range(NT):
                        nc.vector.bn_aggr(mv[:, t, :], stats[:, t, :]).then_inc(ln_stats, 1)
                    dve.wait_ge(ln_stats, b * 16 + 4 * k + 4)
                    if meanwhile:
                        meanwhile()
                    dve.wait_ge(ln_rstd, b * 4 + k + 1)
                    for t in range(NT):
                        ins = apply(t) if apply else nc.vector.tensor_scalar(
                            dst[:, t, :], src[:, t, :], mv[:, t, 0:1], ln_r[:, t:t + 1], ALU.subtract, ALU.mult)
                        if t < NT - 1:
                            st.mark(ins)
                        else:
                            ins.then_inc(ln_done, 1)
                    st.wait(dve)
                    dve.wait_ge(ln_done, FIRST + b * 4 + k + 1)

                def norm1(h, p):
                    u = b * H + h
                    dve.wait_ge(e1_ready, u * 4 + 4)
                    nc.vector.tensor_copy(denb1[:, p, :], den1[:, p, :]).then_inc(n1_step, 1)
                    dve.wait_ge(n1_step, u * 2 + 1)
                    nc.vector.reciprocal(rden1[:, p, :], denb1[:, p, :]).then_inc(n1_step, 1)
                    dve.wait_ge(n1_step, u * 2 + 2)
                    for t in range(NT):
                        nc.vector.tensor_scalar(e1[:, p, t, :], e1[:, p, t, :], rden1[:, p, t:t + 1], None,
                                                ALU.mult).then_inc(p1_ready, 1)

                def out1(h):
                    u = b * H + h
                    dve.wait_ge(o1_mm, FIRST + u + 1)
                    nc.vector.tensor_copy(o_nat[:, :, bass.ts(h, HD)],
                                          bank[:, 6, 0:NT * HD].rearrange("p (t j) -> p t j", t=NT)).then_inc(o1_evac, 1)

                def half_evac1(h):
                    u = b * H + h
                    dve.wait_ge(p1_tr, FIRST + u + 1)
                    dve.wait_ge(o1_mm, FIRST + u)
                    nc.vector.tensor_copy(p1T[:, 2:4, :].rearrange("p a n -> p (a n)"), bankb(5)).then_inc(p1_evac, 1)

                scores1(b, 1, 1)
                norm1(0, 0)
                with dve.Fori(0, H // 2 - 1) as i:
                    for p in range(2):
                        h = i * 2 + (2 + p)
                        scores1(b, h, p)
                        if p == 1:
                            half_evac1(h - 2)
                        norm1(h - 1, 1 - p)
                        out1(h - 2)
                norm1(H - 1, 1)
                out1(H - 2)
                half_evac1(H - 1)
                out1(H - 1)

                def remainder(u):
                    m = unit_list[u][1]
                    dve.wait_ge(pj_hi, b * UNITS + u + 1)
                    if u >= 3:
                        dve.wait_ge(pj_parts, b * UNITS + u - 2)
                    nc.vector.scalar_tensor_tensor(rest[:, u % 3, :], bank[:, unit_bank(u), :], unit_bias[u][:, m:m + 1],
                                                   parts[:, u % PART_BUFS, 0, :], ALU.add, ALU.subtract).then_inc(pj_rest, 1)

                def lowest(u):
                    dve.wait_ge(pj_mid, b * UNITS + u + 1)
                    nc.vector.tensor_tensor(parts[:, u % PART_BUFS, 2, :], rest[:, u % 3, :], parts[:, u % PART_BUFS, 1, :],
                                            ALU.subtract).then_inc(pj_parts, 1)

                def values(i):
                    dve.wait_ge(vj_mm, FIRST + b * PAIRS + i + 1)
                    row, t = (bcv_row, NT + 2 * i) if i < CTX_PAIRS else (bv_row, 2 * (i - CTX_PAIRS))
                    nc.vector.tensor_tensor(v_all[:, t:t + 2, :, 0:HD], bank[:, 2 + i % 4, :].rearrange("p (t h j) -> p t h j", t=2, h=H),
                                            row[:].rearrange("p (h j) -> p h j", h=H).unsqueeze(1).broadcast_to([P, 2, H, HD]),
                                            ALU.add).then_inc(vj_evac, 1)

                dve.wait_ge(xn_in, b * 16 + 16)
                for i in range(2):
                    dve.wait_ge(out_mm, b * 4 + i + 1)
                    nc.vector.tensor_tensor(x_res[:, 2 * i:2 * i + 2, :].rearrange("p a n -> p (a n)"),
                                            x_res[:, 2 * i:2 * i + 2, :].rearrange("p a n -> p (a n)"), bank[:, i, :],
                                            ALU.add).then_inc(res_done, 1)
                dve.wait_ge(res_done, b * 2 + 2)

                def first_pair():
                    values(0)

                layernorm(0, x_res, x_res, first_pair)
                for i in range(1, CTX_PAIRS):
                    values(i)
                remainder(0)
                for u in range(1, UNITS):
                    remainder(u)
                    lowest(u - 1)
                lowest(UNITS - 1)
                for i in range(CTX_PAIRS, PAIRS):
                    values(i)

                def over_tiles(row):
                    return row[:].unsqueeze(1).broadcast_to([P, NT, D])

                def maxima(h, p, i, order=SCORES):
                    kind, j = order[i]
                    n = b * H + h
                    if kind == SELF and j == (3 if order is SCORES else 0):
                        dve.wait_ge(parts_ready[SELF], FIRST + n)
                    if kind == CROSS and j == 0 and order is SCORES:
                        dve.wait_ge(cross_max, FIRST + n - 1)
                    dve.wait_ge(s_mm, FIRST + n * 12 + i + 1)
                    if kind == SELF:
                        nc.vector.tensor_reduce(max_self[:, j:j + 1], bank[:, i % 2, 0:P * (j + 1)], AX.X, ALU.max).then_inc(max_done, 1)
                    else:
                        nc.vector.tensor_reduce(max_half[:, p, j // 2, j % 2:j % 2 + 1], bank[:, i % 2, :], AX.X, ALU.max).then_inc(max_done, 1)

                def cross_top(h, p):
                    n = b * H + h
                    dve.wait_ge(max_done, n * 12 + 12)
                    dve.wait_ge(parts_ready[CROSS], FIRST + n)
                    nc.vector.tensor_tensor(max_cross[:], max_half[:, p, :, 0], max_half[:, p, :, 1], ALU.max).then_inc(cross_max, 1)

                def put_rows(kind, h):
                    dve.wait_ge(max_tr[kind], FIRST + b * H + h + 1)
                    stack = q_self if kind == SELF else q_cross
                    nc.vector.tensor_copy(stack[SHIFT:ROWS, h, :], bankb(7)[0:3, S * kind:S * (kind + 1)]).then_inc(max_rows, 1)

                def finish(h):
                    n = b * H + h
                    dve.wait_ge(o_mm, n + 1)
                    o = bank[:, 6, 0:NT * 2 * (HD + 1)].rearrange("p (t k j) -> p t k j", t=NT, k=2)
                    nc.vector.reciprocal(rec[:], o[:, :, :, HD]).then_inc(y_step, 1)
                    dve.wait_ge(y_step, n * 2 + 1)
                    nc.vector.tensor_tensor(y_tmp[:], o[:, :, :, 0:HD], rec[:].unsqueeze(3).broadcast_to([P, NT, 2, HD]),
                                            ALU.mult).then_inc(y_done, 1)
                    dve.wait_ge(y_done, FIRST + n + 1)
                    nc.vector.tensor_tensor(y_sb[:, :, bass.ts(h, HD)], y_tmp[:, :, 0, :], y_tmp[:, :, 1, :],
                                            ALU.add).then_inc(y_step, 1)

                def head(h, p, first=False, last=False):
                    def next_maxima(*places):
                        if not last:
                            for i in places:
                                maxima(h + 1, 1 - p, i)

                    next_maxima(0)
                    cross_top(h, p)
                    next_maxima(1, 2, 3)
                    put_rows(CROSS, h)
                    next_maxima(4, 5, 6, 7, 8, 9, 10)
                    if last:
                        do(nc.vector.tensor_tensor(x_res[:], x_res[:], over_tiles(bp_row), ALU.add))
                    if not first:
                        finish(h - 1)
                    if not last:
                        put_rows(SELF, h + 1)
                    next_maxima(11)

                for i in range(12):
                    maxima(0, 0, i, FIRST_SCORES)
                put_rows(SELF, 0)
                dve.wait_ge(out_dma, FIRST + b * 16)
                head(0, 0, first=True)
                with dve.Fori(0, H // 2 - 1) as i:
                    for p in range(2):
                        head(i * 2 + (p + 1), (p + 1) % 2)
                head(H - 1, 1, last=True)
                if not last:
                    convolve(b + 1)
                finish(H - 1)

                for i in range(2):
                    dve.wait_ge(out_mm, b * 4 + 2 + i + 1)
                    half = x_res[:, 2 * i:2 * i + 2, :].rearrange("p a n -> p (a n)")
                    do(nc.vector.tensor_tensor(half, half, bank[:, i, :], ALU.add))
                layernorm(1, x_res, y_sb, None if last else lambda: add_position(b + 1))

                def calibrate():
                    def over_segments(ap, n):
                        return ap.unsqueeze(2).broadcast_to([P, N, n])

                    def over_gates(ap, n):
                        return ap.unsqueeze(1).broadcast_to([P, N, n])

                    do(nc.vector.tensor_scalar(gates, gates, 1.0, None, ALU.add))
                    do(nc.vector.reciprocal(gates, gates))
                    do(nc.vector.tensor_scalar(gates, gates, float(NK - 1), None, ALU.mult))
                    do(nc.vector.tensor_tensor(at_least, over_segments(gates, NK - 2), over_gates(segments[:, 1:NK - 1], NK - 2), ALU.is_ge))
                    do(nc.vector.tensor_reduce(low, at_least, AX.X, ALU.add))
                    st.mark(nc.vector.tensor_tensor(frac, gates, low, ALU.subtract))
                    do(nc.vector.tensor_tensor(segment, over_segments(low, NK - 1), over_gates(segments[:], NK - 1), ALU.is_equal))
                    st.mark(nc.vector.tensor_tensor(seg_step, segment, over_gates(knot_step[:], NK - 1), ALU.mult))
                    do(nc.vector.tensor_tensor(seg_knot, segment, over_gates(knot_row[:, 0:NK - 1], NK - 1), ALU.mult))
                    st.mark(nc.vector.tensor_reduce(step_at, seg_step, AX.X, ALU.add))
                    do(nc.vector.tensor_reduce(knot_at, seg_knot, AX.X, ALU.add))
                    do(nc.vector.tensor_tensor(frac, frac, step_at, ALU.mult))
                    do(nc.vector.tensor_tensor(gates, frac, knot_at, ALU.add))

                def first_max(eq, pick):
                    values = gates.rearrange("p (t n) -> p t n", t=NT)
                    do(nc.vector.tensor_reduce(top, values, AX.X, ALU.max))
                    do(nc.vector.tensor_tensor(eq, values, top.unsqueeze(2).broadcast_to([P, NT, CL]), ALU.is_equal))
                    do(nc.vector.tensor_tensor(eq, eq, first_weight[:].unsqueeze(1).broadcast_to([P, NT, CL]), ALU.mult))
                    do(nc.vector.tensor_reduce(best, eq, AX.X, ALU.max))
                    do(nc.vector.tensor_tensor(pick, eq, best.unsqueeze(2).broadcast_to([P, NT, CL]), ALU.is_equal))

                dve.wait_ge(gate_exp, b * 2 + 1)
                calibrate()
                first_max(c_eq, c_pick)
                for t in range(NT):
                    st.mark(nc.vector.tensor_tensor(sel_all[:, t, :].rearrange("p (c l) -> p c l", c=CL),
                                                    bank[:, 0, ST * t + CL:ST * (t + 1)].rearrange("p (c l) -> p c l", c=CL),
                                                    c_pick[:, t, :].unsqueeze(2).broadcast_to([P, CL, TPC]), ALU.mult))
                st.wait(dve)
                nc.vector.tensor_reduce(scores_sel.rearrange("p (t l) -> p t l", t=NT), sel_all.rearrange("p t (c l) -> p t l c", c=CL),
                                        AX.X, ALU.add).then_inc(sel_ready, 1)
                dve.wait_ge(gate_exp, b * 2 + 2)
                calibrate()
                first_max(l_eq, l_pick)
                for t in range(NT):
                    ins = nc.vector.tensor_tensor(expert[:, t, :].rearrange("p (c l) -> p c l", c=CL),
                                                  c_pick[:, t, :].unsqueeze(2).broadcast_to([P, CL, TPC]),
                                                  l_pick[:, t, :].unsqueeze(1).broadcast_to([P, CL, TPC]), ALU.mult)
                    ins.then_inc(expert_ready, 1)

                do(nc.vector.tensor_tensor(y_beta, y_sb[:], over_tiles(beta_row), ALU.add))
                dve.wait_ge(comp_mm, b + 1)
                nc.vector.tensor_tensor(comp_in, bank[:, 2, 0:2 * NT].rearrange("p (t i) -> p t i", t=NT),
                                        cb2_row[:].unsqueeze(1).broadcast_to([P, NT, 2]), ALU.add).then_inc(comp_b, 1)
                dve.wait_ge(comp_done, b + 1)
                dve.wait_ge(gather_mm, b + 1)

                def column(i):
                    return comp[:, :, i:i + 1].broadcast_to([P, NT, G])

                do(nc.vector.tensor_tensor(hh, bank[:, 4:4 + NT, T_W1:T_W1 + G], column(0), ALU.mult))
                do(nc.vector.tensor_tensor(hh2, bank[:, 4:4 + NT, T_W1 + G:T_B1], column(1), ALU.mult))
                do(nc.vector.tensor_tensor(hh, hh, hh2, ALU.add))
                do(nc.vector.tensor_tensor(hh, bank[:, 4:4 + NT, T_B1:T_W2], hh, ALU.add))
                do(nc.vector.tensor_scalar(hh, hh, 0.0, None, ALU.max))
                do(nc.vector.tensor_tensor(hh, bank[:, 4:4 + NT, T_W2:T_B2], hh, ALU.mult))
                do(nc.vector.tensor_reduce(mag, hh, AX.X, ALU.add))
                do(nc.vector.tensor_tensor(mag, bank[:, 4:4 + NT, T_B2], mag, ALU.add))
                do(nc.vector.tensor_scalar(mag, mag, scale_col[:, 0:1], None, ALU.mult))
                for t in range(NT):
                    st.mark(nc.vector.scalar_tensor_tensor(x_res[:, t, :], bank[:, 4 + t, 0:D], mag[:, t:t + 1], y_sb[:, t, :],
                                                           ALU.mult, ALU.add))
                st.wait(dve)

                def less_mean():
                    for t in range(NT):
                        st.mark(nc.vector.scalar_tensor_tensor(x_res[:, t, :], x_res[:, t, :], mv[:, t, 0:1], gamma_row[:],
                                                               ALU.subtract, ALU.mult))
                    st.wait(dve)

                layernorm(2, x_res, y_sb, less_mean, lambda t: nc.vector.scalar_tensor_tensor(
                    y_sb[:, t, :], x_res[:, t, :], ln_r[:, t:t + 1], y_beta[:, t, :], ALU.mult, ALU.add))
                layernorm(3, y_sb, y_sb, None if last else lambda: scores1(b + 1, 0, 0))
                st.end()

            dve.wait_ge(w_first, W_FIRST)
            dve.wait_ge(pad_ready, 2)
            convolve(0)
            add_position(0)
            dve.wait_ge(w_in, W_IN)
            dve.wait_ge(const_ready, 1)
            q0, q1 = sig_work[:, 0, :], sig_work[:, 1, :]
            setup = [0]

            def link(ins):
                ins.then_inc(sig_ready, 1)
                setup[0] += 1
                dve.wait_ge(sig_ready, setup[0])

            link(nc.vector.tensor_scalar(q0, sig_raw[:], 0.3, None, ALU.is_gt))
            link(nc.vector.tensor_scalar(q1, sig_raw[:], -0.3, None, ALU.is_lt))
            link(nc.vector.tensor_tensor(q0, q0, q1, ALU.subtract))
            link(nc.vector.tensor_tensor(q0, q0, sig_raw[:], ALU.subtract))
            link(nc.vector.tensor_tensor(q0, q0, sig_raw[:], ALU.add))
            SIG_NAT = setup[0]
            dve.wait_ge(sig_tr, 1)
            link(nc.vector.tensor_copy(sigT[:, :, CL:ST], bank[:, 0, 0:KD * TILES].rearrange("p (k n) -> p k n", k=KD)))
            members = sigT[:, :, CL:ST].rearrange("p k (c i) -> p k c i", i=TPC)
            link(nc.vector.tensor_tensor(sig_sum[:, 0], members[:, :, :, 0], members[:, :, :, 1], ALU.add))
            for i in range(2, TPC):
                link(nc.vector.tensor_tensor(sig_sum[:, 0], sig_sum[:, 0], members[:, :, :, i], ALU.add))
            link(nc.vector.tensor_scalar(sig_sum[:, 1], sig_sum[:, 0], 0.0, None, ALU.is_lt))
            link(nc.vector.tensor_scalar(sig_sum[:, 0], sig_sum[:, 0], 0.0, None, ALU.is_gt))
            link(nc.vector.tensor_tensor(sigT[:, :, 0:CL], sig_sum[:, 0], sig_sum[:, 1], ALU.subtract))
            link(nc.vector.tensor_tensor(knot_step[:], knot_row[:, 1:NK], knot_row[:, 0:NK - 1], ALU.subtract))
            link(nc.vector.tensor_scalar(temp[:, 1:2], temp[:, 0:1], 1e-6, None, ALU.add))
            link(nc.vector.reciprocal(temp[:, 2:3], temp[:, 1:2]))
            link(nc.vector.tensor_scalar(temp[:, 2:3], temp[:, 2:3], -1.0, None, ALU.mult))
            assert setup[0] == SIG_STEPS and SIG_NAT == 5

            scores1(0, 0, 0)
            with dve.Fori(0, B - 1) as b:
                batch(b)
            batch(B - 1, last=True)

        @block.tensor
        def _(pe):
            for primed in (vj_mm, pj_mm, ck_mm, sT_mm, s_mm, max_tr[SELF], max_tr[CROSS], o1_mm, p1_tr):
                pe.sem_inc(primed, FIRST)
            pe.sem_inc(pv_mm, PV_FIRST)
            mm = nc.tensor.matmul
            def project(dst, lhsT, rhs, tiles=KD):
                for k in range(tiles):
                    last = mm(dst, lhsT(k), rhs(k), start=(k == 0), stop=(k == tiles - 1))
                return last

            def position(b):
                pe.wait_ge(conv_done, FIRST + b * KD + KD)
                for m in range(KD):
                    project(bank[:, 4 + m, :], lambda k: pe_sb[:, k, P * m:P * (m + 1)], lambda k: xs[:, k, :]).then_inc(pe_mm, 1)

            def first_qk(b, *tiles):
                for i in tiles:
                    if i >= 2:
                        pe.wait_ge(qk_evac, b * 2 * KD + i - 1)
                    project(bank[:, 6 + i % 2, :], lambda k: qkv_sb[:, k, P * i:P * (i + 1)], lambda k: xs[:, k, :]).then_inc(qk_mm, 1)

            def first_v(b):
                for i in range(NT):
                    last = project(bank[:, 4 + i // 2, D * (i % 2):D * (i % 2 + 1)], lambda k: xs[:, k, P * i:P * (i + 1)],
                                   lambda k: qkv_sb[:, k, 2 * D:3 * D])
                    if i % 2:
                        last.then_inc(v_mm, 1)

            def context_keys(b):
                pe.wait_ge(ctx_in, b * 16 + 16)
                for u, (_, m, c0) in enumerate(ctx_units):
                    mm(bank[:, u, :], wck_sb[:, P * m:P * (m + 1)], ctx_sb[:, c0:c0 + S], start=True, stop=True).then_inc(ck_mm, 1)

            def batch(b, last_batch=False):
                def scores1(h, static):
                    u = b * H + h
                    for t in range(NT):
                        if not static:
                            pe.wait_ge(s1_evac, u * 4 + (t - 3))
                        mm(bank[:, t, :], q1T[:, bass.ds(h * S + P * t, P)],
                           k1T[:, :, bass.ts(h, RH)], start=True, stop=True).then_inc(s1_mm, 1)

                def transpose1(h, p):
                    u = b * H + h
                    pe.wait_ge(p1_evac, FIRST + u * 2)
                    for t in range(NT):
                        pe.wait_ge(p1_ready, FIRST + u * 4 + t + 1)
                        for j in range(4):
                            last = nc.tensor.transpose(bankb(4, 2)[:, S * j + P * t:S * j + P * (t + 1)],
                                                       e1[:, p, t, P * j:P * (j + 1)], identb[:])
                    last.then_inc(p1_tr, 1)

                def pv1(h):
                    u = b * H + h
                    pe.wait_ge(p1_evac, FIRST + u * 2 + 2)
                    pe.wait_ge(o1_evac, FIRST + u)
                    for t in range(NT):
                        for j in range(4):
                            last = mm(bank[:, 6, HD * t:HD * (t + 1)], p1T[:, j, P * t:P * (t + 1)], v1[:, h, j, :],
                                      start=(j == 0), stop=(j == 3))
                    last.then_inc(o1_mm, 1)

                pe.wait_ge(qk1_in, FIRST + (b + 1) * 16 * 2 * KD)
                pe.wait_ge(q1_ready, b * 4 + 4)
                pe.wait_ge(v_evac, b * 2 + 2)
                pe.wait_ge(v1_ready, b * 16 + 16)
                pe.wait_ge(ck_evac, (b + 1) * CTX_UNITS)
                scores1(0, True)
                scores1(1, False)
                scores1(2, False)
                transpose1(0, 0)

                def head1(h, p):
                    if not (isinstance(h, int) and h == H - 1):
                        scores1(h + 1, False)
                    pv1(h - 2)
                    transpose1(h - 1, 1 - p)

                with pe.Fori(0, H // 2 - 2) as i:
                    for p in range(2):
                        head1(i * 2 + (2 + p), p)
                def values(i):
                    if i >= 4:
                        pe.wait_ge(vj_evac, b * PAIRS + i - 3)
                    for half in range(2):
                        dst = bank[:, 2 + i % 4, D * half:D * (half + 1)]
                        if i < CTX_PAIRS:
                            t = 2 * i + half
                            last = mm(dst, ctx_sb[:, P * t:P * (t + 1)], wcv_sb[:], start=True, stop=True)
                        else:
                            t = 2 * (i - CTX_PAIRS) + half
                            last = project(dst, lambda k: featB[:, k, P * t:P * (t + 1)], lambda k: wv_sb[:, k, :])
                    last.then_inc(vj_mm, 1)

                for h in (H - 2, H - 1):
                    head1(h, h % 2)
                pe.wait_ge(s1_evac, (b + 1) * H * 4)
                values(0)
                pv1(H - 2)
                transpose1(H - 1, 1)
                values(1)
                pv1(H - 1)

                pe.wait_ge(o1_evac, FIRST + (b + 1) * H)
                for t in range(NT):
                    for k in range(KD):
                        last = nc.tensor.transpose(bankb(7)[:, S * k + P * t:S * k + P * (t + 1)],
                                                   o_nat[:, t, P * k:P * (k + 1)], identb[:])
                last.then_inc(feat_tr, 1)

                def keep_clock(n, c):
                    for _ in range(n):
                        mm(bank[:, c, 0:P], identb[:], mask_q[:], start=True, stop=True)

                def token_out(w):
                    for t in range(NT):
                        last = project(bank[:, t // 2, D * (t % 2):D * (t % 2 + 1)], lambda k: featA[:, k, P * t:P * (t + 1)],
                                       lambda k: w[:, k, :])
                        if t % 2:
                            last.then_inc(out_mm, 1)

                def to_features(src, first_bank):
                    for t in range(NT):
                        for k in range(KD):
                            last = nc.tensor.transpose(bank[:, first_bank + k, P * t:P * (t + 1)], src[:, t, P * k:P * (k + 1)], ident[:])
                    last.then_inc(feat_tr, 1)

                def unit(u):
                    m = unit_list[u][1]
                    if u >= 4:
                        pe.wait_ge(pj_rest, b * UNITS + u - 3)
                    elif u >= 2:
                        pe.wait_ge(vj_evac, b * PAIRS + u + 1)
                    w = (wq_sb, wk_sb, wcq_sb)[u % 3]
                    project(bank[:, unit_bank(u), :], lambda k: w[:, k, P * m:P * (m + 1)], lambda k: featB[:, k, :]).then_inc(pj_mm, 1)

                values(2)
                pe.wait_ge(feat_evac, b * 4 + 1)
                token_out(out_sb)
                values(3)
                keep_clock(56, 6)
                pe.wait_ge(ln_done, FIRST + b * 4 + 1)
                to_features(x_res, 0)
                pe.wait_ge(feat_evac, b * 4 + 2)
                for u in range(UNITS):
                    unit(u)
                for i in range(CTX_PAIRS, PAIRS):
                    values(i)

                def scores(h, i, order=SCORES, static=False):
                    kind, j = order[i]
                    if not (static and i < 2):
                        pe.wait_ge(max_done, (b * H + h) * 12 + i - 1)
                    if kind == SELF:
                        n = P * (j + 1)
                        mm(bank[:, i % 2, 0:n], q_self[0:SHIFT, h, P * j:n], k_self[0:SHIFT, h, 0:n], start=True, stop=False)
                        mm(bank[:, i % 2, P * j:n], identb[:], mask_q[:], start=False, stop=True).then_inc(s_mm, 1)
                    else:
                        mm(bank[:, i % 2, :], q_cross[0:SHIFT, h, P * (j // 2):P * (j // 2 + 1)],
                           k_cross[0:SHIFT, h, S * (j % 2):S * (j % 2 + 1)], start=True, stop=True).then_inc(s_mm, 1)

                def max_transpose(kind, h):
                    n = b * H + h
                    pe.wait_ge(parts_ready[kind], FIRST + n + 1)
                    pe.wait_ge(max_rows, FIRST + n * 2 + kind)
                    for t in range(NT):
                        last = nc.tensor.transpose(bankb(7)[0:3, S * kind + P * t:S * kind + P * (t + 1)],
                                                   max_parts[:, kind, t, :], identb[:])
                    last.then_inc(max_tr[kind], 1)

                def scoresT(kind, h, u, static=False):
                    n = b * H + h
                    if u == 0:
                        pe.wait_ge(max_rows, FIRST + n * 2 + kind + 1)
                    if not (static and kind == SELF and u < 2):
                        pe.wait_ge(pT_ready, n * 8 + 4 * kind + u - 1)
                    c = 2 + 2 * (u % 2)
                    if kind == SELF:
                        w = S - P * u
                        mm(bank[:, c, 0:w], k_self[0:ROWS, h, P * u:P * (u + 1)], q_self[0:ROWS, h, P * u:S], start=True, stop=False)
                        mm(bank[:, c, 0:P], identb[:], mask_k[:], start=False, stop=True).then_inc(sT_mm, 1)
                    else:
                        for i in range(2):
                            t = 2 * u + i
                            last = mm(bank[:, c + i, :], k_cross[0:ROWS, h, P * t:P * (t + 1)], q_cross[0:ROWS, h, :], start=True, stop=True)
                        last.then_inc(sT_mm, 1)

                def pv(h, p, r):
                    n = b * H + h
                    pe.wait_ge(pT_ready, n * 8 + 4 + 2 + r)
                    if r == 0:
                        pe.wait_ge(v_ready, n + 1)
                        pe.wait_ge(v_pad, b * 2 + 2)
                        pe.wait_ge(y_done, FIRST + n)
                    for kind, t, g in ROUNDS[r]:
                        tiles = GROUP_TILES[g]
                        q0 = P * t if kind == SELF else 0
                        pT = pT_self[p] if kind == SELF else pT_cross
                        ins = mm(bank[GROUP * g:GROUP * (g + 1), 6, q0:S], v_head[p][:, t if kind == SELF else NT + t, :],
                                 pT[:, t, q0:S], start=((kind, t) == tiles[0]), stop=((kind, t) == tiles[-1]),
                                 tile_position=(0, GROUP * g))
                        if (kind, t) == tiles[-1]:
                            ins.then_inc(pv_mm, 1)

                def sum_groups(h):
                    pe.wait_ge(pv_evac, b * H + h + 1)
                    w = 2 * (HD + 1)
                    for t in range(NT):
                        last = mm(bank[:, 6, w * t:w * (t + 1)], o_groups[:, P * t:P * (t + 1)], gather_groups[:],
                                  start=True, stop=True)
                    last.then_inc(o_mm, 1)

                def head(h, p, first=False, last=False):
                    def next_scores(*places):
                        if not last:
                            for i in places:
                                scores(h + 1, i)

                    def outputs(r):
                        if not first:
                            pv(h - 1, 1 - p, r)

                    scoresT(SELF, h, 0, first)
                    next_scores(0)
                    scoresT(SELF, h, 1, first)
                    next_scores(1)
                    outputs(0)
                    next_scores(2)
                    scoresT(SELF, h, 2, first)
                    next_scores(3)
                    outputs(1)
                    max_transpose(CROSS, h)
                    scoresT(SELF, h, 3, first)
                    next_scores(4)
                    outputs(2)
                    next_scores(5)
                    scoresT(CROSS, h, 0)
                    next_scores(6, 7)
                    scoresT(CROSS, h, 1)
                    next_scores(8, 9)
                    scoresT(CROSS, h, 2)
                    next_scores(10)
                    if not first:
                        sum_groups(h - 1)
                    if not last:
                        max_transpose(SELF, h + 1)
                    scoresT(CROSS, h, 3)
                    next_scores(11)

                pe.wait_ge(stack_in[SELF], stacks_loaded(b, SELF))
                pe.wait_ge(vj_evac, (b + 1) * PAIRS)
                for i in range(4):
                    scores(0, i, FIRST_SCORES, static=True)
                pe.wait_ge(stack_in[CROSS], stacks_loaded(b, CROSS))
                for i in range(4, 12):
                    scores(0, i, FIRST_SCORES)
                max_transpose(SELF, 0)
                head(0, 0, first=True)
                with pe.Fori(0, HT // 2 - 1) as i:
                    for p in range(2):
                        head(i * 2 + (p + 1), (p + 1) % 2)
                pe.wait_ge(stack_in[LATER], stacks_loaded(b, LATER))
                own_wait(nc.tensor)
                with pe.Fori(HT // 2 - 1, H // 2 - 1) as i:
                    for p in range(2):
                        head(i * 2 + (p + 1), (p + 1) % 2)
                head(H - 1, 1, last=True)
                for r in range(len(ROUNDS)):
                    pv(H - 1, 1, r)
                sum_groups(H - 1)

                keep_clock(18, 7)
                pe.wait_ge(y_step, (b + 1) * H * 2)
                to_features(y_sb, 2)
                pe.wait_ge(feat_evac, b * 4 + 3)
                token_out(wp_sb)
                if not last_batch:
                    position(b + 1)
                keep_clock(30, 7)
                pe.wait_ge(ln_done, FIRST + b * 4 + 2)
                to_features(y_sb, 2)
                pe.wait_ge(feat_evac, b * 4 + 4)
                for t in range(NT):
                    last = project(bank[:, 0, ST * t:ST * (t + 1)], lambda k: featB[:, k, P * t:P * (t + 1)], lambda k: sigT[:, k, :])
                last.then_inc(route_mm, 1)
                project(bank[0:HID, 1, :], lambda k: cw1_sb[:, k, :], lambda k: featB[:, k, :]).then_inc(gelu_in, 1)
                if not last_batch:
                    pe.wait_ge(xs_ready, (b + 1) * KD + KD)
                    first_v(b + 1)
                    first_qk(b + 1, 0, 1, 2, 3)
                    pe.wait_ge(v_evac, (b + 2) * 2)
                pe.wait_ge(expert_ready, b * NT + NT)
                own_wait(nc.tensor)
                for t in range(NT):
                    last = nc.tensor.transpose(bank[0:TILES, 3, P * t:P * (t + 1)], expert[:, t, :], ident[:])
                last.then_inc(expert_tr, 1)
                pe.wait_ge(expert_evac, b + 1)
                if not last_batch:
                    pe.wait_ge(qk_evac, (b + 2) * 2 * KD)
                for t in range(NT):
                    last = mm(bank[:, 4 + t, 0:TABLE], expertT[:, P * t:P * (t + 1)], table[:], start=True, stop=True)
                last.then_inc(gather_mm, 1)
                pe.wait_ge(gelu_done, b + 1)
                for t in range(NT):
                    last = mm(bank[:, 2, 2 * t:2 * t + 2], hT[:, P * t:P * (t + 1)], cw2_sb[:], start=True, stop=True)
                last.then_inc(comp_mm, 1)
                if not last_batch:
                    pe.wait_ge(comp_b, b + 1)
                    context_keys(b + 1)

            pe.wait_ge(w_first, W_FIRST)
            position(0)
            pe.wait_ge(xs_ready, KD)
            first_qk(0, 0, 1)
            first_v(0)
            first_qk(0, 2, 3)
            pe.wait_ge(const_ready, 1)
            pe.wait_ge(w_in, W_IN)
            pe.wait_ge(sig_ready, 5)
            for k in range(KD):
                last = nc.tensor.transpose(bank[:, 0, TILES * k:TILES * (k + 1)], sig_work[:, 0, P * k:P * (k + 1)],
                                           ident[0:TILES, 0:TILES])
            last.then_inc(sig_tr, 1)
            pe.wait_ge(sig_ready, SIG_STEPS)
            context_keys(0)
            pe.wait_ge(minus_ones, 2)
            with pe.Fori(0, B - 1) as b:
                batch(b)
            batch(B - 1, last_batch=True)


_OUT = ((8, 512, 256), "float32")


def kernel(**inputs):
    import numpy as np
    import concourse.bacc as bacc
    from concourse.bass_utils import run_bass_kernel_spmd

    nc = bacc.Bacc("TRN2", target_bir_lowering=False, num_devices=1)
    given = {k: np.asarray(v) for k, v in inputs.items()}

    def attn(n):
        return given["L0_attn_" + n]

    arrays = {"x": given["x"], "xT": given["x"].transpose(0, 2, 1), "ctxT": given["ctx_512"].transpose(0, 2, 1),
              "conv_w": attn("conv_w")[:, 0, :, 1], "peT": attn("pe_w").T, "qkvT": attn("qkv_w").T, "outT": attn("out_w").T}
    for n in ("Wk", "bk", "Wq", "bq", "Wv", "bv", "Wck", "bck", "Wcq", "bcq", "Wcv", "bcv", "Wp", "bp"):
        arrays[n] = given["L0_xattn_" + n]
    for n in ("signatures_raw", "knot_values", "temperature", "compress_w1", "compress_b1", "compress_w2", "compress_b2",
              "spline_w1", "spline_b1", "spline_w2", "spline_b2", "directions", "norm_gamma", "norm_beta", "output_scale"):
        arrays[n] = given["L0_ffn_" + n]
    for n in ("Wq", "Wk", "Wcq", "Wck"):
        w = arrays[n]
        arrays[n] = w.reshape(w.shape[0], 2, 8, 16).transpose(0, 1, 3, 2).reshape(w.shape)
    for n in ("bq", "bk", "bcq", "bck"):
        arrays[n] = arrays[n].reshape(2, 8, 16).transpose(2, 1, 0).reshape(128, 2)
    arrays = {n: np.ascontiguousarray(a) for n, a in arrays.items()}
    args = [nc.dram_tensor(n, a.shape, mybir.dt.from_np(a.dtype), kind="ExternalInput").ap() for n, a in arrays.items()]
    out = nc.dram_tensor("out", _OUT[0], mybir.dt.float32, kind="ExternalOutput").ap()
    decoder_layer(nc, *args, out)
    return run_bass_kernel_spmd(nc, [arrays], core_ids=[0]).results[0]["out"]
```
